# Optimizing a Trainium2 kernel written in Bass

```python
import numpy as np
import jax
import jax.numpy as jnp

def _softmax(x, axis=-1):
    return jax.nn.softmax(x, axis=axis)

def _gelu(x):
    return jax.nn.gelu(x, approximate=True)

def _silu(x):
    return jax.nn.silu(x)

def _sigmoid(x):
    return jax.nn.sigmoid(x)

def _layernorm(x, axis=-1, eps=1e-05):
    m = jnp.mean(x, axis=axis, keepdims=True)
    v = jnp.var(x, axis=axis, keepdims=True)
    return (x - m) / jnp.sqrt(v + eps)

def _scatter_add(tgt, idx, src, axis=0):
    return tgt.at[idx].add(src)

def _segment_sum(src, seg, n):
    return jax.ops.segment_sum(src, seg, n)
kernel_name = 'mk_seq_preln_d4_jaxref_r8_82406e'

def setup_inputs(seed: int=0):
    np.random.seed(seed)
    _w = jnp.asarray

    def _L0_attn_setup():
        import jax, jax.numpy as jnp
        import numpy as np
        from jax.scipy.linalg import solve_triangular
        B, T, D = (4, 1024, 128)
        HEAD_DIM = 128
        CHUNK = 64
        key = jax.random.key(seed)
        ks = jax.random.split(key, 8)
        H = D // HEAD_DIM
        x = jax.random.normal(ks[0], (B, T, D), dtype=jnp.float32)
        W_write = jax.random.normal(ks[1], (D, D), dtype=jnp.float32) * 0.02
        W_gate = jax.random.normal(ks[2], (H, D), dtype=jnp.float32) * 0.02
        W_out = jax.random.normal(ks[3], (D, D), dtype=jnp.float32) * 0.02
        W_beta = jax.random.normal(ks[4], (H, D), dtype=jnp.float32) * 0.02
        W_alpha = jax.random.normal(ks[5], (H, D), dtype=jnp.float32) * 0.02
        u = jax.random.uniform(ks[6], (H,), dtype=jnp.float32)
        dt = jnp.exp(u * (jnp.log(jnp.float32(0.1)) - jnp.log(jnp.float32(0.001))) + jnp.log(jnp.float32(0.001)))
        dt_bias = dt + jnp.log(-jnp.expm1(-dt))
        A_log = jnp.log(jax.random.uniform(ks[7], (H,), dtype=jnp.float32, minval=0.001, maxval=16.0))
        return {'x': x, 'W_write': W_write, 'W_gate': W_gate, 'W_out': W_out, 'W_beta': W_beta, 'W_alpha': W_alpha, 'dt_bias': dt_bias, 'A_log': A_log}
    _L0_attn_in = _L0_attn_setup()

    def _L0_ffn_setup():
        import jax, jax.numpy as jnp
        import numpy as np
        DIM = 128
        DEPTH = 6
        HEADS = 16
        DIM_HEAD = 64
        WINDOW = 32
        INNER = HEADS * DIM_HEAD
        DIM_INNER = int(DIM * 4 * 2 / 3)
        QK_SCALE = 8.0

        def shift_tokens(t):
            a, s = jnp.split(t, 2, -1)
            s = jnp.pad(s, ((0, 0), (1, 0), (0, 0)))[:, :-1]
            return jnp.concatenate([a, s], -1)

        def l2norm(t):
            return t / jnp.maximum(jnp.linalg.norm(t, axis=-1, keepdims=True), 1e-12)

        def rotate_half(x):
            x1, x2 = jnp.split(x, 2, -1)
            return jnp.concatenate([-x2, x1], -1)

        def rotary_tables(n):
            half = jnp.arange(0, DIM_HEAD, 2, dtype=jnp.float32)
            inv_freq = 1.0 / 10000.0 ** (half / DIM_HEAD)
            t = jnp.arange(n, dtype=jnp.float32)
            freqs = t[:, None] * inv_freq[None, :]
            freqs = jnp.concatenate([freqs, freqs], -1)
            base_scale = (half + 0.4 * DIM_HEAD) / (1.4 * DIM_HEAD)
            power = (t - n // 2) / (WINDOW // 2)
            scale = base_scale[None, :] ** power[:, None]
            scale = jnp.concatenate([scale, scale], -1)
            return (freqs, scale)

        def local_attention(q, k, v):
            b, h, n, d = q.shape
            w = WINDOW
            nw = n // w
            bq = q.reshape(b, h, nw, w, d)
            bk = k.reshape(b, h, nw, w, d)
            bv = v.reshape(b, h, nw, w, d)

            def look(t):
                p = jnp.pad(t, ((0, 0), (0, 0), (1, 0), (0, 0), (0, 0)))
                return jnp.concatenate([p[:, :, :nw], p[:, :, 1:]], axis=3)
            bk2, bv2 = (look(bk), look(bv))
            seq = jnp.arange(n).reshape(nw, w)
            seq_p = jnp.pad(seq, ((1, 0), (0, 0)), constant_values=-1)
            jt = jnp.concatenate([seq_p[:nw], seq_p[1:]], axis=1)
            it = seq[:, :, None]
            jb = jt[:, None, :]
            mask = (it < jb) | (it > jb + w) | (jb == -1)
            sim = jnp.einsum('bhwie,bhwje->bhwij', bq, bk2) * QK_SCALE
            sim = jnp.where(mask, -jnp.finfo(sim.dtype).max, sim)
            attn = jax.nn.softmax(sim, -1)
            out = jnp.einsum('bhwij,bhwje->bhwie', attn, bv2)
            return out.reshape(b, h, n, d)

        def attn_layer(x, Wqkv, qs, ksc, Wo):
            b, n, _ = x.shape
            qkv = x @ Wqkv
            q, k, v = jnp.split(qkv, 3, -1)
            sh = lambda t: t.reshape(b, n, HEADS, DIM_HEAD).transpose(0, 2, 1, 3)
            q, k, v = (sh(q), sh(k), sh(v))
            q = l2norm(q) * qs
            k = l2norm(k) * ksc
            freqs, scale = rotary_tables(n)
            cos, sin = (jnp.cos(freqs), jnp.sin(freqs))
            q = q * cos * scale + rotate_half(q) * sin * scale
            inv = 1.0 / scale
            k = k * cos * inv + rotate_half(k) * sin * inv
            out = local_attention(q, k, v)
            out = out.transpose(0, 2, 1, 3).reshape(b, n, INNER)
            return out @ Wo

        def ffn_layer(x, g, bln, W1, b1, W2, b2):
            mu = x.mean(-1, keepdims=True)
            var = ((x - mu) ** 2).mean(-1, keepdims=True)
            xn = (x - mu) / jnp.sqrt(var + 1e-05) * g + bln
            hg = xn @ W1 + b1
            a, gate = jnp.split(hg, 2, -1)
            return a * jax.nn.gelu(gate, approximate=False) @ W2 + b2
        key = jax.random.key(seed)
        ks = jax.random.split(key, 8)
        B, N = (2, 256)
        init = lambda k, shape: jax.random.normal(k, shape, jnp.float32) * 0.02
        return {'x': jax.random.normal(ks[0], (B, N, DIM), jnp.float32), 'Wqkv': init(ks[1], (DEPTH, DIM, 3 * INNER)), 'q_scale': jnp.ones((DEPTH, DIM_HEAD), jnp.float32), 'k_scale': jnp.ones((DEPTH, DIM_HEAD), jnp.float32), 'Wo': init(ks[2], (DEPTH, INNER, DIM)), 'ln_g': jnp.ones((DEPTH, DIM), jnp.float32), 'ln_b': jnp.zeros((DEPTH, DIM), jnp.float32), 'W1': init(ks[3], (DEPTH, DIM, 2 * DIM_INNER)), 'b1': jnp.zeros((DEPTH, 2 * DIM_INNER), jnp.float32), 'W2': init(ks[4], (DEPTH, DIM_INNER, DIM)), 'b2': jnp.zeros((DEPTH, DIM), jnp.float32)}
    _L0_ffn_in = _L0_ffn_setup()

    def _L1_attn_setup():
        import jax, jax.numpy as jnp
        import numpy as np
        D_HEAD = 128
        ROTARY_BASE = 10000.0
        NEG = 1e+30

        def frac_rope(x, base=ROTARY_BASE):
            rot, skip = jnp.split(x, 2, axis=-1)
            T, W = (rot.shape[-2], rot.shape[-1])
            pos = jnp.arange(T)[:, None]
            dims = jnp.arange(W // 2)
            ang = jnp.power(base, -dims / (W // 2))[None, :]
            rad = pos * ang
            cos = jnp.cos(rad).astype(x.dtype)
            sin = jnp.sin(rad).astype(x.dtype)
            even, odd = jnp.split(rot, 2, axis=-1)
            r_even = even * cos - odd * sin
            r_odd = even * sin + odd * cos
            return jnp.concatenate([r_even, r_odd, skip], axis=-1)
        key = jax.random.key(seed)
        B, T, M, D = (4, 256, 128, D_HEAD)
        H = M // D
        ks = jax.random.split(key, 5)
        scale = M ** (-0.5)
        x = jax.random.normal(ks[0], (B, T, M), dtype=jnp.float32)
        wq = jax.random.normal(ks[1], (M, H, D), dtype=jnp.float32) * scale
        wk = jax.random.normal(ks[2], (M, H, D), dtype=jnp.float32) * scale
        wv = jax.random.normal(ks[3], (M, H, D), dtype=jnp.float32) * scale
        wo = jax.random.normal(ks[4], (H, D, M), dtype=jnp.float32) * scale
        return {'x': x, 'wq': wq, 'wk': wk, 'wv': wv, 'wo': wo}
    _L1_attn_in = _L1_attn_setup()

    def _L1_ffn_setup():
        import jax, jax.numpy as jnp
        import numpy as np
        N_EMBED = 128
        FFN_HIDDEN = 512
        NUM_EXPERTS = 8
        TOP_K = 2
        key = jax.random.key(seed)
        ks = jax.random.split(key, 8)
        d, f, E = (N_EMBED, FFN_HIDDEN, NUM_EXPERTS)
        s_d = 1.0 / np.sqrt(d)
        s_f = 1.0 / np.sqrt(f)
        return {'x': jax.random.normal(ks[0], (2, 256, d), dtype=jnp.float32), 'Wg': jax.random.uniform(ks[1], (d, E), jnp.float32, -s_d, s_d), 'bg': jax.random.uniform(ks[2], (E,), jnp.float32, -s_d, s_d), 'W1': jax.random.uniform(ks[3], (E, d, f), jnp.float32, -s_d, s_d), 'b1': jax.random.uniform(ks[4], (E, f), jnp.float32, -s_d, s_d), 'W2': jax.random.uniform(ks[5], (E, f, d), jnp.float32, -s_f, s_f), 'b2': jax.random.uniform(ks[6], (E, d), jnp.float32, -s_f, s_f)}
    _L1_ffn_in = _L1_ffn_setup()

    def _L2_attn_setup():
        import math
        import jax, jax.numpy as jnp
        import numpy as np
        DIM = 128
        DIM_QK = 128
        DIM_V = 128
        CHUNK = 64
        NUM_BUCKETS = 32
        MAX_DISTANCE = 128

        def _rel_pos_bucket(n_q, n_k):
            q_pos = jnp.arange(n_q, dtype=jnp.int32)
            k_pos = jnp.arange(n_k, dtype=jnp.int32)
            rel = k_pos[None, :] - q_pos[:, None]
            n = jnp.maximum(-rel, 0)
            max_exact = NUM_BUCKETS // 2
            is_small = n < max_exact
            n_f = jnp.maximum(n, 1).astype(jnp.float32)
            val_large = max_exact + jnp.log(n_f / max_exact) / math.log(MAX_DISTANCE / max_exact) * (NUM_BUCKETS - max_exact)
            val_large = jnp.minimum(val_large, NUM_BUCKETS - 1)
            bucket = jnp.where(is_small, n.astype(jnp.float32), val_large)
            return bucket.astype(jnp.int32)
        key = jax.random.key(seed)
        ks = jax.random.split(key, 6)
        b, s = (8, 512)
        x = jax.random.normal(ks[0], (b, s, DIM), dtype=jnp.float32)
        Wqk = jax.random.normal(ks[1], (DIM, DIM_QK), dtype=jnp.float32) * (1.0 / math.sqrt(DIM))
        bqk = jnp.zeros((DIM_QK,), dtype=jnp.float32)
        Wv = jax.random.normal(ks[2], (DIM, DIM_V), dtype=jnp.float32) * (1.0 / math.sqrt(DIM))
        bv = jnp.zeros((DIM_V,), dtype=jnp.float32)
        gamma = jax.random.normal(ks[3], (2, DIM_QK), dtype=jnp.float32) * 0.02
        beta = jnp.zeros((2, DIM_QK), dtype=jnp.float32)
        rel_emb = jax.random.normal(ks[4], (NUM_BUCKETS, 1), dtype=jnp.float32) * 0.05
        return {'x': x, 'Wqk': Wqk, 'bqk': bqk, 'Wv': Wv, 'bv': bv, 'gamma': gamma, 'beta': beta, 'rel_emb': rel_emb}
    _L2_attn_in = _L2_attn_setup()

    def _L2_ffn_setup():
        import jax, jax.numpy as jnp
        import numpy as np
        B, L, D, F, E = (2, 128, 128, 512, 8)
        key = jax.random.key(seed)
        ks = jax.random.split(key, 7)
        return {'x': jax.random.normal(ks[0], (B, L, D), dtype=jnp.float32), 'router_w': jax.random.normal(ks[1], (D, E), dtype=jnp.float32) * 0.02, 'router_b': jax.random.normal(ks[2], (E,), dtype=jnp.float32) * 0.02, 'W1': jax.random.normal(ks[3], (E, D, F), dtype=jnp.float32) * (1.0 / np.sqrt(D)), 'b1': jax.random.normal(ks[4], (E, F), dtype=jnp.float32) * 0.02, 'W2': jax.random.normal(ks[5], (E, F, D), dtype=jnp.float32) * (1.0 / np.sqrt(F)), 'b2': jax.random.normal(ks[6], (E, D), dtype=jnp.float32) * 0.02}
    _L2_ffn_in = _L2_ffn_setup()

    def _L3_attn_setup():
        import jax, jax.numpy as jnp
        import numpy as np
        NEG = 10000.0
        key = jax.random.key(seed)
        ks = jax.random.split(key, 5)
        B, S, D = (2, 256, 128)
        std = 1.0 / np.sqrt(D)
        return {'x': jax.random.normal(ks[0], (B, S, D), dtype=jnp.float32), 'Wq': jax.random.normal(ks[1], (D, D), dtype=jnp.float32) * std, 'bq': jnp.zeros((D,), jnp.float32), 'Wk': jax.random.normal(ks[2], (D, D), dtype=jnp.float32) * std, 'bk': jnp.zeros((D,), jnp.float32), 'Wv': jax.random.normal(ks[3], (D, D), dtype=jnp.float32) * std, 'bv': jnp.zeros((D,), jnp.float32), 'Wo': jax.random.normal(ks[4], (D, D), dtype=jnp.float32) * std, 'bo': jnp.zeros((D,), jnp.float32)}
    _L3_attn_in = _L3_attn_setup()

    def _L3_ffn_setup():
        import jax, jax.numpy as jnp
        import numpy as np
        DIM, HIDDEN, E = (128, 512, 8)
        B, L = (2, 256)
        key = jax.random.key(seed)
        ks = jax.random.split(key, 6)
        s_in = 1.0 / np.sqrt(DIM)
        s_h = 1.0 / np.sqrt(HIDDEN)
        return {'x': jax.random.normal(ks[0], (B, L, DIM), dtype=jnp.float32), 'Wg': jax.random.uniform(ks[1], (E, DIM), jnp.float32, -s_in, s_in), 'W1': jax.random.uniform(ks[2], (E, DIM, HIDDEN), jnp.float32, -s_in, s_in), 'b1': jax.random.uniform(ks[3], (E, HIDDEN), jnp.float32, -s_in, s_in), 'W2': jax.random.uniform(ks[4], (E, HIDDEN, DIM), jnp.float32, -s_h, s_h), 'b2': jax.random.uniform(ks[5], (E, DIM), jnp.float32, -s_h, s_h)}
    _L3_ffn_in = _L3_ffn_setup()
    _d = {'L0_attn_x': _L0_attn_in['x'], 'L0_attn_W_write': _L0_attn_in['W_write'], 'L0_attn_W_gate': _L0_attn_in['W_gate'], 'L0_attn_W_out': _L0_attn_in['W_out'], 'L0_attn_W_beta': _L0_attn_in['W_beta'], 'L0_attn_W_alpha': _L0_attn_in['W_alpha'], 'L0_attn_dt_bias': _L0_attn_in['dt_bias'], 'L0_attn_A_log': _L0_attn_in['A_log'], 'L0_ffn_Wqkv': _L0_ffn_in['Wqkv'], 'L0_ffn_q_scale': _L0_ffn_in['q_scale'], 'L0_ffn_k_scale': _L0_ffn_in['k_scale'], 'L0_ffn_Wo': _L0_ffn_in['Wo'], 'L0_ffn_ln_g': _L0_ffn_in['ln_g'], 'L0_ffn_ln_b': _L0_ffn_in['ln_b'], 'L0_ffn_W1': _L0_ffn_in['W1'], 'L0_ffn_b1': _L0_ffn_in['b1'], 'L0_ffn_W2': _L0_ffn_in['W2'], 'L0_ffn_b2': _L0_ffn_in['b2'], 'L1_attn_wq': _L1_attn_in['wq'], 'L1_attn_wk': _L1_attn_in['wk'], 'L1_attn_wv': _L1_attn_in['wv'], 'L1_attn_wo': _L1_attn_in['wo'], 'L1_ffn_Wg': _L1_ffn_in['Wg'], 'L1_ffn_bg': _L1_ffn_in['bg'], 'L1_ffn_W1': _L1_ffn_in['W1'], 'L1_ffn_b1': _L1_ffn_in['b1'], 'L1_ffn_W2': _L1_ffn_in['W2'], 'L1_ffn_b2': _L1_ffn_in['b2'], 'L2_attn_Wqk': _L2_attn_in['Wqk'], 'L2_attn_bqk': _L2_attn_in['bqk'], 'L2_attn_Wv': _L2_attn_in['Wv'], 'L2_attn_bv': _L2_attn_in['bv'], 'L2_attn_gamma': _L2_attn_in['gamma'], 'L2_attn_beta': _L2_attn_in['beta'], 'L2_attn_rel_emb': _L2_attn_in['rel_emb'], 'L2_ffn_router_w': _L2_ffn_in['router_w'], 'L2_ffn_router_b': _L2_ffn_in['router_b'], 'L2_ffn_W1': _L2_ffn_in['W1'], 'L2_ffn_b1': _L2_ffn_in['b1'], 'L2_ffn_W2': _L2_ffn_in['W2'], 'L2_ffn_b2': _L2_ffn_in['b2'], 'L3_attn_Wq': _L3_attn_in['Wq'], 'L3_attn_bq': _L3_attn_in['bq'], 'L3_attn_Wk': _L3_attn_in['Wk'], 'L3_attn_bk': _L3_attn_in['bk'], 'L3_attn_Wv': _L3_attn_in['Wv'], 'L3_attn_bv': _L3_attn_in['bv'], 'L3_attn_Wo': _L3_attn_in['Wo'], 'L3_attn_bo': _L3_attn_in['bo'], 'L3_ffn_Wg': _L3_ffn_in['Wg'], 'L3_ffn_W1': _L3_ffn_in['W1'], 'L3_ffn_b1': _L3_ffn_in['b1'], 'L3_ffn_W2': _L3_ffn_in['W2'], 'L3_ffn_b2': _L3_ffn_in['b2']}
    _x0 = _d['L0_attn_x']
    _d['L0_attn_x'] = jax.random.normal(jax.random.fold_in(jax.random.key(seed), 1), (8, 512, 128), dtype=_x0.dtype)
    del _x0
    return _d

def reference(L0_attn_x, L0_attn_W_write, L0_attn_W_gate, L0_attn_W_out, L0_attn_W_beta, L0_attn_W_alpha, L0_attn_dt_bias, L0_attn_A_log, L0_ffn_Wqkv, L0_ffn_q_scale, L0_ffn_k_scale, L0_ffn_Wo, L0_ffn_ln_g, L0_ffn_ln_b, L0_ffn_W1, L0_ffn_b1, L0_ffn_W2, L0_ffn_b2, L1_attn_wq, L1_attn_wk, L1_attn_wv, L1_attn_wo, L1_ffn_Wg, L1_ffn_bg, L1_ffn_W1, L1_ffn_b1, L1_ffn_W2, L1_ffn_b2, L2_attn_Wqk, L2_attn_bqk, L2_attn_Wv, L2_attn_bv, L2_attn_gamma, L2_attn_beta, L2_attn_rel_emb, L2_ffn_router_w, L2_ffn_router_b, L2_ffn_W1, L2_ffn_b1, L2_ffn_W2, L2_ffn_b2, L3_attn_Wq, L3_attn_bq, L3_attn_Wk, L3_attn_bk, L3_attn_Wv, L3_attn_bv, L3_attn_Wo, L3_attn_bo, L3_ffn_Wg, L3_ffn_W1, L3_ffn_b1, L3_ffn_W2, L3_ffn_b2):

    def _L0_attn_ref(x, W_write, W_gate, W_out, W_beta, W_alpha, dt_bias, A_log):
        import jax, jax.numpy as jnp
        import numpy as np
        from jax.scipy.linalg import solve_triangular
        B, T, D = (4, 1024, 128)
        HEAD_DIM = 128
        CHUNK = 64
        Bn, Tn, Dm = x.shape
        H = A_log.shape[0]
        d = Dm // H
        C = CHUNK
        assert Tn % C == 0
        N = Tn // C
        xf = x.astype(jnp.float32)
        v = (xf @ W_write.T).reshape(Bn, Tn, H, d)
        gate = jax.nn.sigmoid(xf @ W_gate.T)[..., None]
        beta = jax.nn.sigmoid(xf @ W_beta.T)
        decay = -jnp.exp(A_log) * jax.nn.softplus(xf @ W_alpha.T + dt_bias)
        rk = xf.reshape(Bn, Tn, H, d)
        rk = rk / jnp.maximum(jnp.linalg.norm(rk, axis=-1, keepdims=True), 1e-12)
        wk = jnp.pad(rk[:, :-1], ((0, 0), (1, 0), (0, 0), (0, 0)))
        rk = rk.transpose(0, 2, 1, 3)
        wk = wk.transpose(0, 2, 1, 3)
        v = v.transpose(0, 2, 1, 3)
        bt = beta.transpose(0, 2, 1)[..., None]
        v = v * bt
        wk_beta = wk * bt
        rk = rk.reshape(Bn, H, N, C, d)
        wk = wk.reshape(Bn, H, N, C, d)
        v = v.reshape(Bn, H, N, C, d)
        wk_beta = wk_beta.reshape(Bn, H, N, C, d)
        dec = jnp.cumsum(decay.transpose(0, 2, 1).reshape(Bn, H, N, C), axis=-1)
        dec_exp = jnp.exp(dec)[..., None]
        lower = jnp.tril(jnp.ones((C, C), dtype=bool))
        strict_lower = jnp.tril(jnp.ones((C, C), dtype=bool), -1)
        diff = dec[..., :, None] - dec[..., None, :]
        L_mask = jnp.exp(jnp.where(lower, diff, -jnp.inf))
        M = jnp.einsum('bhnid,bhnjd->bhnij', wk_beta, wk) * L_mask
        M = jnp.where(strict_lower, M, jnp.float32(0.0))
        eye = jnp.eye(C, dtype=jnp.float32)
        A = solve_triangular(eye + M, jnp.broadcast_to(eye, M.shape), lower=True)
        v = A @ v
        wk_cumdecay = A @ (wk_beta * dec_exp)
        xs = (rk.transpose(2, 0, 1, 3, 4), wk.transpose(2, 0, 1, 3, 4), v.transpose(2, 0, 1, 3, 4), wk_cumdecay.transpose(2, 0, 1, 3, 4), dec.transpose(2, 0, 1, 3), L_mask.transpose(2, 0, 1, 3, 4))
        S0 = jnp.zeros((Bn, H, d, d), dtype=jnp.float32)

        def step(S, inp):
            rk_i, wk_i, v_i, wkcd_i, dec_i, L_i = inp
            attn = jnp.einsum('bhid,bhjd->bhij', rk_i, wk_i) * L_i
            attn = jnp.where(lower, attn, jnp.float32(0.0))
            v_new = v_i - wkcd_i @ S
            o_i = rk_i * jnp.exp(dec_i)[..., None] @ S + attn @ v_new
            dw = jnp.exp(dec_i[..., -1:] - dec_i)[..., None]
            S_new = S * jnp.exp(dec_i[..., -1])[..., None, None] + jnp.einsum('bhcd,bhce->bhde', wk_i * dw, v_new)
            return (S_new, o_i)
        _, o = jax.lax.scan(step, S0, xs)
        o = o.transpose(1, 2, 0, 3, 4).reshape(Bn, H, Tn, d).transpose(0, 2, 1, 3)
        o = (o * gate).reshape(Bn, Tn, Dm)
        return (x + o @ W_out.T).astype(x.dtype)

    def _L0_ffn_ref(x, Wqkv, q_scale, k_scale, Wo, ln_g, ln_b, W1, b1, W2, b2):
        import jax, jax.numpy as jnp
        import numpy as np
        DIM = 128
        DEPTH = 6
        HEADS = 16
        DIM_HEAD = 64
        WINDOW = 32
        INNER = HEADS * DIM_HEAD
        DIM_INNER = int(DIM * 4 * 2 / 3)
        QK_SCALE = 8.0

        def shift_tokens(t):
            a, s = jnp.split(t, 2, -1)
            s = jnp.pad(s, ((0, 0), (1, 0), (0, 0)))[:, :-1]
            return jnp.concatenate([a, s], -1)

        def l2norm(t):
            return t / jnp.maximum(jnp.linalg.norm(t, axis=-1, keepdims=True), 1e-12)

        def rotate_half(x):
            x1, x2 = jnp.split(x, 2, -1)
            return jnp.concatenate([-x2, x1], -1)

        def rotary_tables(n):
            half = jnp.arange(0, DIM_HEAD, 2, dtype=jnp.float32)
            inv_freq = 1.0 / 10000.0 ** (half / DIM_HEAD)
            t = jnp.arange(n, dtype=jnp.float32)
            freqs = t[:, None] * inv_freq[None, :]
            freqs = jnp.concatenate([freqs, freqs], -1)
            base_scale = (half + 0.4 * DIM_HEAD) / (1.4 * DIM_HEAD)
            power = (t - n // 2) / (WINDOW // 2)
            scale = base_scale[None, :] ** power[:, None]
            scale = jnp.concatenate([scale, scale], -1)
            return (freqs, scale)

        def local_attention(q, k, v):
            b, h, n, d = q.shape
            w = WINDOW
            nw = n // w
            bq = q.reshape(b, h, nw, w, d)
            bk = k.reshape(b, h, nw, w, d)
            bv = v.reshape(b, h, nw, w, d)

            def look(t):
                p = jnp.pad(t, ((0, 0), (0, 0), (1, 0), (0, 0), (0, 0)))
                return jnp.concatenate([p[:, :, :nw], p[:, :, 1:]], axis=3)
            bk2, bv2 = (look(bk), look(bv))
            seq = jnp.arange(n).reshape(nw, w)
            seq_p = jnp.pad(seq, ((1, 0), (0, 0)), constant_values=-1)
            jt = jnp.concatenate([seq_p[:nw], seq_p[1:]], axis=1)
            it = seq[:, :, None]
            jb = jt[:, None, :]
            mask = (it < jb) | (it > jb + w) | (jb == -1)
            sim = jnp.einsum('bhwie,bhwje->bhwij', bq, bk2) * QK_SCALE
            sim = jnp.where(mask, -jnp.finfo(sim.dtype).max, sim)
            attn = jax.nn.softmax(sim, -1)
            out = jnp.einsum('bhwij,bhwje->bhwie', attn, bv2)
            return out.reshape(b, h, n, d)

        def attn_layer(x, Wqkv, qs, ksc, Wo):
            b, n, _ = x.shape
            qkv = x @ Wqkv
            q, k, v = jnp.split(qkv, 3, -1)
            sh = lambda t: t.reshape(b, n, HEADS, DIM_HEAD).transpose(0, 2, 1, 3)
            q, k, v = (sh(q), sh(k), sh(v))
            q = l2norm(q) * qs
            k = l2norm(k) * ksc
            freqs, scale = rotary_tables(n)
            cos, sin = (jnp.cos(freqs), jnp.sin(freqs))
            q = q * cos * scale + rotate_half(q) * sin * scale
            inv = 1.0 / scale
            k = k * cos * inv + rotate_half(k) * sin * inv
            out = local_attention(q, k, v)
            out = out.transpose(0, 2, 1, 3).reshape(b, n, INNER)
            return out @ Wo

        def ffn_layer(x, g, bln, W1, b1, W2, b2):
            mu = x.mean(-1, keepdims=True)
            var = ((x - mu) ** 2).mean(-1, keepdims=True)
            xn = (x - mu) / jnp.sqrt(var + 1e-05) * g + bln
            hg = xn @ W1 + b1
            a, gate = jnp.split(hg, 2, -1)
            return a * jax.nn.gelu(gate, approximate=False) @ W2 + b2
        for i in range(DEPTH):
            x = attn_layer(shift_tokens(x), Wqkv[i], q_scale[i], k_scale[i], Wo[i]) + x
            x = ffn_layer(shift_tokens(x), ln_g[i], ln_b[i], W1[i], b1[i], W2[i], b2[i]) + x
        return x

    def _L1_attn_ref(x, wq, wk, wv, wo):
        import jax, jax.numpy as jnp
        import numpy as np
        D_HEAD = 128
        ROTARY_BASE = 10000.0
        NEG = 1e+30

        def frac_rope(x, base=ROTARY_BASE):
            rot, skip = jnp.split(x, 2, axis=-1)
            T, W = (rot.shape[-2], rot.shape[-1])
            pos = jnp.arange(T)[:, None]
            dims = jnp.arange(W // 2)
            ang = jnp.power(base, -dims / (W // 2))[None, :]
            rad = pos * ang
            cos = jnp.cos(rad).astype(x.dtype)
            sin = jnp.sin(rad).astype(x.dtype)
            even, odd = jnp.split(rot, 2, axis=-1)
            r_even = even * cos - odd * sin
            r_odd = even * sin + odd * cos
            return jnp.concatenate([r_even, r_odd, skip], axis=-1)
        T = x.shape[1]
        q = jnp.einsum('btm,mhd->bhtd', x, wq)
        k = jnp.einsum('btm,mhd->bhtd', x, wk)
        v = jnp.einsum('btm,mhd->bhtd', x, wv)
        q = frac_rope(q) * D_HEAD ** (-0.5)
        k = frac_rope(k) * D_HEAD ** (-0.5)
        s = jnp.einsum('bhid,bhjd->bhij', q, k)
        i = jnp.arange(T)[:, None]
        j = jnp.arange(T)[None, :]
        s = s - NEG * jnp.less(i, j).astype(s.dtype)
        p = jax.nn.softmax(s, axis=-1)
        o = jnp.einsum('bhij,bhjd->bhid', p, v)
        return jnp.einsum('bhid,hdm->bim', o, wo)

    def _L1_ffn_ref(x, Wg, bg, W1, b1, W2, b2):
        import jax, jax.numpy as jnp
        import numpy as np
        N_EMBED = 128
        FFN_HIDDEN = 512
        NUM_EXPERTS = 8
        TOP_K = 2
        gate_scores = jax.nn.softmax(x @ Wg + bg, axis=-1)
        topk_scores, topk_idx = jax.lax.top_k(gate_scores, TOP_K)
        topk_scores = topk_scores / (jnp.sum(topk_scores, axis=-1, keepdims=True) + 1e-08)
        onehot = jax.nn.one_hot(topk_idx, NUM_EXPERTS, dtype=x.dtype)
        combine_w = jnp.einsum('bsk,bske->bse', topk_scores, onehot)
        output = jnp.zeros_like(x)
        for e in range(NUM_EXPERTS):
            h = jax.nn.gelu(x @ W1[e] + b1[e])
            y = h @ W2[e] + b2[e]
            output = output + y * combine_w[..., e:e + 1]
        return output

    def _L2_attn_ref(x, Wqk, bqk, Wv, bv, gamma, beta, rel_emb):
        import math
        import jax, jax.numpy as jnp
        import numpy as np
        DIM = 128
        DIM_QK = 128
        DIM_V = 128
        CHUNK = 64
        NUM_BUCKETS = 32
        MAX_DISTANCE = 128

        def _rel_pos_bucket(n_q, n_k):
            q_pos = jnp.arange(n_q, dtype=jnp.int32)
            k_pos = jnp.arange(n_k, dtype=jnp.int32)
            rel = k_pos[None, :] - q_pos[:, None]
            n = jnp.maximum(-rel, 0)
            max_exact = NUM_BUCKETS // 2
            is_small = n < max_exact
            n_f = jnp.maximum(n, 1).astype(jnp.float32)
            val_large = max_exact + jnp.log(n_f / max_exact) / math.log(MAX_DISTANCE / max_exact) * (NUM_BUCKETS - max_exact)
            val_large = jnp.minimum(val_large, NUM_BUCKETS - 1)
            bucket = jnp.where(is_small, n.astype(jnp.float32), val_large)
            return bucket.astype(jnp.int32)
        b, s, dim = x.shape
        qk = jax.nn.swish(x @ Wqk + bqk)
        v = jax.nn.swish(x @ Wv + bv)
        os = qk[..., None, :] * gamma + beta
        q, k = (os[..., 0, :], os[..., 1, :])
        c = CHUNK
        nk = s // c
        q = q.reshape(b, nk, c, DIM_QK)
        k = k.reshape(b, nk, c, DIM_QK)
        vc = v.reshape(b, nk, c, DIM_V)
        scale = dim ** (-0.5)
        sim = jnp.einsum('bkiz,bkjz->bkij', q, k) * scale
        bucket = _rel_pos_bucket(c, c)
        bias = rel_emb[bucket, 0] * DIM_QK ** 0.5
        sim = sim + bias
        future = jnp.triu(jnp.ones((c, c), dtype=bool), k=1)
        sim = jnp.where(future, -jnp.inf, sim)
        attn = jax.nn.softmax(sim, axis=-1)
        out = jnp.einsum('bkij,bkjz->bkiz', attn, vc)
        return out.reshape(b, s, DIM_V)

    def _L2_ffn_ref(x, router_w, router_b, W1, b1, W2, b2):
        import jax, jax.numpy as jnp
        import numpy as np
        B, L, D, F, E = (2, 128, 128, 512, 8)
        b, l, d = x.shape
        xf = x.reshape(b * l, d)
        logits = xf @ router_w + router_b
        top1 = jnp.argmax(logits, axis=-1)
        h = jax.nn.gelu(jnp.einsum('td,edf->etf', xf, W1) + b1[:, None, :], approximate=False)
        y_all = jnp.einsum('etf,efd->etd', h, W2) + b2[:, None, :]
        onehot = jax.nn.one_hot(top1, E, dtype=x.dtype)
        yf = jnp.einsum('te,etd->td', onehot, y_all)
        return yf.reshape(b, l, d)

    def _L3_attn_ref(x, Wq, bq, Wk, bk, Wv, bv, Wo, bo):
        import jax, jax.numpy as jnp
        import numpy as np
        NEG = 10000.0
        q = jax.nn.relu(x @ Wq + bq)
        k = jax.nn.relu(x @ Wk + bk)
        v = jax.nn.relu(x @ Wv + bv)
        D = q.shape[-1]
        e = jnp.einsum('bqd,bkd->bqk', q, k) / jnp.sqrt(jnp.float32(D))
        S = e.shape[-1]
        causal = (jnp.arange(S)[None, :] > jnp.arange(S)[:, None]).astype(e.dtype)
        e = e - NEG * causal[None, :, :]
        e = jnp.exp(e - jnp.max(e, axis=-1, keepdims=True))
        attn = e / jnp.sum(e, axis=-1, keepdims=True)
        y = jnp.einsum('bqk,bkd->bqd', attn, v)
        return jax.nn.relu(y @ Wo + bo)

    def _L3_ffn_ref(x, Wg, W1, b1, W2, b2):
        import jax, jax.numpy as jnp
        import numpy as np
        DIM, HIDDEN, E = (128, 512, 8)
        B, L = (2, 256)
        gate_logits = jnp.einsum('bld,ed->ble', x, Wg)
        top1 = jnp.argmax(gate_logits, axis=-1)
        out = jnp.zeros_like(x)
        for e in range(E):
            mask = (top1 == e)[..., None]
            h = jax.nn.gelu(jnp.einsum('bld,dh->blh', x, W1[e]) + b1[e], approximate=False)
            y = jnp.einsum('blh,hd->bld', h, W2[e]) + b2[e]
            out = jnp.where(mask, y, out)
        return out
    x = L0_attn_x
    x = x + _L0_attn_ref(_layernorm(x, axis=-1), L0_attn_W_write, L0_attn_W_gate, L0_attn_W_out, L0_attn_W_beta, L0_attn_W_alpha, L0_attn_dt_bias, L0_attn_A_log)
    x = x + _L0_ffn_ref(_layernorm(x, axis=-1), L0_ffn_Wqkv, L0_ffn_q_scale, L0_ffn_k_scale, L0_ffn_Wo, L0_ffn_ln_g, L0_ffn_ln_b, L0_ffn_W1, L0_ffn_b1, L0_ffn_W2, L0_ffn_b2)
    x = x + _L1_attn_ref(_layernorm(x, axis=-1), L1_attn_wq, L1_attn_wk, L1_attn_wv, L1_attn_wo)
    x = x + _L1_ffn_ref(_layernorm(x, axis=-1), L1_ffn_Wg, L1_ffn_bg, L1_ffn_W1, L1_ffn_b1, L1_ffn_W2, L1_ffn_b2)
    x = x + _L2_attn_ref(_layernorm(x, axis=-1), L2_attn_Wqk, L2_attn_bqk, L2_attn_Wv, L2_attn_bv, L2_attn_gamma, L2_attn_beta, L2_attn_rel_emb)
    x = x + _L2_ffn_ref(_layernorm(x, axis=-1), L2_ffn_router_w, L2_ffn_router_b, L2_ffn_W1, L2_ffn_b1, L2_ffn_W2, L2_ffn_b2)
    x = x + _L3_attn_ref(_layernorm(x, axis=-1), L3_attn_Wq, L3_attn_bq, L3_attn_Wk, L3_attn_bk, L3_attn_Wv, L3_attn_bv, L3_attn_Wo, L3_attn_bo)
    x = x + _L3_ffn_ref(_layernorm(x, axis=-1), L3_ffn_Wg, L3_ffn_W1, L3_ffn_b1, L3_ffn_W2, L3_ffn_b2)
    return x

_drawn_inputs = setup_inputs


def setup_inputs(seed=0):
    import zlib

    import numpy as np

    out = dict(_drawn_inputs(seed))
    spreads = {'L0_ffn_q_scale': (1.0, 0.6),
     'L0_ffn_k_scale': (1.0, 0.6),
     'L0_ffn_ln_g': (1.0, 0.6),
     'L0_ffn_ln_b': (0.0, 0.8),
     'L0_ffn_b1': (0.0, 0.38),
     'L0_ffn_b2': (0.0, 0.1),
     'L2_attn_bqk': (0.0, 2.0),
     'L2_attn_bv': (0.0, 0.1),
     'L2_attn_beta': (0.0, 0.8),
     'L3_attn_bq': (0.0, 0.8),
     'L3_attn_bk': (0.0, 0.8),
     'L3_attn_bv': (0.0, 0.572),
     'L3_attn_bo': (0.0, 0.371)}
    factors = {'L0_attn_W_write': 8.0,
     'L0_attn_W_gate': 8.0,
     'L0_attn_W_out': 8.0,
     'L0_attn_W_beta': 8.0,
     'L0_attn_W_alpha': 8.0,
     'L1_attn_wq': 4.449,
     'L1_attn_wk': 4.184,
     'L1_ffn_bg': 2.75,
     'L1_ffn_b1': 4.883,
     'L2_attn_Wqk': 8.0,
     'L2_attn_gamma': 8.0,
     'L2_ffn_b1': 8.0,
     'L2_ffn_b2': 6.593,
     'L3_attn_Wq': 7.531,
     'L3_attn_Wk': 6.953,
     'L3_ffn_b1': 8.0,
     'L3_ffn_b2': 6.78}
    for name, (base, spread) in spreads.items():
        noise = np.random.default_rng([zlib.crc32(name.encode()), seed]).standard_normal(out[name].shape)
        drawn = base * np.exp(spread * noise) if base else spread * noise
        out[name] = jnp.asarray(drawn.astype(out[name].dtype))
    for name, factor in factors.items():
        out[name] = (out[name] * factor).astype(out[name].dtype)
    return out
```

```python
import math

import numpy as np

import concourse.bass as bass
from concourse import mybir
from contextlib import ExitStack

F32 = mybir.dt.float32
ALU = mybir.AluOpType
ACT = mybir.ActivationFunctionType
AX = mybir.AxisListType.X

P = 128
SEQS = 8
TOKENS = 512
TILES = TOKENS // P
LN_EPS = 1e-5
NEVER = -3.0e38


class Phase:

    def __init__(self, nc, name, ctx):
        self.nc, self.name, self.ctx = nc, name, ctx
        self.sems = []

    def sb(self, name, shape, dtype=F32):
        return self.ctx.enter_context(self.nc.sbuf_tensor(f"{self.name}_{name}", shape, dtype))

    def ps(self, name, shape, dtype=F32):
        return self.ctx.enter_context(self.nc.psum_tensor(f"{self.name}_{name}", shape, dtype))

    def sem(self, name):
        s = self.nc.alloc_semaphore(f"{self.name}_{name}")
        self.sems.append(s)
        return s


def run_phase(nc, name, body):
    with ExitStack() as ctx:
        ph = Phase(nc, name, ctx)
        body(ph)
    nc.clear_and_free_semaphores(ph.sems)
    nc.all_engine_barrier()


def layernorm_pass(nc, g, name):

    def body(ph):
        stats = ph.sb("stats", [P, SEQS * TILES, 6])
        mean_var = ph.sb("mean_var", [P, SEQS * TILES, 2])
        var_eps = ph.sb("var_eps", [P, SEQS * TILES])
        rstd = ph.sb("rstd", [P, SEQS * TILES])
        x_hat = ph.sb("x_hat", [P, 2, TOKENS])
        turned = [ph.ps(f"turned{i}", [P, TOKENS]) for i in range(2)]
        stats_ready = ph.sem("stats_ready")
        aggregated = ph.sem("aggregated")
        var_ready = ph.sem("var_ready")
        rstd_ready = ph.sem("rstd_ready")
        x_hat_ready = [ph.sem(f"x_hat_ready{i}") for i in range(2)]
        turned_ready = [ph.sem(f"turned_ready{i}") for i in range(2)]
        turned_used = [ph.sem(f"turned_used{i}") for i in range(2)]
        PAIRS = SEQS // 2

        with nc.Block() as block:

            @block.vector
            def _(dve):
                with dve.Fori(0, SEQS) as s:
                    for t in range(TILES):
                        last = nc.vector.bn_stats(stats[:, bass.ds(s * TILES + t, 1), :], g.X[:, bass.ds(s, 1), t * P:(t + 1) * P])
                    last.then_inc(stats_ready, 1)
                dve.wait_ge(stats_ready, SEQS)
                for n in range(SEQS * TILES):
                    last = nc.vector.bn_aggr(mean_var[:, n, :], stats[:, n, :])
                last.then_inc(aggregated, 1)
                dve.wait_ge(aggregated, 1)
                nc.vector.tensor_scalar(var_eps[:], mean_var[:, :, 1], LN_EPS, None, ALU.add).then_inc(var_ready, 1)
                dve.wait_ge(rstd_ready, 1)
                for i in range(2):
                    dve.sem_inc(x_hat_ready[i], 1)
                with dve.Fori(1, PAIRS + 1) as pair:
                    for i in range(2):
                        dve.wait_ge(turned_ready[i], pair)
                        for t in range(TILES):
                            row = pair * (2 * TILES) + ((i - 2) * TILES + t)
                            last = nc.vector.tensor_scalar(
                                x_hat[:, i, t * P:(t + 1) * P], g.X[:, bass.ds(pair * 2 + (i - 2), 1), t * P:(t + 1) * P],
                                mean_var[:, bass.ds(row, 1), 0], rstd[:, bass.ds(row, 1)], ALU.subtract, ALU.mult)
                        last.then_inc(x_hat_ready[i], 1)

            @block.gpsimd
            def _(pool):
                pool.wait_ge(var_ready, 1)
                nc.gpsimd.tensor_tensor(rstd[:], var_eps[:], g.minus_half[:, 0:SEQS * TILES], ALU.pow).then_inc(rstd_ready, 1)

            @block.tensor
            def _(pe):
                for i in range(2):
                    pe.sem_inc(turned_ready[i], 1)
                with pe.Fori(1, PAIRS + 1) as pair:
                    for i in range(2):
                        pe.wait_ge(x_hat_ready[i], pair + 1)
                        pe.wait_ge(turned_used[i], pair)
                        for t in range(TILES):
                            last = nc.tensor.transpose(turned[i][:, t * P:(t + 1) * P], x_hat[:, i, t * P:(t + 1) * P], g.ident[:])
                        last.then_inc(turned_ready[i], 1)

            @block.scalar
            def _(act):
                for i in range(2):
                    act.sem_inc(turned_used[i], 1)
                with act.Fori(1, PAIRS + 1) as pair:
                    for i in range(2):
                        act.wait_ge(turned_ready[i], pair + 1)
                        nc.scalar.copy(g.XH[:, bass.ds(pair * 2 + (i - 2), 1), :], turned[i][:]).then_inc(turned_used[i], 1)

    run_phase(nc, name, body)


def moe_phase(nc, g, name, w, gelu, top2):
    E, FC = 8, 4

    def body(ph):
        w1 = ph.sb("w1", [P, E, FC, P])
        w2 = ph.sb("w2", [P, E, FC, P])
        b1 = ph.sb("b1", [P, E, FC])
        b2 = ph.sb("b2", [E, P])
        wg = ph.sb("wg", [P, E])
        wg_rows = ph.sb("wg_rows", [E, P])
        bg = ph.sb("bg", [P, E])
        xs = ph.sb("xs", [P, TOKENS])
        hid = ph.sb("hid", [P, 2, FC, TOKENS])
        score = ph.sb("score", [P, TILES, E])
        tmp = ph.sb("tmp", [P, TILES, E])
        tmp2 = ph.sb("tmp2", [P, TILES, E])
        pick = ph.sb("pick", [P, 2, TILES, E])
        combine = ph.sb("combine", [P, TILES, E])
        small = ph.sb("small", [P, 8, TILES])
        combine_t = ph.sb("combine_t", [E, TOKENS])
        acc = ph.sb("acc", [P, TOKENS])
        hid_ps = [ph.ps(f"hid_ps{i}", [P, TOKENS]) for i in range(4)]
        y_ps = [ph.ps(f"y_ps{i}", [P, TOKENS]) for i in range(2)]
        small_ps = ph.ps("small_ps", [P, TOKENS])
        bias_ps = ph.ps("bias_ps", [P, TOKENS])
        loaded = ph.sem("loaded")
        router_turned = ph.sem("router_turned")
        router_ready = ph.sem("router_ready")
        xs_ready = ph.sem("xs_ready")
        logits_ready = ph.sem("logits_ready")
        step = ph.sem("routing_step")
        probs_ready = ph.sem("probs_ready")
        combine_ready = ph.sem("combine_ready")
        combine_turned = ph.sem("combine_turned")
        combine_t_ready = ph.sem("combine_t_ready")
        bias_ready = ph.sem("bias_ready")
        hid_done = ph.sem("hid_done")
        gelu_done = ph.sem("gelu_done")
        y_done = ph.sem("y_done")
        y_added = ph.sem("y_added")
        acc_started = ph.sem("acc_started")
        STEPS = 25 if top2 else 6
        has_gbias = w["bg"] is not None
        wg_by_expert = w["wg_t"] is not None
        LOADS = 16 * (4 + 1 + (1 if has_gbias else 0))

        with nc.Block() as block:

            @block.sync
            def _(sp):
                if wg_by_expert:
                    sp.dma_start(wg_rows[:], w["wg_t"]).then_inc(loaded, 16)
                else:
                    sp.dma_start(wg[:], w["wg"]).then_inc(loaded, 16)
                sp.dma_start(w1[:].rearrange("p e b f -> p e (b f)"), w["w1"].rearrange("e d f -> d e f")).then_inc(loaded, 16)
                sp.dma_start(w2[:], w["w2"].rearrange("e (b f) d -> f e b d", f=P)).then_inc(loaded, 16)
                sp.dma_start(b1[:], w["b1"].rearrange("e (b f) -> f e b", f=P), allow_slow_non_contiguous=True).then_inc(loaded, 16)
                sp.dma_start(b2[:], w["b2"]).then_inc(loaded, 16)
                if has_gbias:
                    sp.dma_start(bg[:], w["bg"].partition_broadcast(P)).then_inc(loaded, 16)

            @block.scalar
            def _(act):
                act.sem_inc(gelu_done, E * FC)
                act.wait_ge(loaded, LOADS)
                with act.Fori(1, SEQS + 1) as s:
                    act.wait_ge(hid_done, s * (E * FC))
                    nc.scalar.copy(xs[:], g.XH[:, bass.ds(s - 1, 1), :]).then_inc(xs_ready, 1)
                    if top2:
                        act.wait_ge(step, s * STEPS + 3)
                        nc.scalar.activation(score[:], tmp[:], ACT.Exp).then_inc(probs_ready, 1)
                    for e in range(E):
                        for b in range(FC):
                            n = e * FC + b
                            act.wait_ge(hid_done, s * (E * FC) + (n + 1))
                            if b == 0:
                                act.wait_ge(y_done, s * E + (e - 1) if e >= 2 else (s - 1) * E + (e + E - 1))
                            nc.scalar.activation(hid[:, e % 2, b, :], hid_ps[n % 4][:], gelu, bias=b1[:, e, b:b + 1]).then_inc(gelu_done, 1)
                        if e == 1:
                            act.wait_ge(combine_turned, s)
                            nc.scalar.copy(combine_t[:], small_ps[0:E, :]).then_inc(combine_t_ready, 1)

            @block.tensor
            def _(pe):
                pe.sem_inc(hid_done, E * FC)
                pe.sem_inc(y_done, E)
                pe.wait_ge(loaded, LOADS)
                if wg_by_expert:
                    nc.tensor.transpose(small_ps[:, 0:E], wg_rows[:], g.ident[0:E, 0:E]).then_inc(router_turned, 1)
                    pe.wait_ge(router_ready, 1)
                with pe.Fori(1, SEQS + 1) as s:

                    def down(e):
                        pe.wait_ge(gelu_done, s * (E * FC) + FC * (e + 1))
                        pe.wait_ge(y_added, s * E + (e - 1) if e >= 2 else (s - 1) * E + (e + E - 1))
                        for t in range(TILES):
                            for b in range(FC):
                                last = nc.tensor.matmul(y_ps[e % 2][:, t * P:(t + 1) * P], hid[:, e % 2, b, t * P:(t + 1) * P],
                                                        w2[:, e, b, :], start=(b == 0), stop=(b == FC - 1))
                        last.then_inc(y_done, 1)

                    pe.wait_ge(xs_ready, s)
                    for t in range(TILES):
                        last = nc.tensor.matmul(small_ps[:, t * E:(t + 1) * E], xs[:, t * P:(t + 1) * P], wg[:], start=True, stop=True)
                    last.then_inc(logits_ready, 1)
                    for e in range(E):
                        for b in range(FC):
                            n = e * FC + b
                            pe.wait_ge(gelu_done, s * (E * FC) + (n - 3) if n >= 4 else (s - 1) * (E * FC) + (n + E * FC - 3))
                            nc.tensor.matmul(hid_ps[n % 4][:], w1[:, e, b, :], xs[:], start=True, stop=True).then_inc(hid_done, 1)
                        if e == 1:
                            pe.wait_ge(combine_ready, s)
                            for t in range(TILES):
                                last = nc.tensor.transpose(small_ps[0:E, t * P:(t + 1) * P], combine[:, t, :], g.ident[:])
                            last.then_inc(combine_turned, 1)
                        if e == 2:
                            pe.wait_ge(combine_t_ready, s)
                            for t in range(TILES):
                                last = nc.tensor.matmul(bias_ps[:, t * P:(t + 1) * P], combine_t[:, t * P:(t + 1) * P], b2[:], start=True, stop=True)
                            last.then_inc(bias_ready, 1)
                        if e >= 1:
                            down(e - 1)
                    down(E - 1)

            @block.vector
            def _(dve):
                dve.sem_inc(step, STEPS)
                dve.sem_inc(y_added, E)
                dve.wait_ge(loaded, LOADS)
                if wg_by_expert:
                    dve.wait_ge(router_turned, 1)
                    nc.vector.tensor_copy(wg[:], small_ps[:, 0:E]).then_inc(router_ready, 1)
                with dve.Fori(1, SEQS + 1) as s:
                    made = 0

                    def done(ins):
                        nonlocal made
                        made += 1
                        ins.then_inc(step, 1)
                        dve.wait_ge(step, s * STEPS + made)

                    def spread(row):
                        return small[:, row, :].unsqueeze(2).to_broadcast([P, TILES, E])

                    def first_of(src, row, onehot):
                        done(nc.vector.tensor_tensor(tmp[:], src, spread(row), ALU.is_equal))
                        done(nc.vector.tensor_tensor(tmp[:], tmp[:], g.rank8[:].unsqueeze(1).to_broadcast([P, TILES, E]), ALU.mult))
                        done(nc.vector.tensor_reduce(small[:, row + 2, :], tmp[:], AX, ALU.max))
                        done(nc.vector.tensor_tensor(onehot, tmp[:], spread(row + 2), ALU.is_equal))

                    dve.wait_ge(logits_ready, s)
                    logits = small_ps[:, 0:TILES * E].rearrange("p (t e) -> p t e", e=E)
                    if has_gbias:
                        done(nc.vector.tensor_tensor(score[:], logits, bg[:].unsqueeze(1).to_broadcast([P, TILES, E]), ALU.add))
                    else:
                        done(nc.vector.tensor_copy(score[:], logits))
                    done(nc.vector.tensor_reduce(small[:, 0, :], score[:], AX, ALU.max))
                    if top2:
                        done(nc.vector.tensor_tensor(tmp[:], score[:], spread(0), ALU.subtract))
                        dve.wait_ge(probs_ready, s)
                        done(nc.vector.tensor_reduce(small[:, 4, :], score[:], AX, ALU.add))
                        done(nc.vector.reciprocal(small[:, 5, :], small[:, 4, :]))
                        done(nc.vector.tensor_tensor(score[:], score[:], spread(5), ALU.mult))
                        done(nc.vector.tensor_reduce(small[:, 0, :], score[:], AX, ALU.max))
                        first_of(score[:], 0, pick[:, 0])
                        done(nc.vector.scalar_tensor_tensor(tmp2[:], pick[:, 0], -4.0, score[:], ALU.mult, ALU.add))
                        done(nc.vector.tensor_reduce(small[:, 1, :], tmp2[:], AX, ALU.max))
                        first_of(tmp2[:], 1, pick[:, 1])
                        done(nc.vector.tensor_tensor(small[:, 4, :], small[:, 0, :], small[:, 1, :], ALU.add))
                        done(nc.vector.tensor_scalar(small[:, 5, :], small[:, 4, :], 1e-8, None, ALU.add))
                        done(nc.vector.reciprocal(small[:, 4, :], small[:, 5, :]))
                        for k in range(2):
                            done(nc.vector.tensor_tensor(small[:, 6 + k, :], small[:, k, :], small[:, 4, :], ALU.mult))
                            done(nc.vector.tensor_tensor(pick[:, k], pick[:, k], spread(6 + k), ALU.mult))
                        done(nc.vector.tensor_tensor(combine[:], pick[:, 0], pick[:, 1], ALU.add))
                    else:
                        first_of(score[:], 0, combine[:])
                    assert made == STEPS
                    dve.sem_inc(combine_ready, 1)
                    dve.wait_ge(bias_ready, s)
                    nc.vector.tensor_tensor(acc[:], bias_ps[:], g.X[:, bass.ds(s - 1, 1), :].rearrange("p a t -> p (a t)"), ALU.add).then_inc(acc_started, 1)
                    dve.wait_ge(acc_started, s)
                    for e in range(E):
                        dve.wait_ge(y_done, s * E + (e + 1))
                        if e:
                            dve.wait_ge(y_added, s * E + e)
                        for t in range(TILES):
                            cols = slice(t * P, (t + 1) * P)
                            out = acc[:, cols] if e < E - 1 else g.X[:, bass.ds(s - 1, 1), cols].rearrange("p a t -> p (a t)")
                            last = nc.vector.scalar_tensor_tensor(out, y_ps[e % 2][:, cols], combine[:, t, e:e + 1], acc[:, cols], ALU.mult, ALU.add)
                        last.then_inc(y_added, 1)

    run_phase(nc, name, body)


def softmax_attention_phase(nc, g, name, w, causal_only):
    rope = causal_only

    def body(ph):
        wq = ph.sb("wq", [P, P])
        wk = ph.sb("wk", [P, P])
        wv = ph.sb("wv", [P, P])
        wo = ph.sb("wo", [P, P])
        mask = ph.sb("mask", [P, 7 * P])
        if rope:
            wq_rot = ph.sb("wq_rot", [P, 64])
            wk_rot = ph.sb("wk_rot", [P, 64])
            cos = ph.sb("cos", [P, TOKENS])
            sin = ph.sb("sin", [64, TOKENS])
            rotated = ph.sb("rotated", [64, TOKENS])
        else:
            bias = ph.sb("bias", [P, 3])
            bo = ph.sb("bo", [P, P])
            y = ph.sb("y", [P, P])
        xs = ph.sb("xs", [P, TOKENS])
        q_t = ph.sb("q_t", [P, TOKENS])
        k_t = ph.sb("k_t", [P, TOKENS])
        v_t = ph.sb("v_t", [P, TOKENS])
        vo = ph.sb("vo", [P, TILES, P])
        masked = ph.sb("masked", [P, 2, TOKENS])
        probs = ph.sb("probs", [P, 2, TOKENS])
        probs_t = ph.sb("probs_t", [P, 2, TOKENS])
        neg_max = ph.sb("neg_max", [P, TILES])
        row_sum = ph.sb("row_sum", [P, TILES])
        inv_sum = ph.sb("inv_sum", [P, TILES])
        proj_ps = [ph.ps(f"proj_ps{i}", [P, TOKENS]) for i in range(4)]
        score_ps = [ph.ps(f"score_ps{i}", [P, TOKENS]) for i in range(2)]
        turn_ps = ph.ps("turn_ps", [P, TOKENS])
        out_ps = [ph.ps("out_ps", [P, TOKENS]), proj_ps[3]]
        names = ["loaded", "rot_ready", "xs_ready", "q_projected", "k_projected", "v_projected", "q_scaled", "q_rotated", "q_ready",
                 "k_scaled", "k_rotated", "k_ready", "v_ready", "vo_done", "vo_ready", "scores_done", "masked_ready",
                 "max_ready", "probs_ready", "turned", "probs_t_ready", "out_done", "inv_ready", "y_ready", "x_added"]
        q = {n: ph.sem(n) for n in names}
        LOADS = 16 * (7 if rope else 9)
        SCALE = 1.0 if rope else float(P) ** -0.5
        def keys(t):
            return t + 1 if causal_only else TILES

        with nc.Block() as block:

            @block.sync
            def _(sp):
                for dst, key in ((wq, "wq"), (wk, "wk"), (wv, "wv"), (wo, "wo"), (mask, "mask")):
                    sp.dma_start(dst[:], w[key]).then_inc(q["loaded"], 16)
                if rope:
                    sp.dma_start(cos[:], w["cos"]).then_inc(q["loaded"], 16)
                    sp.dma_start(sin[:], w["sin"]).then_inc(q["loaded"], 16)
                else:
                    for i, key in enumerate(("bq", "bk", "bv")):
                        sp.dma_start(bias[:, i:i + 1], w[key].unsqueeze(1)).then_inc(q["loaded"], 16)
                    sp.dma_start(bo[:], w["bo"].partition_broadcast(P)).then_inc(q["loaded"], 16)

            @block.scalar
            def _(act):
                act.sem_inc(q["probs_ready"], TILES)
                act.wait_ge(q["loaded"], LOADS)
                with act.Fori(1, SEQS + 1) as s:

                    def copy_probs_t(t):
                        act.wait_ge(q["turned"], (s - 1) * TILES + (t + 1))
                        act.wait_ge(q["out_done"], s * TILES + (t - 1) if t >= 2 else (s - 1) * TILES + (t + 3))
                        n = keys(t) * P
                        nc.scalar.copy(probs_t[:, t % 2, 0:n], turn_ps[:, 0:n]).then_inc(q["probs_t_ready"], 1)

                    nc.scalar.copy(xs[:], g.XH[:, bass.ds(s - 1, 1), :]).then_inc(q["xs_ready"], 1)
                    if not rope:
                        act.wait_ge(q["q_projected"], s)
                        nc.scalar.activation(q_t[:], proj_ps[0][:], ACT.Relu, bias=bias[:, 0:1]).then_inc(q["q_ready"], 1)
                        act.wait_ge(q["k_projected"], s)
                        nc.scalar.activation(k_t[:], proj_ps[2][:], ACT.Relu, bias=bias[:, 1:2]).then_inc(q["k_ready"], 1)
                    act.wait_ge(q["v_projected"], s)
                    if rope:
                        nc.scalar.copy(v_t[:], turn_ps[:]).then_inc(q["v_ready"], 1)
                    else:
                        nc.scalar.activation(v_t[:], turn_ps[:], ACT.Relu, bias=bias[:, 2:3]).then_inc(q["v_ready"], 1)
                    act.wait_ge(q["vo_done"], s)
                    nc.scalar.copy(vo[:].rearrange("p t d -> p (t d)"), out_ps[0][:]).then_inc(q["vo_ready"], 1)
                    for t in range(TILES):
                        act.wait_ge(q["max_ready"], (s - 1) * TILES + (t + 1))
                        n = keys(t) * P
                        nc.scalar.activation(probs[:, t % 2, 0:n], masked[:, t % 2, 0:n], ACT.Exp, bias=neg_max[:, t:t + 1],
                                             accum_out=row_sum[:, t:t + 1]).then_inc(q["probs_ready"], 1)
                        if t:
                            copy_probs_t(t - 1)
                    copy_probs_t(TILES - 1)

            @block.tensor
            def _(pe):
                pe.sem_inc(q["out_done"], TILES)
                pe.wait_ge(q["loaded"], LOADS)
                if rope:
                    pe.wait_ge(q["rot_ready"], 1)
                with pe.Fori(1, SEQS + 1) as s:

                    def scores(t):
                        pe.wait_ge(q["masked_ready"], s * TILES + (t - 1) if t >= 2 else (s - 1) * TILES + (t + 3))
                        nc.tensor.matmul(score_ps[t % 2][:, 0:keys(t) * P], q_t[:, t * P:(t + 1) * P], k_t[:, 0:keys(t) * P],
                                         start=True, stop=True).then_inc(q["scores_done"], 1)

                    pe.wait_ge(q["xs_ready"], s)
                    if rope:
                        nc.tensor.matmul(proj_ps[0][:], wq[:], xs[:], start=True, stop=True)
                        nc.tensor.matmul(proj_ps[1][0:64, :], wq_rot[:], xs[:], start=True, stop=True).then_inc(q["q_projected"], 1)
                        nc.tensor.matmul(proj_ps[2][:], wk[:], xs[:], start=True, stop=True)
                        pe.wait_ge(q["x_added"], s * TILES)
                        nc.tensor.matmul(proj_ps[3][0:64, :], wk_rot[:], xs[:], start=True, stop=True).then_inc(q["k_projected"], 1)
                    else:
                        nc.tensor.matmul(proj_ps[0][:], wq[:], xs[:], start=True, stop=True).then_inc(q["q_projected"], 1)
                        nc.tensor.matmul(proj_ps[2][:], wk[:], xs[:], start=True, stop=True).then_inc(q["k_projected"], 1)
                    nc.tensor.matmul(turn_ps[:], wv[:], xs[:], start=True, stop=True).then_inc(q["v_projected"], 1)
                    pe.wait_ge(q["q_ready"], s)
                    pe.wait_ge(q["k_ready"], s)
                    scores(0)
                    scores(1)
                    pe.wait_ge(q["v_ready"], s)
                    if not rope:
                        pe.wait_ge(q["x_added"], s * TILES)
                    for t in range(TILES):
                        last = nc.tensor.matmul(out_ps[0][:, t * P:(t + 1) * P], v_t[:, t * P:(t + 1) * P], wo[:], start=True, stop=True)
                    last.then_inc(q["vo_done"], 1)
                    pe.wait_ge(q["vo_ready"], s)
                    for t in range(TILES):
                        pe.wait_ge(q["probs_ready"], s * TILES + (t + 1))
                        for k in range(keys(t)):
                            last = nc.tensor.transpose(turn_ps[:, k * P:(k + 1) * P], probs[:, t % 2, k * P:(k + 1) * P], g.ident[:])
                        last.then_inc(q["turned"], 1)
                        if t + 2 < TILES:
                            scores(t + 2)
                        pe.wait_ge(q["probs_t_ready"], (s - 1) * TILES + (t + 1))
                        if t >= 2:
                            pe.wait_ge(q["x_added"], s * TILES + (t - 1))
                        for k in range(keys(t)):
                            last = nc.tensor.matmul(out_ps[t % 2][:, 0:P], probs_t[:, t % 2, k * P:(k + 1) * P], vo[:, k, :],
                                                    start=(k == 0), stop=(k == keys(t) - 1))
                        last.then_inc(q["out_done"], 1)

            @block.vector
            def _(dve):
                dve.sem_inc(q["masked_ready"], TILES)
                dve.sem_inc(q["x_added"], TILES)
                dve.wait_ge(q["loaded"], LOADS)
                if rope:
                    for src, dst in ((wq, wq_rot), (wk, wk_rot)):
                        nc.vector.tensor_scalar(dst[:, 0:32], src[:, 32:64], -1.0, None, ALU.mult)
                        last = nc.vector.tensor_copy(dst[:, 32:64], src[:, 0:32])
                    last.then_inc(q["rot_ready"], 1)
                with dve.Fori(1, SEQS + 1) as s:

                    def add_output(t):
                        cols = slice(t * P, (t + 1) * P)
                        xt = g.X[:, bass.ds(s - 1, 1), cols].rearrange("p a t -> p (a t)")
                        out = out_ps[t % 2][:, 0:P]
                        dve.wait_ge(q["out_done"], s * TILES + (t + 1))
                        nc.vector.reciprocal(inv_sum[:, t:t + 1], row_sum[:, t:t + 1]).then_inc(q["inv_ready"], 1)
                        dve.wait_ge(q["inv_ready"], (s - 1) * TILES + (t + 1))
                        if rope:
                            nc.vector.scalar_tensor_tensor(xt, out, inv_sum[:, t:t + 1], xt, ALU.mult, ALU.add).then_inc(q["x_added"], 1)
                        else:
                            nc.vector.scalar_tensor_tensor(y[:], out, inv_sum[:, t:t + 1], bo[:], ALU.mult, ALU.add).then_inc(q["y_ready"], 1)
                            dve.wait_ge(q["y_ready"], (s - 1) * TILES + (t + 1))
                            nc.vector.scalar_tensor_tensor(xt, y[:], 0.0, xt, ALU.max, ALU.add).then_inc(q["x_added"], 1)

                    if rope:
                        for side, dst, a in (("q", q_t, 0), ("k", k_t, 2)):
                            dve.wait_ge(q[side + "_projected"], s)
                            if side == "k":
                                dve.wait_ge(q["q_ready"], s)
                            nc.vector.tensor_tensor(dst[:], proj_ps[a][:], cos[:], ALU.mult).then_inc(q[side + "_scaled"], 1)
                            nc.vector.tensor_tensor(rotated[:], proj_ps[a + 1][0:64, :], sin[:], ALU.mult).then_inc(q[side + "_rotated"], 1)
                            dve.wait_ge(q[side + "_scaled"], s)
                            dve.wait_ge(q[side + "_rotated"], s)
                            nc.vector.tensor_tensor(dst[0:64, :], dst[0:64, :], rotated[:], ALU.add).then_inc(q[side + "_ready"], 1)
                    for t in range(TILES):
                        n = keys(t) * P
                        dve.wait_ge(q["scores_done"], (s - 1) * TILES + (t + 1))
                        dve.wait_ge(q["probs_ready"], s * TILES + (t - 1) if t >= 2 else (s - 1) * TILES + (t + 3))
                        at = (TILES - 1 - t) * P
                        nc.vector.scalar_tensor_tensor(masked[:, t % 2, 0:n], score_ps[t % 2][:, 0:n], SCALE, mask[:, at:at + n],
                                                       ALU.mult, ALU.add).then_inc(q["masked_ready"], 1)
                        dve.wait_ge(q["masked_ready"], s * TILES + (t + 1))
                        nc.vector.tensor_reduce(neg_max[:, t:t + 1], masked[:, t % 2, 0:n], AX, ALU.max, negate=True).then_inc(q["max_ready"], 1)
                        if t:
                            add_output(t - 1)
                    add_output(TILES - 1)

    run_phase(nc, name, body)


def chunk_attention_phase(nc, g, name, w):
    PAIRS = SEQS // 2
    SPAN = 2 * P - 1

    def body(ph):
        wqk = ph.sb("wqk", [P, P])
        wv = ph.sb("wv", [P, P])
        bqk = ph.sb("bqk", [P, 1])
        bv = ph.sb("bv", [P, P])
        gamma = ph.sb("gamma", [P, 2])
        beta = ph.sb("beta", [P, 2])
        rel = ph.sb("rel", [32, 1])
        rel_wide = ph.sb("rel_wide", [32, P])
        bucket = ph.sb("bucket", [32, SPAN])
        by_distance = ph.sb("by_distance", [P, SPAN])
        mask = ph.sb("mask", [P, P])
        bias = ph.sb("bias", [P, P])
        xs = ph.sb("xs", [P, 2, TOKENS])
        qk = ph.sb("qk", [P, 2, TOKENS])
        q_t = ph.sb("q_t", [P, 2, TOKENS])
        k_t = ph.sb("k_t", [P, 2, TOKENS])
        v_raw = ph.sb("v_raw", [P, 2, TOKENS])
        v = ph.sb("v", [P, 2, TOKENS])
        masked = ph.sb("masked", [P, 2, TOKENS])
        probs = ph.sb("probs", [P, 2, TOKENS])
        probs_t = ph.sb("probs_t", [P, 2, TOKENS])
        top = ph.sb("top", [P, 2, TILES])
        total = ph.sb("total", [P, 2, TILES])
        inv = ph.sb("inv", [P, 2, TILES])
        a_ps = [ph.ps(f"a_ps{i}", [P, TOKENS]) for i in range(2)]
        v_ps = [ph.ps(f"v_ps{i}", [P, TOKENS]) for i in range(2)]
        s_ps = [ph.ps(f"s_ps{i}", [P, TOKENS]) for i in range(2)]
        o_ps = [ph.ps(f"o_ps{i}", [P, TOKENS]) for i in range(2)]
        skew = nc.dram_tensor(f"{name}_skew", [P, SPAN], F32, kind="Internal").ap()
        names = ["loaded", "rel_ready", "distance_ready", "distance_copied", "skew_written", "skew_read", "bias_ready",
                 "xs_ready", "qk_projected", "v_projected", "qk_ready", "v_raw_ready", "v_ready", "q_ready",
                 "scores_done", "masked_ready", "max_ready", "centred", "probs_ready", "sum_ready", "inv_ready", "turned",
                 "probs_t_ready", "out_done", "x_added"]
        q = {n: ph.sem(n) for n in names}
        LOADS = 16 * 9

        with nc.Block() as block:

            @block.sync
            def _(sp):
                for dst, src in ((wqk[:], w["Wqk"]), (wv[:], w["Wv"]), (bqk[:], w["bqk"].unsqueeze(1)),
                                 (bv[:], w["bv"].partition_broadcast(P)), (rel[:], w["rel_emb"]),
                                 (bucket[:], w["bucket"]), (mask[:], w["chunk_mask"])):
                    sp.dma_start(dst, src).then_inc(q["loaded"], 16)
                sp.dma_start(gamma[:], w["gamma"].rearrange("a d -> d a"), allow_slow_non_contiguous=True).then_inc(q["loaded"], 16)
                sp.dma_start(beta[:], w["beta"].rearrange("a d -> d a"), allow_slow_non_contiguous=True).then_inc(q["loaded"], 16)
                sp.wait_ge(q["distance_copied"], 1)
                sp.dma_start(skew, by_distance[:]).then_inc(q["skew_written"], 16)
                sp.wait_ge(q["skew_written"], 16)
                skewed = bass.AP(skew.tensor, P - 1, [[SPAN - 1, P], [1, P]])
                sp.dma_start(bias[:], skewed).then_inc(q["skew_read"], 16)

            @block.scalar
            def _(act):
                act.wait_ge(q["loaded"], LOADS)
                act.wait_ge(q["distance_ready"], 1)
                nc.scalar.mul(by_distance[:], o_ps[0][:, 0:SPAN], float(P) ** 0.5).then_inc(q["distance_copied"], 1)
                with act.Fori(1, PAIRS + 1) as pair:
                    def at(i):
                        return (pair - 1) * 2 + (i + 1)

                    for i in range(2):
                        nc.scalar.copy(xs[:, i], g.XH[:, bass.ds(pair * 2 + (i - 2), 1), :].rearrange("p a t -> p (a t)")).then_inc(q["xs_ready"], 1)
                    for i in range(2):
                        act.wait_ge(q["qk_projected"], at(i))
                        nc.scalar.activation(qk[:, i], a_ps[i][:], ACT.Silu, bias=bqk[:]).then_inc(q["qk_ready"], 1)
                    for i in range(2):
                        act.wait_ge(q["v_raw_ready"], at(i))
                        nc.scalar.activation(v[:, i], v_raw[:, i], ACT.Silu).then_inc(q["v_ready"], 1)
                    for i in range(2):
                        act.wait_ge(q["centred"], at(i))
                        nc.scalar.activation(probs[:, i], masked[:, i], ACT.Exp).then_inc(q["probs_ready"], 1)
                    for i in range(2):
                        act.wait_ge(q["turned"], at(i))
                        nc.scalar.copy(probs_t[:, i], a_ps[i][:]).then_inc(q["probs_t_ready"], 1)

            @block.tensor
            def _(pe):
                pe.sem_inc(q["out_done"], 2)
                pe.wait_ge(q["loaded"], LOADS)
                pe.wait_ge(q["rel_ready"], 1)
                nc.tensor.matmul(o_ps[0][:, 0:SPAN], rel_wide[:], bucket[:], start=True, stop=True).then_inc(q["distance_ready"], 1)
                pe.wait_ge(q["distance_copied"], 1)
                with pe.Fori(1, PAIRS + 1) as pair:
                    def at(i):
                        return (pair - 1) * 2 + (i + 1)

                    for i in range(2):
                        pe.wait_ge(q["xs_ready"], at(i))
                        nc.tensor.matmul(a_ps[i][:], wqk[:], xs[:, i], start=True, stop=True).then_inc(q["qk_projected"], 1)
                        for t in range(TILES):
                            last = nc.tensor.matmul(v_ps[i][:, t * P:(t + 1) * P], xs[:, i, t * P:(t + 1) * P], wv[:], start=True, stop=True)
                        last.then_inc(q["v_projected"], 1)
                    for i in range(2):
                        pe.wait_ge(q["q_ready"], at(i))
                        for t in range(TILES):
                            last = nc.tensor.matmul(s_ps[i][:, t * P:(t + 1) * P], q_t[:, i, t * P:(t + 1) * P], k_t[:, i, t * P:(t + 1) * P],
                                                    start=True, stop=True)
                        last.then_inc(q["scores_done"], 1)
                    for i in range(2):
                        pe.wait_ge(q["probs_ready"], at(i))
                        for t in range(TILES):
                            last = nc.tensor.transpose(a_ps[i][:, t * P:(t + 1) * P], probs[:, i, t * P:(t + 1) * P], g.ident[:])
                        last.then_inc(q["turned"], 1)
                    for i in range(2):
                        pe.wait_ge(q["probs_t_ready"], at(i))
                        pe.wait_ge(q["v_ready"], at(i))
                        pe.wait_ge(q["x_added"], at(i))
                        for t in range(TILES):
                            last = nc.tensor.matmul(o_ps[i][:, t * P:(t + 1) * P], probs_t[:, i, t * P:(t + 1) * P], v[:, i, t * P:(t + 1) * P],
                                                    start=True, stop=True)
                        last.then_inc(q["out_done"], 1)

            @block.vector
            def _(dve):
                dve.sem_inc(q["x_added"], 2)
                dve.wait_ge(q["loaded"], LOADS)
                nc.vector.tensor_copy(rel_wide[:], rel[:].to_broadcast([32, P])).then_inc(q["rel_ready"], 1)
                dve.wait_ge(q["skew_read"], 16)
                nc.vector.tensor_tensor(bias[:], bias[:], mask[:], ALU.add).then_inc(q["bias_ready"], 1)
                dve.wait_ge(q["bias_ready"], 1)
                with dve.Fori(1, PAIRS + 1) as pair:
                    def at(i):
                        return (pair - 1) * 2 + (i + 1)

                    def tiles(buf, i):
                        return buf[:, i].rearrange("p (t k) -> p t k", k=P)

                    def spread(col, i):
                        return col[:, i, :].unsqueeze(2).to_broadcast([P, TILES, P])

                    for i in range(2):
                        dve.wait_ge(q["v_projected"], at(i))
                        nc.vector.tensor_tensor(tiles(v_raw, i), v_ps[i][:].rearrange("p (t d) -> p t d", d=P),
                                                bv[:].unsqueeze(1).to_broadcast([P, TILES, P]), ALU.add).then_inc(q["v_raw_ready"], 1)
                        dve.wait_ge(q["qk_ready"], at(i))
                        nc.vector.tensor_scalar(q_t[:, i], qk[:, i], gamma[:, 0:1], beta[:, 0:1], ALU.mult, ALU.add)
                        nc.vector.tensor_scalar(k_t[:, i], qk[:, i], gamma[:, 1:2], beta[:, 1:2], ALU.mult, ALU.add).then_inc(q["q_ready"], 1)
                    for i in range(2):
                        dve.wait_ge(q["scores_done"], at(i))
                        nc.vector.scalar_tensor_tensor(tiles(masked, i), s_ps[i][:].rearrange("p (t k) -> p t k", k=P), float(P) ** -0.5,
                                                       bias[:].unsqueeze(1).to_broadcast([P, TILES, P]), ALU.mult, ALU.add).then_inc(q["masked_ready"], 1)
                        dve.wait_ge(q["masked_ready"], at(i))
                        nc.vector.tensor_reduce(top[:, i], tiles(masked, i), AX, ALU.max).then_inc(q["max_ready"], 1)
                        dve.wait_ge(q["max_ready"], at(i))
                        nc.vector.tensor_tensor(tiles(masked, i), tiles(masked, i), spread(top, i), ALU.subtract).then_inc(q["centred"], 1)
                    for i in range(2):
                        dve.wait_ge(q["probs_ready"], at(i))
                        nc.vector.tensor_reduce(total[:, i], tiles(probs, i), AX, ALU.add).then_inc(q["sum_ready"], 1)
                        dve.wait_ge(q["sum_ready"], at(i))
                        nc.vector.reciprocal(inv[:, i], total[:, i]).then_inc(q["inv_ready"], 1)
                    for i in range(2):
                        dve.wait_ge(q["inv_ready"], at(i))
                        dve.wait_ge(q["out_done"], at(i) + 2)
                        for t in range(TILES):
                            xt = g.X[:, bass.ds(pair * 2 + (i - 2), 1), t * P:(t + 1) * P].rearrange("p a t -> p (a t)")
                            last = nc.vector.scalar_tensor_tensor(xt, o_ps[i][:, t * P:(t + 1) * P], inv[:, i, t:t + 1], xt, ALU.mult, ALU.add)
                        last.then_inc(q["x_added"], 1)

    run_phase(nc, name, body)


def local_transformer_phase(nc, g, name, w):
    LAYERS, HEADS, HD, BLOCK, WIN, BACK = 6, 16, 64, 64, 96, 32
    INNER = HEADS * HD
    CH = INNER // P
    GROUPS = 4
    HPG = HEADS // GROUPS
    HIDDEN = 341
    HCH = [(0, P), (P, P), (2 * P, HIDDEN - 2 * P)]
    PV_HEADS = [(0, 6), (6, 11), (11, 16)]
    A_OF = [0, 1, 2, 3]
    S_OF = [2, 3, 0, 1]

    def body(ph):
        sb = ph.sb
        wqkv = sb("wqkv", [P, 3 * INNER])
        wo = sb("wo", [P, CH, P])
        w1 = sb("w1", [P, 2 * HIDDEN])
        w2 = sb("w2", [P, 3, P])
        b1 = sb("b1", [P, 6])
        ln = sb("ln", [P, 3])
        scales = sb("scales", [P, 2, LAYERS, HD])
        base = sb("base", [P, TILES, 4, HD])
        table = sb("table", [P, TILES, 4, HD])
        band = sb("band", [P, 2, WIN])
        ys = sb("ys", [P, BACK + TOKENS])
        squares = sb("squares", [P, 2 * INNER])
        normed = sb("normed", [P, 2 * INNER])
        rot = sb("rot", [P, 2 * INNER])
        norm2 = sb("norm2", [P, 2 * HEADS])
        norm2c = sb("norm2c", [P, 2 * HEADS])
        inv_norm = sb("inv_norm", [P, 2 * HEADS])
        q_t = sb("q_t", [P, CH, P])
        k_t = sb("k_t", [P, CH, BACK + TOKENS])
        scores = sb("scores", [P, HEADS, WIN])
        probs = sb("probs", [P, HEADS, WIN])
        top = sb("top", [P, HEADS])
        probs_t = sb("probs_t", [WIN, HEADS, P])
        vals = sb("vals", [WIN, 2, HEADS, HD + 1])
        inv_sum = sb("inv_sum", [P, HEADS])
        att = sb("att", [P, INNER])
        att_t = sb("att_t", [P, CH, P])
        y1 = sb("y1", [P, TOKENS])
        y1s = sb("y1s", [P, TOKENS])
        stats = sb("stats", [P, TILES, 6])
        mean_var = sb("mean_var", [P, TILES, 2])
        var_eps = sb("var_eps", [P, TILES])
        rstd = sb("rstd", [P, TILES])
        y_hat = sb("y_hat", [P, TOKENS])
        xn = sb("xn", [P, TOKENS])
        gates = sb("gates", [P, 3, TOKENS])
        prods = sb("prods", [P, 3, TOKENS])
        A = [ph.ps(f"A{i}", [P, TOKENS]) for i in range(4)]
        B = [ph.ps(f"B{i}", [P, TOKENS]) for i in range(4)]

        per_tile = {"qk_projected": 4, "scores_done": 4, "v_projected": 4, "probs_turned": 4, "pv_done": 3, "qk_turned": 4,
                    "out_turned": 2, "wo_done": 1,
                    "squared": 4, "v_copied": 4, "exp_done": 1, "probs_t_ready": 4, "qkt_copied": 4, "out_copied": 2,
                    "masked": 4, "max_ready": 1, "norms_ready": 1, "qk_normed": 4, "cos_ready": 1, "sums_inverted": 1,
                    "att_ready": 3, "y_added": 1,
                    "centred": 1, "norms_guarded": 1, "inv_norms_ready": 1, "sin_ready": 1, "rotated": 1}
        per_seq = {"ffn_turned": 1, "ffn_back": 1, "gate_done": 3, "a_done": 3, "w2_done": 1,
                   "ys_ready": 1, "y1s_ready": 1, "xn_ready": 1, "gelu_done": 3,
                   "stats_ready": 1, "aggregated": 1, "var_ready": 1, "y_hat_ready": 1, "prod_ready": 3, "seq_done": 1,
                   "rstd_ready": 1}
        q = {k: ph.sem(k) for k in (*per_tile, *per_seq)}
        consts_loaded, wqkv_loaded, wo_loaded, ffn_loaded = (ph.sem(k) for k in ("consts_loaded", "wqkv_loaded", "wo_loaded", "ffn_loaded"))
        wait_taken = ph.sem("wait_taken")
        tables_ready, pads_ready = ph.sem("tables_ready"), ph.sem("pads_ready")
        CONST_LOADS, FFN_LOADS = 16 * 4, 16 * 11
        PE_MADE = ("qk_projected", "scores_done", "v_projected", "probs_turned", "pv_done", "qk_turned", "out_turned", "wo_done",
                   "ffn_turned", "ffn_back", "gate_done", "a_done", "w2_done")
        ACT_MADE = ("squared", "v_copied", "exp_done", "probs_t_ready", "qkt_copied", "out_copied", "ys_ready", "y1s_ready",
                    "xn_ready", "gelu_done")
        DVE_MADE = ("masked", "max_ready", "norms_ready", "norms_guarded", "qk_normed", "cos_ready", "sums_inverted", "att_ready", "y_added",
                    "stats_ready", "aggregated", "var_ready", "y_hat_ready", "prod_ready", "seq_done")
        POOL_MADE = ("centred", "inv_norms_ready", "sin_ready", "rotated", "rstd_ready")

        def credit(eng, made):
            for k in made:
                eng.sem_inc(q[k], per_tile[k] * TILES if k in per_tile else per_seq[k])

        def of_tile(n, key, t, k):
            c = per_tile[key]
            return n * (TILES * c) + (t * c + k)

        def of_seq(n, key, k=1):
            return n * per_seq[key] + k

        def place(h):
            return 8 * (h // 8) + HPG * (h % 2) + (h % 8) // 2

        def y_of(s, c0=0, c1=TOKENS, rows=slice(0, P)):
            return g.XH[rows, bass.ds(s - 1, 1), c0:c1].rearrange("p a t -> p (a t)")

        with nc.Block() as block:

            @block.sync
            def _(sp):
                sp.dma_start(base[:], w["rotary"]).then_inc(consts_loaded, 16)
                sp.dma_start(band[:], w["band"]).then_inc(consts_loaded, 16)
                for i, key in enumerate(("q_scale", "k_scale")):
                    sp.dma_start(scales[:, i].rearrange("p l d -> p (l d)"), w[key].rearrange("l d -> (l d)").partition_broadcast(P)).then_inc(consts_loaded, 16)
                with sp.Fori(1, LAYERS + 1) as layer:
                    one = bass.ds(layer - 1, 1)
                    sp.wait_ge(q["v_projected"], layer * (SEQS * TILES * 4) - (SEQS - 1) * TILES * 4)
                    sp.dma_start(wqkv[:], w["Wqkv"][one].rearrange("a d n -> (a d) n")).then_inc(wqkv_loaded, 16)
                    sp.wait_ge(q["wo_done"], layer * (SEQS * TILES) - (SEQS - 1) * TILES)
                    sp.dma_start(wo[:], w["Wo"][one].rearrange("a (c p) d -> p (a c) d", p=P)).then_inc(wo_loaded, 16)
                    sp.wait_ge(q["seq_done"], layer * SEQS - (SEQS - 1))
                    sp.dma_start(w1[:], w["W1"][one].rearrange("a d n -> (a d) n")).then_inc(ffn_loaded, 16)
                    sp.dma_start(w2[:, 0:2], w["W2"][one, 0:2 * P].rearrange("a (c p) d -> p (a c) d", p=P)).then_inc(ffn_loaded, 16)
                    sp.dma_start(w2[0:HIDDEN - 2 * P, 2], w["W2"][one, 2 * P:HIDDEN].rearrange("a p d -> (a p) d")).then_inc(ffn_loaded, 16)
                    for i, key in enumerate(("ln_g", "ln_b", "b2")):
                        sp.dma_start(ln[:, i:i + 1], w[key][one].rearrange("a d -> d a")).then_inc(ffn_loaded, 16)
                    for side in range(2):
                        at = side * HIDDEN
                        sp.dma_start(b1[:, 3 * side:3 * side + 2], w["b1"][one, at:at + 2 * P].rearrange("a (c p) -> p (a c)", p=P),
                                     allow_slow_non_contiguous=True).then_inc(ffn_loaded, 16)
                        sp.dma_start(b1[0:HIDDEN - 2 * P, 3 * side + 2:3 * side + 3], w["b1"][one, at + 2 * P:at + HIDDEN].rearrange("a p -> p a")).then_inc(ffn_loaded, 16)
                    sp.nop().then_inc(ffn_loaded, 16)

            @block.tensor
            def _(pe):
                credit(pe, PE_MADE)
                pe.wait_ge(pads_ready, 2)
                with pe.Fori(1, LAYERS + 1) as layer:
                    pe.wait_ge(wqkv_loaded, layer * 16)
                    pe.wait_ge(wo_loaded, layer * 16)
                    pe.wait_ge(ffn_loaded, layer * FFN_LOADS)
                    pe.sem_inc(wait_taken, 1)
                    with pe.Fori(1, SEQS + 1) as s:
                        n = pe.snap(layer * SEQS + (s - SEQS))

                        def project_qk(t):
                            for i in range(4):
                                nc.tensor.matmul(A[i][:], ys[:, BACK + t * P:BACK + (t + 1) * P], wqkv[:, i * 512:(i + 1) * 512],
                                                 start=True, stop=True).then_inc(q["qk_projected"], 1)

                        def turn_qk(t):
                            pe.wait_ge(q["rotated"], of_tile(n, "rotated", t, 1))
                            for i in range(4):
                                for j in range(4):
                                    last = nc.tensor.transpose(A[i][:, j * P:(j + 1) * P], rot[:, (4 * i + j) * P:(4 * i + j + 1) * P], g.ident[:])
                                last.then_inc(q["qk_turned"], 1)

                        def make_scores(t):
                            pe.wait_ge(q["qkt_copied"], of_tile(n, "qkt_copied", t, 4))
                            pe.sem_inc(wait_taken, 1)
                            for half8 in range(2):
                                if t and half8 == 1:
                                    pe.wait_ge(q["y_added"], of_tile(n, "y_added", t - 1, 1))
                                    pe.sem_inc(wait_taken, 1)
                                for j in range(HPG):
                                    for odd in range(2):
                                        rows, c = slice(HD * odd, HD * odd + HD), 4 * half8 + j
                                        bank = B[S_OF[2 * half8 + odd]]
                                        for b in range(2):
                                            c0 = t * P + b * BLOCK
                                            last = nc.tensor.matmul(bank[b * BLOCK:(b + 1) * BLOCK, j * WIN:(j + 1) * WIN],
                                                                    q_t[rows, c, b * BLOCK:(b + 1) * BLOCK], k_t[rows, c, c0:c0 + WIN],
                                                                    start=True, stop=True)
                                        if j == HPG - 1:
                                            last.then_inc(q["scores_done"], 1)

                        def project_v(t):
                            for i in range(4):
                                b, half = i // 2, i % 2
                                c0 = t * P + b * BLOCK
                                pe.wait_ge(q["masked"], of_tile(n, "masked", t, i + 1))
                                nc.tensor.matmul(B[S_OF[i]][0:WIN, :], ys[:, c0:c0 + WIN], wqkv[:, 2 * INNER + half * 512:2 * INNER + (half + 1) * 512],
                                                 start=True, stop=True).then_inc(q["v_projected"], 1)

                        def turn_probs(t):
                            pe.wait_ge(q["exp_done"], of_tile(n, "exp_done", t, 1))
                            for i in range(GROUPS):
                                if t + 1 < TILES:
                                    pe.wait_ge(q["qk_normed"], of_tile(n, "qk_normed", t + 1, i + 1))
                                for h in range(HPG * i, HPG * (i + 1)):
                                    last = nc.tensor.transpose(A[i][0:WIN, (h % HPG) * P:(h % HPG + 1) * P], probs[:, h, :], g.ident[:])
                                last.then_inc(q["probs_turned"], 1)

                        def weigh_values(t):
                            pe.wait_ge(q["v_copied"], of_tile(n, "v_copied", t, 4))
                            for i, (h0, h1) in enumerate(PV_HEADS):
                                pe.wait_ge(q["probs_t_ready"], of_tile(n, "probs_t_ready", t, 2 if h1 <= 8 else 4))
                                for h in range(h0, h1):
                                    for b in range(2):
                                        last = nc.tensor.matmul(B[i][b * BLOCK:(b + 1) * BLOCK, (h - h0) * (HD + 1):(h - h0 + 1) * (HD + 1)],
                                                                probs_t[:, place(h), b * BLOCK:(b + 1) * BLOCK], vals[:, b, h, :], start=True, stop=True)
                                last.then_inc(q["pv_done"], 1)

                        def turn_out(t):
                            pe.wait_ge(q["att_ready"], of_tile(n, "att_ready", t, 3))
                            for i in range(2):
                                for j in range(4):
                                    c = 4 * i + j
                                    last = nc.tensor.transpose(B[(3, 0)[i]][:, j * P:(j + 1) * P], att[:, c * P:(c + 1) * P], g.ident[:])
                                last.then_inc(q["out_turned"], 1)

                        def project_out(t):
                            pe.wait_ge(q["out_copied"], of_tile(n, "out_copied", t, 2))
                            for c in range(CH):
                                last = nc.tensor.matmul(B[1][:, 0:P], wo[:, c, :], att_t[:, c, :], start=(c == 0), stop=(c == CH - 1))
                            last.then_inc(q["wo_done"], 1)

                        pe.wait_ge(q["ys_ready"], of_seq(n, "ys_ready"))
                        pe.wait_ge(q["seq_done"], n)
                        project_qk(0)
                        turn_qk(0)
                        for t in range(TILES):
                            make_scores(t)
                            if t + 1 < TILES:
                                project_qk(t + 1)
                            project_v(t)
                            turn_probs(t)
                            weigh_values(t)
                            if t + 1 < TILES:
                                turn_qk(t + 1)
                            turn_out(t)
                            project_out(t)

                        pe.wait_ge(q["y1s_ready"], of_seq(n, "y1s_ready"))
                        for t in range(TILES):
                            last = nc.tensor.transpose(A[0][:, t * P:(t + 1) * P], y1s[:, t * P:(t + 1) * P], g.ident[:])
                        last.then_inc(q["ffn_turned"], 1)
                        pe.wait_ge(q["y_hat_ready"], of_seq(n, "y_hat_ready"))
                        for t in range(TILES):
                            last = nc.tensor.transpose(A[1][:, t * P:(t + 1) * P], y_hat[:, t * P:(t + 1) * P], g.ident[:])
                        last.then_inc(q["ffn_back"], 1)
                        pe.wait_ge(q["xn_ready"], of_seq(n, "xn_ready"))
                        for i, (h0, hn) in enumerate(HCH):
                            nc.tensor.matmul(A[(2, 3, 0)[i]][0:hn, :], w1[:, HIDDEN + h0:HIDDEN + h0 + hn], xn[:], start=True, stop=True).then_inc(q["gate_done"], 1)
                            nc.tensor.matmul(B[(2, 3, 0)[i]][0:hn, :], w1[:, h0:h0 + hn], xn[:], start=True, stop=True).then_inc(q["a_done"], 1)
                        for i, (h0, hn) in enumerate(HCH):
                            pe.wait_ge(q["prod_ready"], of_seq(n, "prod_ready", i + 1))
                            last = nc.tensor.matmul(A[1][:], w2[0:hn, i, :], prods[0:hn, i, :], start=(i == 0), stop=(i == 2))
                        last.then_inc(q["w2_done"], 1)

            @block.scalar
            def _(act):
                credit(act, ACT_MADE)
                act.wait_ge(pads_ready, 2)
                with act.Fori(1, LAYERS + 1) as layer:
                    act.wait_ge(ffn_loaded, layer * FFN_LOADS)
                    act.sem_inc(wait_taken, 1)
                    with act.Fori(1, SEQS + 1) as s:
                        n = act.snap(layer * SEQS + (s - SEQS))

                        def square(t):
                            for i in range(4):
                                act.wait_ge(q["qk_projected"], of_tile(n, "qk_projected", t, i + 1))
                                if i == 0:
                                    act.wait_ge(q["rotated"], of_tile(n, "rotated", t - 1, 1))
                                nc.scalar.activation(squares[:, i * 512:(i + 1) * 512], A[i][:], ACT.Square).then_inc(q["squared"], 1)

                        def copy_qk(t):
                            for i in range(4):
                                act.wait_ge(q["qk_turned"], of_tile(n, "qk_turned", t, i + 1))
                                src = A[i][:].rearrange("p (c t) -> p c t", t=P)
                                dst = q_t[:, 4 * i:4 * i + 4, :] if i < 2 else k_t[:, 4 * i - 8:4 * i - 4, BACK + t * P:BACK + (t + 1) * P]
                                nc.scalar.copy(dst, src).then_inc(q["qkt_copied"], 1)

                        def copy_v(t):
                            for i in range(4):
                                act.wait_ge(q["v_projected"], of_tile(n, "v_projected", t, i + 1))
                                nc.scalar.copy(vals[:, i // 2, 8 * (i % 2):8 * (i % 2) + 8, 0:HD],
                                               B[S_OF[i]][0:WIN, :].rearrange("p (h d) -> p h d", d=HD)).then_inc(q["v_copied"], 1)

                        act.wait_ge(q["seq_done"], n)
                        nc.scalar.copy(ys[0:HD, BACK:], y_of(s, rows=slice(0, HD)))
                        nc.scalar.copy(ys[HD:P, BACK + 1:], y_of(s, 0, TOKENS - 1, rows=slice(HD, P))).then_inc(q["ys_ready"], 1)
                        square(0)
                        copy_qk(0)
                        for t in range(TILES):
                            if t + 1 < TILES:
                                square(t + 1)
                            copy_v(t)
                            act.wait_ge(q["centred"], of_tile(n, "centred", t, 1))
                            nc.scalar.activation(probs[:], scores[:], ACT.Exp).then_inc(q["exp_done"], 1)
                            for i in range(GROUPS):
                                act.wait_ge(q["probs_turned"], of_tile(n, "probs_turned", t, i + 1))
                                nc.scalar.copy(probs_t[:, HPG * i:HPG * (i + 1), :], A[i][0:WIN, :].rearrange("p (h t) -> p h t", t=P)).then_inc(q["probs_t_ready"], 1)
                            if t + 1 < TILES:
                                copy_qk(t + 1)
                            for i in range(2):
                                act.wait_ge(q["out_turned"], of_tile(n, "out_turned", t, i + 1))
                                nc.scalar.copy(att_t[:, 4 * i:4 * i + 4, :], B[(3, 0)[i]][:].rearrange("p (c t) -> p c t", t=P)).then_inc(q["out_copied"], 1)

                        act.wait_ge(q["y_added"], of_tile(n, "y_added", TILES - 1, 1))
                        nc.scalar.copy(y1s[0:HD, :], y1[0:HD, :])
                        nc.scalar.copy(y1s[HD:P, 1:], y1[HD:P, 0:TOKENS - 1]).then_inc(q["y1s_ready"], 1)
                        act.wait_ge(q["ffn_back"], of_seq(n, "ffn_back"))
                        nc.scalar.activation(xn[:], A[1][:], ACT.Identity, bias=ln[:, 1:2], scale=ln[:, 0:1]).then_inc(q["xn_ready"], 1)
                        for i, (h0, hn) in enumerate(HCH):
                            act.wait_ge(q["gate_done"], of_seq(n, "gate_done", i + 1))
                            nc.scalar.activation(gates[0:hn, i, :], A[(2, 3, 0)[i]][0:hn, :], ACT.Gelu, bias=b1[0:hn, 3 + i:4 + i]).then_inc(q["gelu_done"], 1)

            @block.gpsimd
            def _(pool):
                nc.gpsimd.memset(k_t[:, :, 0:BACK], 0.0)
                nc.gpsimd.memset(vals[:, :, :, HD:HD + 1], 1.0).then_inc(pads_ready, 1)
                credit(pool, POOL_MADE)
                with pool.Fori(1, LAYERS + 1) as layer:
                    pool.wait_ge(tables_ready, layer)
                    pool.sem_inc(wait_taken, 1)
                    with pool.Fori(1, SEQS + 1) as s:
                        n = pool.snap(layer * SEQS + (s - SEQS))

                        def heads(buf):
                            return buf[:].rearrange("p (a h d) -> p a h d", a=2, d=HD)

                        def rotate(t):
                            pool.wait_ge(q["norms_guarded"], of_tile(n, "norms_guarded", t, 1))
                            nc.gpsimd.tensor_tensor(inv_norm[:], norm2c[:], g.minus_half[:, 0:2 * HEADS], ALU.pow).then_inc(q["inv_norms_ready"], 1)
                            pool.wait_ge(q["qk_normed"], of_tile(n, "qk_normed", t, 4))
                            for half in range(2):
                                to, of = slice(32 * half, 32 * half + 32), slice(32 - 32 * half, 64 - 32 * half)
                                last = nc.gpsimd.tensor_tensor(heads(squares)[:, :, :, to], heads(normed)[:, :, :, of],
                                                               table[:, t, 1::2, to].unsqueeze(2).to_broadcast([P, 2, HEADS, 32]), ALU.mult)
                            last.then_inc(q["sin_ready"], 1)
                            pool.wait_ge(q["sin_ready"], of_tile(n, "sin_ready", t, 1))
                            pool.wait_ge(q["cos_ready"], of_tile(n, "cos_ready", t, 1))
                            nc.gpsimd.tensor_tensor(rot[:], rot[:], squares[:], ALU.add).then_inc(q["rotated"], 1)

                        rotate(0)
                        for t in range(TILES):
                            pool.wait_ge(q["max_ready"], of_tile(n, "max_ready", t, 1))
                            nc.gpsimd.tensor_tensor(scores[:], scores[:], top[:].unsqueeze(2).to_broadcast([P, HEADS, WIN]), ALU.subtract).then_inc(q["centred"], 1)
                            if t + 1 < TILES:
                                rotate(t + 1)
                        pool.wait_ge(q["var_ready"], of_seq(n, "var_ready"))
                        nc.gpsimd.tensor_tensor(rstd[:], var_eps[:], g.minus_half[:, 0:TILES], ALU.pow).then_inc(q["rstd_ready"], 1)

            @block.vector
            def _(dve):
                nc.vector.memset(ys[:], 0.0)
                nc.vector.memset(y1s[:], 0.0).then_inc(pads_ready, 1)
                credit(dve, DVE_MADE)
                dve.wait_ge(consts_loaded, CONST_LOADS)
                with dve.Fori(1, LAYERS + 1) as layer:
                    dve.wait_ge(q["rotated"], layer * (SEQS * TILES) - (SEQS - 1) * TILES)
                    for a in range(2):
                        def scale_of(cols, width):
                            return scales[:, a, bass.ds(layer - 1, 1), cols].to_broadcast([P, TILES, width])
                        nc.vector.tensor_tensor(table[:, :, 2 * a, :], base[:, :, 2 * a, :], scale_of(slice(0, 64), 64), ALU.mult)
                        nc.vector.tensor_tensor(table[:, :, 2 * a + 1, 0:32], base[:, :, 2 * a + 1, 0:32], scale_of(slice(32, 64), 32), ALU.mult)
                        last = nc.vector.tensor_tensor(table[:, :, 2 * a + 1, 32:64], base[:, :, 2 * a + 1, 32:64], scale_of(slice(0, 32), 32), ALU.mult)
                    last.then_inc(tables_ready, 1)
                    dve.wait_ge(tables_ready, layer)
                    dve.wait_ge(ffn_loaded, layer * FFN_LOADS)
                    dve.sem_inc(wait_taken, 1)
                    with dve.Fori(1, SEQS + 1) as s:
                        n = dve.snap(layer * SEQS + (s - SEQS))

                        def normalise_qk(t):
                            for i in range(4):
                                dve.wait_ge(q["squared"], of_tile(n, "squared", t, i + 1))
                                last = nc.vector.tensor_reduce(norm2[:, 8 * i:8 * i + 8], squares[:, i * 512:(i + 1) * 512].rearrange("p (h d) -> p h d", d=HD), AX, ALU.add)
                            last.then_inc(q["norms_ready"], 1)
                            dve.wait_ge(q["norms_ready"], of_tile(n, "norms_ready", t, 1))
                            nc.vector.tensor_scalar(norm2c[:], norm2[:], 1e-24, None, ALU.max).then_inc(q["norms_guarded"], 1)
                            dve.wait_ge(q["inv_norms_ready"], of_tile(n, "inv_norms_ready", t, 1))
                            for i in range(4):
                                nc.vector.tensor_tensor(normed[:, i * 512:(i + 1) * 512].rearrange("p (h d) -> p h d", d=HD), A[i][:].rearrange("p (h d) -> p h d", d=HD),
                                                        inv_norm[:, 8 * i:8 * i + 8].unsqueeze(2).to_broadcast([P, 8, HD]), ALU.mult).then_inc(q["qk_normed"], 1)
                            dve.wait_ge(q["qk_normed"], of_tile(n, "qk_normed", t, 4))
                            dve.wait_ge(q["qk_turned"], of_tile(n, "qk_turned", t - 1, 4))
                            nc.vector.tensor_tensor(rot[:].rearrange("p (a h d) -> p a h d", a=2, d=HD), normed[:].rearrange("p (a h d) -> p a h d", a=2, d=HD),
                                                    table[:, t, 0::2, :].unsqueeze(2).to_broadcast([P, 2, HEADS, HD]), ALU.mult).then_inc(q["cos_ready"], 1)

                        normalise_qk(0)
                        for t in range(TILES):
                            for i in range(GROUPS):
                                dve.wait_ge(q["scores_done"], of_tile(n, "scores_done", t, i + 1))
                                if i == 0:
                                    dve.wait_ge(q["exp_done"], of_tile(n, "exp_done", t - 1, 1))
                                src = B[S_OF[i]][:, 0:HPG * WIN].rearrange("p (h k) -> p h k", k=WIN)
                                dst = scores[:, HPG * i:HPG * (i + 1), :]
                                if t == 0:
                                    last = nc.vector.tensor_tensor(dst, src, band[:, 0, :].unsqueeze(1).to_broadcast([P, HPG, WIN]), ALU.add)
                                else:
                                    last = nc.vector.tensor_tensor(dst, src, band[:, 1, :].unsqueeze(1).to_broadcast([P, HPG, WIN]), ALU.add)
                                last.then_inc(q["masked"], 1)
                            dve.wait_ge(q["masked"], of_tile(n, "masked", t, 4))
                            nc.vector.tensor_reduce(top[:], scores[:], AX, ALU.max).then_inc(q["max_ready"], 1)
                            if t + 1 < TILES:
                                normalise_qk(t + 1)
                            for i, (h0, h1) in enumerate(PV_HEADS):
                                dve.wait_ge(q["pv_done"], of_tile(n, "pv_done", t, i + 1))
                                src = B[i][:, 0:(h1 - h0) * (HD + 1)].rearrange("p (h d) -> p h d", d=HD + 1)
                                last = nc.vector.reciprocal(inv_sum[:, h0:h1].unsqueeze(2), src[:, :, HD:HD + 1])
                            last.then_inc(q["sums_inverted"], 1)
                            dve.wait_ge(q["sums_inverted"], of_tile(n, "sums_inverted", t, 1))
                            dve.wait_ge(q["out_turned"], of_tile(n, "out_turned", t - 1, 2))
                            for i, (h0, h1) in enumerate(PV_HEADS):
                                src = B[i][:, 0:(h1 - h0) * (HD + 1)].rearrange("p (h d) -> p h d", d=HD + 1)
                                nc.vector.tensor_tensor(att[:, h0 * HD:h1 * HD].rearrange("p (h d) -> p h d", d=HD), src[:, :, 0:HD],
                                                        inv_sum[:, h0:h1].unsqueeze(2).to_broadcast([P, h1 - h0, HD]), ALU.mult).then_inc(q["att_ready"], 1)
                            dve.wait_ge(q["wo_done"], of_tile(n, "wo_done", t, 1))
                            nc.vector.tensor_tensor(y1[:, t * P:(t + 1) * P], B[1][:, 0:P], y_of(s, t * P, (t + 1) * P), ALU.add).then_inc(q["y_added"], 1)

                        dve.wait_ge(q["ffn_turned"], of_seq(n, "ffn_turned"))
                        for t in range(TILES):
                            last = nc.vector.bn_stats(stats[:, t, :], A[0][:, t * P:(t + 1) * P])
                        last.then_inc(q["stats_ready"], 1)
                        dve.wait_ge(q["stats_ready"], of_seq(n, "stats_ready"))
                        dve.sem_inc(wait_taken, 1)
                        for t in range(TILES):
                            last = nc.vector.bn_aggr(mean_var[:, t, :], stats[:, t, :])
                        last.then_inc(q["aggregated"], 1)
                        dve.wait_ge(q["aggregated"], of_seq(n, "aggregated"))
                        nc.vector.tensor_scalar(var_eps[:], mean_var[:, :, 1], LN_EPS, None, ALU.add).then_inc(q["var_ready"], 1)
                        dve.wait_ge(q["rstd_ready"], of_seq(n, "rstd_ready"))
                        for t in range(TILES):
                            last = nc.vector.tensor_scalar(y_hat[:, t * P:(t + 1) * P], A[0][:, t * P:(t + 1) * P], mean_var[:, t, 0:1], rstd[:, t:t + 1],
                                                           ALU.subtract, ALU.mult)
                        last.then_inc(q["y_hat_ready"], 1)
                        for i, (h0, hn) in enumerate(HCH):
                            dve.wait_ge(q["gelu_done"], of_seq(n, "gelu_done", i + 1))
                            dve.wait_ge(q["a_done"], of_seq(n, "a_done", i + 1))
                            nc.vector.scalar_tensor_tensor(prods[0:hn, i, :], B[(2, 3, 0)[i]][0:hn, :], b1[0:hn, i:i + 1], gates[0:hn, i, :],
                                                           ALU.add, ALU.mult).then_inc(q["prod_ready"], 1)
                        dve.wait_ge(q["w2_done"], of_seq(n, "w2_done"))
                        nc.vector.scalar_tensor_tensor(y_of(s), A[1][:], ln[:, 2:3], y1[:], ALU.add, ALU.add).then_inc(q["seq_done"], 1)

    run_phase(nc, name, body)


def add_back_phase(nc, g, name):

    def body(ph):
        xs = ph.sb("xs", [P, 2, TOKENS])
        turned = [ph.ps(f"turned{i}", [P, TOKENS]) for i in range(2)]
        xs_ready, done, added = ph.sem("xs_ready"), ph.sem("turned_ready"), ph.sem("added")
        PAIRS = SEQS // 2

        with nc.Block() as block:

            @block.scalar
            def _(act):
                with act.Fori(1, PAIRS + 1) as pair:
                    for i in range(2):
                        act.wait_ge(done, (pair - 1) * 2 + (i + 1))
                        nc.scalar.copy(xs[:, i], g.XH[:, bass.ds(pair * 2 + (i - 2), 1), :].rearrange("p a t -> p (a t)")).then_inc(xs_ready, 1)

            @block.tensor
            def _(pe):
                pe.sem_inc(done, 2)
                with pe.Fori(1, PAIRS + 1) as pair:
                    for i in range(2):
                        pe.wait_ge(xs_ready, (pair - 1) * 2 + (i + 1))
                        pe.wait_ge(added, (pair - 1) * 2 + (i + 1))
                        for t in range(TILES):
                            last = nc.tensor.transpose(turned[i][:, t * P:(t + 1) * P], xs[:, i, t * P:(t + 1) * P], g.ident[:])
                        last.then_inc(done, 1)

            @block.vector
            def _(dve):
                dve.sem_inc(added, 2)
                with dve.Fori(1, PAIRS + 1) as pair:
                    for i in range(2):
                        dve.wait_ge(done, pair * 2 + (i + 1))
                        xt = g.X[:, bass.ds(pair * 2 + (i - 2), 1), :].rearrange("p a t -> p (a t)")
                        nc.vector.tensor_tensor(xt, xt, turned[i][:], ALU.add).then_inc(added, 1)

    run_phase(nc, name, body)


def delta_rule_phase(nc, g, name, w):
    PAIRS, CHUNK, LEVELS = SEQS // 2, 64, 6
    CHUNKS = TOKENS // CHUNK

    def body(ph):
        wwrite = ph.sb("wwrite", [P, P])
        wwrite_t = ph.sb("wwrite_t", [P, P])
        wout = ph.sb("wout", [P, P])
        wout_t = ph.sb("wout_t", [P, P])
        wgates = ph.sb("wgates", [P, 3])
        dt_bias = ph.sb("dt_bias", [P, 1])
        a_log = ph.sb("a_log", [P, 1])
        rate = ph.sb("rate", [P, 1])
        until = ph.sb("until", [P, P])
        within = ph.sb("within", [P, P])
        ends = ph.sb("ends", [P, 2])
        ceiling = ph.sb("ceiling", [P, P])
        corner = ph.sb("corner", [P, LEVELS, P])
        big = {n: ph.sb(n, [P, 2, TOKENS]) for n in (
            "xs", "xt", "rk", "wk", "wkb", "vb", "rkd", "wkbd", "wkdw", "wkb_t", "rkd_t", "decayed", "m_t", "attn_t",
            "t1", "inv", "inv_t", "vp", "wkcd_t", "v_new", "o_t", "y")}
        off_t = ph.sb("off_t", [P, 2, LEVELS, TOKENS])
        keys_t = ph.sb("keys_t", [P, 2, TOKENS + 1])
        state = ph.sb("state", [P, 2, P])
        sm = {n: ph.sb(n, [P, 2, TILES]) for n in ("norm2", "norm2c", "inv_norm", "u", "abs_u", "e_u", "ln_u", "sp", "decay", "dec", "to_end", "e_dec", "e_to_end")}
        e_gates = ph.sb("e_gates", [P, 2, TILES, 2])
        e_gates1 = ph.sb("e_gates1", [P, 2, TILES, 2])
        gates = ph.sb("gates", [P, 2, TILES, 2])
        carry = ph.sb("carry", [P, 2, CHUNKS])
        bank = [[ph.ps(f"bank{i}{k}", [P, TOKENS]) for k in range(4)] for i in range(2)]

        pe_made = ["x_turned", "z_done", "v_done", "rk_turned", "decs_done", "dec_rows_done", "wk_turned", "wkb_turned", "rkd_turned",
                   "gram_done", "attn_done", "t1_done", "u_done", "ut_done", "vp_done", "wkcd_done", "vs_done", "update_done", "o_done", "out_done"]
        act_made = ["xs_ready", "xt_ready", "e_gates_ready", "abs_ready", "e_u_ready", "ln_ready", "rk_t_ready", "dec_ready", "e_dec_ready", "carry_ready",
                    "e_to_end_ready", "decayed_ready", "wk_ready", "wkb_t_ready", "rkd_t_ready", "t1_ready", "vp_ready", "wkcd_ready", "o_ready"]
        dve_made = ["squares_ready", "norm2_ready", "norm2c_ready", "rk_ready", "e_gates1_ready", "gates_ready", "u_ready", "sp_ready", "sp_sum_ready", "decay_ready",
                    "to_end_ready", "floor_ready", "wkb_ready", "vb_ready", "m_ready", "attn_ready", "inv_ready", "inv_t_ready",
                    "v_new_ready", "state_ready", "y_ready", "x_added"]
        pool_made = ["inv_norm_ready", "rkd_ready", "wkbd_ready", "wkdw_ready", "off_ready"]
        count = {k: 1 for k in pe_made + act_made + dve_made + pool_made}
        count.update(t1_done=LEVELS, t1_ready=LEVELS - 1, u_done=LEVELS - 2, ut_done=LEVELS - 1, inv_ready=LEVELS, inv_t_ready=LEVELS, off_ready=LEVELS,
                     vs_done=CHUNKS, update_done=CHUNKS, v_new_ready=CHUNKS, state_ready=CHUNKS + 1)
        q = {k: [ph.sem(f"{k}{i}") for i in range(2)] for k in ("t1_done", "t1_ready", "u_done", "ut_done", "inv_ready", "inv_t_ready", "off_ready",
                                                                 "vs_done", "update_done", "v_new_ready", "state_ready")}
        q.update({k: ph.sem(k) for k in count if k not in q})
        loaded, weights_turned, weights_ready, rate_ready, pads_ready, wait_taken = (
            ph.sem(k) for k in ("loaded", "weights_turned", "weights_ready", "rate_ready", "pads_ready", "wait_taken"))
        LOADS = 16 * 12

        def credit(eng, made):
            for k in made:
                if isinstance(q[k], list):
                    for one in q[k]:
                        eng.sem_inc(one, count[k])
                else:
                    eng.sem_inc(q[k], 2)

        def wait(eng, pair, key, i, k=1):
            if isinstance(q[key], list):
                eng.wait_ge(q[key][i], pair * count[key] + k)
            else:
                eng.wait_ge(q[key], pair * 2 + (i + 1))

        def done(ins, key, i):
            ins.then_inc(q[key][i] if isinstance(q[key], list) else q[key], 1)

        def tiled(buf, i):
            return buf[:, i].rearrange("p (t d) -> p t d", d=P)

        def banked(i, k):
            return bank[i][k][:].rearrange("p (t d) -> p t d", d=P)

        def spread(col):
            return col.unsqueeze(2).to_broadcast([P, TILES, P])

        def every(table):
            return table.unsqueeze(1).to_broadcast([P, TILES, P])

        def seq_of(buf, pair, i, c0=0, c1=TOKENS):
            return buf[:, bass.ds(pair * 2 + (i - 2), 1), c0:c1].rearrange("p a t -> p (a t)")

        cols = [slice(t * P, (t + 1) * P) for t in range(TILES)]

        with nc.Block() as block:

            @block.sync
            def _(sp):
                for dst, src in ((wwrite[:], w["W_write"]), (wout[:], w["W_out"]), (wgates[:, 0:1], w["W_gate"].rearrange("a d -> d a")),
                                 (wgates[:, 1:2], w["W_beta"].rearrange("a d -> d a")), (wgates[:, 2:3], w["W_alpha"].rearrange("a d -> d a")),
                                 (dt_bias[:], w["dt_bias"].partition_broadcast(P)), (a_log[:], w["A_log"].partition_broadcast(P)),
                                 (until[:], w["until"]), (within[:], w["within"]), (ends[:], w["ends"]), (ceiling[:], w["ceiling"]),
                                 (corner[:], w["corner"])):
                    sp.dma_start(dst, src).then_inc(loaded, 16)

            @block.tensor
            def _(pe):
                credit(pe, pe_made)
                pe.wait_ge(loaded, LOADS)
                nc.tensor.transpose(bank[0][0][:, 0:P], wwrite[:], g.ident[:])
                nc.tensor.transpose(bank[0][0][:, P:2 * P], wout[:], g.ident[:]).then_inc(weights_turned, 1)
                pe.wait_ge(weights_ready, 1)
                pe.wait_ge(pads_ready, 1)
                with pe.Fori(1, PAIRS + 1) as pair:

                    def products(i, k, lhs, rhs, key):
                        for t in range(TILES):
                            last = nc.tensor.matmul(bank[i][k][:, cols[t]], lhs(t), rhs(t), start=True, stop=True)
                        done(last, key, i)

                    def turns(i, k, src, key):
                        for t in range(TILES):
                            last = nc.tensor.transpose(bank[i][k][:, cols[t]], src(t), g.ident[:])
                        done(last, key, i)

                    for i in range(2):
                        wait(pe, pair, "xs_ready", i)
                        wait(pe, pair - 1, "x_added", i)
                        turns(i, 0, lambda t: big["xs"][:, i, cols[t]], "x_turned")
                        for t in range(TILES):
                            last = nc.tensor.matmul(bank[i][1][:, 3 * t:3 * t + 3], big["xs"][:, i, cols[t]], wgates[:], start=True, stop=True)
                        done(last, "z_done", i)
                        products(i, 2, lambda t: big["xs"][:, i, cols[t]], lambda t: wwrite_t[:], "v_done")
                    for i in range(2):
                        wait(pe, pair, "rk_ready", i)
                        turns(i, 3, lambda t: big["rk"][:, i, cols[t]], "rk_turned")
                    for i in range(2):
                        wait(pe, pair, "decay_ready", i)
                        nc.tensor.matmul(bank[i][1][:, 16:20], until[:], sm["decay"][:, i], start=True, stop=True)
                        nc.tensor.matmul(bank[i][1][:, 20:24], within[:], sm["decay"][:, i], start=True, stop=True)
                        for t in range(TILES):
                            last = nc.tensor.matmul(bank[i][1][:, 24 + 2 * t:26 + 2 * t], sm["decay"][:, i, t:t + 1].to_broadcast([P, P]), ends[:],
                                                    start=True, stop=True)
                        done(last, "decs_done", i)
                        wait(pe, pair, "xt_ready", i)
                        products(i, 0, lambda t: sm["decay"][:, i, t:t + 1].to_broadcast([P, P]), lambda t: until[:], "dec_rows_done")
                    for i in range(2):
                        wait(pe, pair, "rk_t_ready", i)
                        turns(i, 3, lambda t: keys_t[:, i, t * P:(t + 1) * P], "wk_turned")
                    for i in range(2):
                        wait(pe, pair, "rkd_ready", i)
                        wait(pe, pair, "vb_ready", i)
                        turns(i, 2, lambda t: big["rkd"][:, i, cols[t]], "rkd_turned")
                        wait(pe, pair, "wkb_ready", i)
                        wait(pe, pair, "e_to_end_ready", i)
                        wait(pe, pair, "carry_ready", i)
                        turns(i, 1, lambda t: big["wkb"][:, i, cols[t]], "wkb_turned")
                    for i in range(2):
                        wait(pe, pair, "floor_ready", i)
                        products(i, 0, lambda t: keys_t[:, i, t * P:(t + 1) * P], lambda t: keys_t[:, i, t * P + 1:(t + 1) * P + 1], "attn_done")
                        wait(pe, pair, "wkb_t_ready", i)
                        products(i, 3, lambda t: keys_t[:, i, t * P:(t + 1) * P], lambda t: big["wkb_t"][:, i, cols[t]], "gram_done")
                    for level in range(LEVELS):
                        for i in range(2):
                            wait(pe, pair, "off_ready", i, level + 1)
                            if level == 0:
                                wait(pe, pair, "attn_ready", i)
                                wait(pe, pair, "m_ready", i)
                                products(i, 0, lambda t: off_t[:, i, 0, cols[t]], lambda t: g.ident[:], "t1_done")
                                continue
                            wait(pe, pair, "inv_ready", i, level)
                            products(i, 0, lambda t: off_t[:, i, level, cols[t]], lambda t: big["inv"][:, i, cols[t]], "t1_done")
                        if level == 0:
                            continue
                        for i in range(2):
                            wait(pe, pair, "t1_ready", i, level)
                            wait(pe, pair, "inv_t_ready", i, level)
                            if level < LEVELS - 1:
                                products(i, 1, lambda t: big["inv_t"][:, i, cols[t]], lambda t: big["t1"][:, i, cols[t]], "u_done")
                            if level == 1:
                                wait(pe, pair, "rkd_t_ready", i)
                            products(i, 2, lambda t: big["t1"][:, i, cols[t]], lambda t: big["inv_t"][:, i, cols[t]], "ut_done")
                    for i in range(2):
                        wait(pe, pair, "inv_t_ready", i, LEVELS)
                        products(i, 0, lambda t: big["inv_t"][:, i, cols[t]], lambda t: big["vb"][:, i, cols[t]], "vp_done")
                        wait(pe, pair, "wkbd_ready", i)
                        products(i, 1, lambda t: big["wkbd"][:, i, cols[t]], lambda t: big["inv_t"][:, i, cols[t]], "wkcd_done")
                    for c in range(CHUNKS):
                        t, rows, own = c // 2, slice(CHUNK * (c % 2), CHUNK * (c % 2) + CHUNK), slice(c * CHUNK, (c + 1) * CHUNK)
                        for i in range(2):
                            if c == 0:
                                wait(pe, pair, "wkcd_ready", i)
                                wait(pe, pair, "vp_ready", i)
                            wait(pe, pair, "state_ready", i, c + 1)
                            done(nc.tensor.matmul(bank[i][2][rows, 0:P], big["wkcd_t"][:, i, own], state[:, i], start=True, stop=True), "vs_done", i)
                            nc.tensor.matmul(bank[i][3][:, own], state[:, i], big["rkd_t"][:, i, own], start=True, stop=False)
                        for i in range(2):
                            wait(pe, pair, "v_new_ready", i, c + 1)
                            if c == 0:
                                wait(pe, pair, "wkdw_ready", i)
                            last = nc.tensor.matmul(bank[i][3][:, own], big["v_new"][rows, i, cols[t]], big["attn_t"][rows, i, own], start=False, stop=True)
                            if c == CHUNKS - 1:
                                done(last, "o_done", i)
                            done(nc.tensor.matmul(bank[i][0][:, 0:P], big["wkdw"][rows, i, cols[t]], big["v_new"][rows, i, cols[t]], start=True, stop=True), "update_done", i)
                    for i in range(2):
                        wait(pe, pair, "o_ready", i)
                        products(i, 1, lambda t: big["o_t"][:, i, cols[t]], lambda t: wout_t[:], "out_done")

            @block.scalar
            def _(act):
                credit(act, act_made)
                act.wait_ge(loaded, LOADS)
                nc.scalar.activation(rate[:], a_log[:], ACT.Exp).then_inc(rate_ready, 1)
                act.wait_ge(weights_turned, 1)
                nc.scalar.copy(wwrite_t[:], bank[0][0][:, 0:P])
                nc.scalar.copy(wout_t[:], bank[0][0][:, P:2 * P]).then_inc(weights_ready, 1)
                with act.Fori(1, PAIRS + 1) as pair:

                    def copy(i, k, dst, key, done_key):
                        wait(act, pair, done_key, i)
                        done(nc.scalar.copy(dst, bank[i][k][:]), key, i)

                    for i in range(2):
                        wait(act, pair - 1, "out_done", i)
                        done(nc.scalar.copy(big["xs"][:, i], seq_of(g.XH, pair, i)), "xs_ready", i)
                    for i in range(2):
                        wait(act, pair - 1, "x_added", i)
                        copy(i, 0, big["xt"][:, i], "xt_ready", "x_turned")
                        z = bank[i][1][:, 0:12].rearrange("p (t k) -> p t k", k=3)
                        wait(act, pair, "z_done", i)
                        done(nc.scalar.activation(e_gates[:, i], z[:, :, 0:2], ACT.Exp, scale=-1.0), "e_gates_ready", i)
                    for i in range(2):
                        wait(act, pair, "u_ready", i)
                        done(nc.scalar.activation(sm["abs_u"][:, i], sm["u"][:, i], ACT.Abs), "abs_ready", i)
                        wait(act, pair, "abs_ready", i)
                        done(nc.scalar.activation(sm["e_u"][:, i], sm["abs_u"][:, i], ACT.Exp, scale=-1.0), "e_u_ready", i)
                        wait(act, pair, "e_u_ready", i)
                        done(nc.scalar.activation(sm["ln_u"][:, i], sm["e_u"][:, i], ACT.Ln, bias=1.0), "ln_ready", i)
                    for i in range(2):
                        copy(i, 3, keys_t[:, i, 1:TOKENS + 1], "rk_t_ready", "rk_turned")
                    for i in range(2):
                        wait(act, pair, "decs_done", i)
                        done(nc.scalar.copy(sm["dec"][:, i], bank[i][1][:, 16:20]), "dec_ready", i)
                        done(nc.scalar.activation(sm["e_dec"][:, i], bank[i][1][:, 16:20], ACT.Exp), "e_dec_ready", i)
                        done(nc.scalar.activation(carry[:, i], bank[i][1][:, 24:32], ACT.Exp), "carry_ready", i)
                        wait(act, pair, "to_end_ready", i)
                        done(nc.scalar.activation(sm["e_to_end"][:, i], sm["to_end"][:, i], ACT.Exp), "e_to_end_ready", i)
                    for i in range(2):
                        wait(act, pair, "floor_ready", i)
                        done(nc.scalar.activation(big["decayed"][:, i], big["decayed"][:, i], ACT.Exp), "decayed_ready", i)
                        copy(i, 3, big["wk"][:, i], "wk_ready", "wk_turned")
                    for i in range(2):
                        copy(i, 2, big["rkd_t"][:, i], "rkd_t_ready", "rkd_turned")
                        copy(i, 1, big["wkb_t"][:, i], "wkb_t_ready", "wkb_turned")
                    for level in range(1, LEVELS):
                        for i in range(2):
                            wait(act, pair, "t1_done", i, level + 1)
                            done(nc.scalar.copy(big["t1"][:, i], bank[i][0][:]), "t1_ready", i)
                    for i in range(2):
                        copy(i, 0, big["vp"][:, i], "vp_ready", "vp_done")
                        copy(i, 1, big["wkcd_t"][:, i], "wkcd_ready", "wkcd_done")
                    for i in range(2):
                        copy(i, 3, big["o_t"][:, i], "o_ready", "o_done")

            @block.gpsimd
            def _(pool):
                credit(pool, pool_made)
                pool.wait_ge(loaded, LOADS)
                with pool.Fori(1, PAIRS + 1) as pair:
                    for i in range(2):
                        wait(pool, pair, "norm2c_ready", i)
                        done(nc.gpsimd.tensor_tensor(sm["inv_norm"][:, i], sm["norm2c"][:, i], g.minus_half[:, 0:TILES], ALU.pow), "inv_norm_ready", i)
                    for i in range(2):
                        wait(pool, pair, "rk_ready", i)
                        wait(pool, pair, "e_dec_ready", i)
                        done(nc.gpsimd.tensor_tensor(tiled(big["rkd"], i), tiled(big["rk"], i), spread(sm["e_dec"][:, i]), ALU.mult), "rkd_ready", i)
                    for level in range(LEVELS):
                        for i in range(2):
                            wait(pool, pair, "m_ready", i)
                            done(nc.gpsimd.tensor_tensor(off_t[:, i, level].rearrange("p (t d) -> p t d", d=P), tiled(big["m_t"], i), every(corner[:, level]), ALU.mult), "off_ready", i)
                    for i in range(2):
                        wait(pool, pair, "wkb_ready", i)
                        done(nc.gpsimd.tensor_tensor(tiled(big["wkbd"], i), tiled(big["wkb"], i), spread(sm["e_dec"][:, i]), ALU.mult), "wkbd_ready", i)
                        wait(pool, pair, "wk_ready", i)
                        wait(pool, pair, "e_to_end_ready", i)
                        done(nc.gpsimd.tensor_tensor(tiled(big["wkdw"], i), tiled(big["wk"], i), spread(sm["e_to_end"][:, i]), ALU.mult), "wkdw_ready", i)

            @block.vector
            def _(dve):
                nc.vector.memset(keys_t[:], 0.0).then_inc(pads_ready, 1)
                credit(dve, dve_made)
                dve.wait_ge(loaded, LOADS)
                dve.wait_ge(rate_ready, 1)
                with dve.Fori(1, PAIRS + 1) as pair:
                    for i in range(2):
                        wait(dve, pair, "xt_ready", i)
                        done(nc.vector.tensor_tensor(big["y"][:, i], big["xt"][:, i], big["xt"][:, i], ALU.mult), "squares_ready", i)
                        wait(dve, pair, "squares_ready", i)
                        done(nc.vector.tensor_reduce(sm["norm2"][:, i], tiled(big["y"], i), AX, ALU.add), "norm2_ready", i)
                        wait(dve, pair, "norm2_ready", i)
                        done(nc.vector.tensor_scalar(sm["norm2c"][:, i], sm["norm2"][:, i], 1e-24, None, ALU.max), "norm2c_ready", i)
                    for i in range(2):
                        z = bank[i][1][:, 0:12].rearrange("p (t k) -> p t k", k=3)
                        wait(dve, pair, "z_done", i)
                        wait(dve, pair, "e_gates_ready", i)
                        done(nc.vector.tensor_scalar(sm["u"][:, i], z[:, :, 2], dt_bias[:], None, ALU.add), "u_ready", i)
                        done(nc.vector.tensor_scalar(e_gates1[:, i], e_gates[:, i], 1.0, None, ALU.add), "e_gates1_ready", i)
                        wait(dve, pair, "e_gates1_ready", i)
                        done(nc.vector.reciprocal(gates[:, i], e_gates1[:, i]), "gates_ready", i)
                    for i in range(2):
                        wait(dve, pair, "inv_norm_ready", i)
                        done(nc.vector.tensor_tensor(tiled(big["rk"], i), tiled(big["xt"], i), spread(sm["inv_norm"][:, i]), ALU.mult), "rk_ready", i)
                    for i in range(2):
                        wait(dve, pair, "ln_ready", i)
                        done(nc.vector.scalar_tensor_tensor(sm["sp"][:, i], sm["u"][:, i], 0.0, sm["ln_u"][:, i], ALU.max, ALU.add), "sp_ready", i)
                        wait(dve, pair, "sp_ready", i)
                        done(nc.vector.tensor_scalar(sm["decay"][:, i], sm["sp"][:, i], rate[:], -1.0, ALU.mult, ALU.mult), "decay_ready", i)
                    for i in range(2):
                        wait(dve, pair, "v_done", i)
                        wait(dve, pair, "gates_ready", i)
                        done(nc.vector.tensor_tensor(tiled(big["vb"], i), banked(i, 2), spread(gates[:, i, :, 1]), ALU.mult), "vb_ready", i)
                    for i in range(2):
                        wait(dve, pair, "carry_ready", i)
                        done(nc.vector.tensor_tensor(sm["to_end"][:, i], bank[i][1][:, 20:24], sm["dec"][:, i], ALU.subtract), "to_end_ready", i)
                        wait(dve, pair, "dec_rows_done", i)
                        for t in range(TILES):
                            last = nc.vector.scalar_tensor_tensor(big["decayed"][:, i, cols[t]], bank[i][0][:, cols[t]], sm["dec"][:, i, t:t + 1], ceiling[:],
                                                                  ALU.subtract, ALU.min)
                        done(last, "floor_ready", i)
                    for i in range(2):
                        wait(dve, pair, "wk_ready", i)
                        done(nc.vector.tensor_tensor(tiled(big["wkb"], i), tiled(big["wk"], i), spread(gates[:, i, :, 1]), ALU.mult), "wkb_ready", i)
                    for i in range(2):
                        wait(dve, pair, "decayed_ready", i)
                        wait(dve, pair, "attn_done", i)
                        done(nc.vector.tensor_tensor(big["attn_t"][:, i], bank[i][0][:], big["decayed"][:, i], ALU.mult), "attn_ready", i)
                        wait(dve, pair, "gram_done", i)
                        done(nc.vector.tensor_tensor(big["m_t"][:, i], bank[i][3][:], big["decayed"][:, i], ALU.mult), "m_ready", i)
                    for level in range(LEVELS):
                        for i in range(2):
                            if level == 0:
                                wait(dve, pair, "off_ready", i, 1)
                                done(nc.vector.tensor_tensor(tiled(big["inv_t"], i), every(g.ident[:]), off_t[:, i, 0].rearrange("p (t d) -> p t d", d=P), ALU.subtract), "inv_t_ready", i)
                                wait(dve, pair, "t1_done", i, 1)
                                done(nc.vector.tensor_tensor(tiled(big["inv"], i), every(g.ident[:]), banked(i, 0), ALU.subtract), "inv_ready", i)
                                continue
                            if level < LEVELS - 1:
                                wait(dve, pair, "u_done", i, level)
                                wait(dve, pair, "inv_ready", i, level)
                                done(nc.vector.tensor_tensor(big["inv"][:, i], big["inv"][:, i], bank[i][1][:], ALU.subtract), "inv_ready", i)
                            wait(dve, pair, "ut_done", i, level)
                            wait(dve, pair, "inv_t_ready", i, level)
                            done(nc.vector.tensor_tensor(big["inv_t"][:, i], big["inv_t"][:, i], bank[i][2][:], ALU.subtract), "inv_t_ready", i)
                    for i in range(2):
                        done(nc.vector.memset(state[:, i], 0.0), "state_ready", i)
                        dve.sem_inc(q["inv_ready"][i], 1)
                    for c in range(CHUNKS):
                        t, rows = c // 2, slice(CHUNK * (c % 2), CHUNK * (c % 2) + CHUNK)
                        for i in range(2):
                            if c == 0:
                                wait(dve, pair, "vp_ready", i)
                            wait(dve, pair, "vs_done", i, c + 1)
                            done(nc.vector.tensor_tensor(big["v_new"][rows, i, cols[t]], big["vp"][rows, i, cols[t]], bank[i][2][rows, 0:P], ALU.subtract), "v_new_ready", i)
                        for i in range(2):
                            wait(dve, pair, "update_done", i, c + 1)
                            wait(dve, pair, "state_ready", i, c + 1)
                            done(nc.vector.scalar_tensor_tensor(state[:, i], state[:, i], carry[:, i, c:c + 1], bank[i][0][:, 0:P], ALU.mult, ALU.add), "state_ready", i)
                    for i in range(2):
                        wait(dve, pair, "out_done", i)
                        for t in range(TILES):
                            last = nc.vector.scalar_tensor_tensor(big["y"][:, i, cols[t]], bank[i][1][:, cols[t]], gates[:, i, t, 0:1], big["xt"][:, i, cols[t]], ALU.mult, ALU.add)
                        done(last, "y_ready", i)
                        wait(dve, pair, "y_ready", i)
                        xt = seq_of(g.X, pair, i)
                        done(nc.vector.tensor_tensor(xt, xt, big["y"][:, i], ALU.add), "x_added", i)

    run_phase(nc, name, body)


class Kept:

    def __init__(self, nc, ctx):
        def sb(name, shape):
            return ctx.enter_context(nc.sbuf_tensor(name, shape, F32))

        self.X = sb("X", [P, SEQS, TOKENS])
        self.XH = sb("XH", [P, SEQS, TOKENS])
        self.ident = sb("ident", [P, P])
        self.minus_half = sb("minus_half", [P, 64])
        self.rank8 = sb("rank8", [P, 8])


def load_phase(nc, g, x, a):
    def body(ph):
        loaded = ph.sem("loaded")
        with nc.Block() as block:

            @block.sync
            def _(sp):
                sp.dma_start(g.X[:].rearrange("p s (t d) -> p (s t) d", d=P), x.rearrange("s (t p) d -> p (s t) d", p=P)).then_inc(loaded, 16)
                sp.dma_start(g.ident[:], a["ident"]).then_inc(loaded, 16)
                sp.dma_start(g.rank8[:], a["rank8"]).then_inc(loaded, 16)
                sp.wait_ge(loaded, 16 * 3)

            @block.vector
            def _(dve):
                nc.vector.memset(g.minus_half[:], -0.5)

    run_phase(nc, "load", body)


def store_phase(nc, g, out):
    def body(ph):
        stored = ph.sem("stored")
        with nc.Block() as block:

            @block.sync
            def _(sp):
                sp.dma_start(out.rearrange("s (t p) d -> p (s t) d", p=P), g.X[:].rearrange("p s (t d) -> p (s t) d", d=P)).then_inc(stored, 16)
                sp.wait_ge(stored, 16)

    run_phase(nc, "store", body)


def build_program(nc, a, out):
    def of(layer, *names):
        return {n: a[f"{layer}_{n}"] for n in names}

    with ExitStack() as ctx:
        g = Kept(nc, ctx)
        load_phase(nc, g, a["L0_attn_x"], a)

        layernorm_pass(nc, g, "norm0")
        delta_rule_phase(nc, g, "delta", of("L0_attn", "W_write", "W_gate", "W_out", "W_beta", "W_alpha", "dt_bias", "A_log")
                         | {n: a[n] for n in ("until", "within", "ends", "ceiling", "corner")})

        layernorm_pass(nc, g, "norm1")
        local_transformer_phase(nc, g, "local", of("L0_ffn", "Wqkv", "q_scale", "k_scale", "Wo", "ln_g", "ln_b", "W1", "b1", "W2", "b2")
                                | {n: a[n] for n in ("rotary", "band")})
        add_back_phase(nc, g, "back")

        layernorm_pass(nc, g, "norm2")
        l1 = of("L1_attn", "wq", "wk", "wv", "wo")
        softmax_attention_phase(nc, g, "causal", {
            "wq": l1["wq"].rearrange("m h d -> m (h d)"), "wk": l1["wk"].rearrange("m h d -> m (h d)"), "wv": l1["wv"].rearrange("m h d -> m (h d)"),
            "wo": l1["wo"].rearrange("h d m -> (h d) m"), "cos": a["rope_cos"], "sin": a["rope_sin"], "mask": a["never_later"]}, causal_only=True)

        layernorm_pass(nc, g, "norm3")
        moe_phase(nc, g, "moe1", {"wg": a["L1_ffn_Wg"], "wg_t": None, "bg": a["L1_ffn_bg"], "w1": a["L1_ffn_W1"], "b1": a["L1_ffn_b1"],
                                  "w2": a["L1_ffn_W2"], "b2": a["L1_ffn_b2"]}, ACT.Gelu_apprx_tanh, top2=True)

        layernorm_pass(nc, g, "norm4")
        chunk_attention_phase(nc, g, "chunked", of("L2_attn", "Wqk", "bqk", "Wv", "bv", "gamma", "beta", "rel_emb")
                              | {n: a[n] for n in ("bucket", "chunk_mask")})

        layernorm_pass(nc, g, "norm5")
        moe_phase(nc, g, "moe2", {"wg": a["L2_ffn_router_w"], "wg_t": None, "bg": a["L2_ffn_router_b"], "w1": a["L2_ffn_W1"], "b1": a["L2_ffn_b1"],
                                  "w2": a["L2_ffn_W2"], "b2": a["L2_ffn_b2"]}, ACT.Gelu, top2=False)

        layernorm_pass(nc, g, "norm6")
        softmax_attention_phase(nc, g, "relu", {n.lower(): ap for n, ap in of("L3_attn", "Wq", "Wk", "Wv", "Wo", "bq", "bk", "bv", "bo").items()}
                                | {"mask": a["less_later"]}, causal_only=False)

        layernorm_pass(nc, g, "norm7")
        moe_phase(nc, g, "moe3", {"wg": None, "wg_t": a["L3_ffn_Wg"], "bg": None, "w1": a["L3_ffn_W1"], "b1": a["L3_ffn_b1"],
                                  "w2": a["L3_ffn_W2"], "b2": a["L3_ffn_b2"]}, ACT.Gelu, top2=False)

        store_phase(nc, g, out)


def shape_constants():
    f = np.float32
    c = {"ident": np.eye(P, dtype=f), "rank8": np.tile(np.arange(8, 0, -1, dtype=f), (P, 1))}

    j, i = np.arange(P)[:, None], np.arange(P)[None]
    same = j // 64 == i // 64
    c["until"] = (same & (j <= i)).astype(f)
    c["within"] = same.astype(f)
    c["ends"] = (j // 64 == np.arange(2)[None]).astype(f)
    c["ceiling"] = np.where(same & (j <= i), f(-NEVER), f(NEVER))
    c["corner"] = np.stack([((i >> b) % 2 == 1) & (j >> b == (i >> b) - 1) for b in range(6)], 1).astype(f)
    c["chunk_mask"] = np.where(same & (i <= j), f(0), f(NEVER))

    half = np.arange(0, 64, 2, dtype=f)
    angle = np.arange(TOKENS, dtype=f)[:, None] * (f(1) / f(10000) ** (half / f(64)))[None]
    scale = ((half + f(25.6)) / f(89.6))[None] ** ((np.arange(TOKENS, dtype=f) - f(256)) / f(16))[:, None]
    angle, scale = np.tile(angle, 2).astype(np.float64), np.tile(scale, 2)
    cos, sin = np.cos(angle), np.sin(angle) * np.where(np.arange(64) < 32, -1, 1)
    rotary = np.stack([cos * scale * 8, sin * scale * 8, cos / scale, sin / scale], 1).astype(f)
    c["rotary"] = rotary.reshape(TILES, P, 4, 64).transpose(1, 0, 2, 3)
    r, k = np.arange(P)[:, None], np.arange(96)[None]
    near = (k >= r % 64) & (k <= r % 64 + 32)
    c["band"] = np.stack([np.where(near & ((r >= 64) | (k >= 32)), 0, NEVER), np.where(near, 0, NEVER)], 1).astype(f)

    angle = np.arange(TOKENS, dtype=f)[:, None] * (f(10000) ** (-(np.arange(32) / 32)).astype(f))[None]
    cos, sin = np.cos(angle.astype(np.float64)).T, np.sin(angle.astype(np.float64)).T
    root = P ** -0.5
    c["rope_cos"] = (np.concatenate([cos, cos, np.ones((64, TOKENS))]) * root).astype(f)
    c["rope_sin"] = (np.concatenate([sin, sin]) * root).astype(f)
    later = np.arange(7 * P)[None] - 3 * P > np.arange(P)[:, None]
    c["never_later"] = np.where(later, f(-1e30), f(0))
    c["less_later"] = np.where(later, f(-1e4), f(0))

    n = np.arange(64)
    large = 16 + np.log(np.maximum(n, 1).astype(f) / 16) / math.log(8) * 16
    bucket = np.where(n < 16, n, np.minimum(large, 31)).astype(np.int32)
    c["bucket"] = np.zeros((32, 2 * P - 1), f)
    c["bucket"][bucket, P - 1 - n] = 1
    return {name: np.ascontiguousarray(table) for name, table in c.items()}


def kernel(**inputs):
    import concourse.bacc as bacc
    from concourse.bass_utils import run_bass_kernel_spmd

    nc = bacc.Bacc("TRN2", target_bir_lowering=False, num_devices=1)
    arrays, aps = {}, {}
    for name, array in [*inputs.items(), *shape_constants().items()]:
        array = np.ascontiguousarray(array)
        arrays[f"in_{name}"] = array
        aps[name] = nc.dram_tensor(f"in_{name}", array.shape, mybir.dt.from_np(array.dtype), kind="ExternalInput").ap()
    out = nc.dram_tensor("out_x", (SEQS, TOKENS, P), F32, kind="ExternalOutput").ap()
    build_program(nc, aps, out)
    return run_bass_kernel_spmd(nc, [arrays], core_ids=[0]).results[0]["out_x"]
```

```python
import math

import numpy as np

import concourse.bass as bass
from concourse import mybir
from contextlib import ExitStack

F32 = mybir.dt.float32
F32R = mybir.dt.float32r
ALU = mybir.AluOpType
ACT = mybir.ActivationFunctionType
AX = mybir.AxisListType.X

P = 128
SEQS = 8
TOKENS = 512
TILES = TOKENS // P
LN_EPS = 1e-5
NEVER = -3.0e38


class Phase:

    def __init__(self, nc, name, ctx):
        self.nc, self.name, self.ctx = nc, name, ctx
        self.sems = []

    def sb(self, name, shape, dtype=F32):
        return self.ctx.enter_context(self.nc.sbuf_tensor(f"{self.name}_{name}", shape, dtype))

    def ps(self, name, shape, dtype=F32):
        return self.ctx.enter_context(self.nc.psum_tensor(f"{self.name}_{name}", shape, dtype))

    def sem(self, name):
        s = self.nc.alloc_semaphore(f"{self.name}_{name}")
        self.sems.append(s)
        return s


def run_phase(nc, name, body):
    with ExitStack() as ctx:
        ph = Phase(nc, name, ctx)
        body(ph)
    nc.clear_and_free_semaphores(ph.sems)
    nc.all_engine_barrier()


def layernorm_pass(nc, g, name):

    def body(ph):
        stats = ph.sb("stats", [P, SEQS * TILES, 6])
        mean_var = ph.sb("mean_var", [P, SEQS * TILES, 2])
        var_eps = ph.sb("var_eps", [P, SEQS * TILES])
        rstd = ph.sb("rstd", [P, SEQS * TILES])
        x_hat = ph.sb("x_hat", [P, 2, TOKENS])
        turned = [ph.ps(f"turned{i}", [P, TOKENS]) for i in range(2)]
        stats_ready = ph.sem("stats_ready")
        aggregated = ph.sem("aggregated")
        var_ready = ph.sem("var_ready")
        rstd_ready = ph.sem("rstd_ready")
        x_hat_ready = [ph.sem(f"x_hat_ready{i}") for i in range(2)]
        turned_ready = [ph.sem(f"turned_ready{i}") for i in range(2)]
        turned_used = [ph.sem(f"turned_used{i}") for i in range(2)]
        PAIRS = SEQS // 2

        with nc.Block() as block:

            @block.vector
            def _(dve):
                with dve.Fori(0, SEQS) as s:
                    for t in range(TILES):
                        last = nc.vector.bn_stats(stats[:, bass.ds(s * TILES + t, 1), :], g.X[:, bass.ds(s, 1), t * P:(t + 1) * P])
                    last.then_inc(stats_ready, 1)
                dve.wait_ge(stats_ready, SEQS)
                for n in range(SEQS * TILES):
                    last = nc.vector.bn_aggr(mean_var[:, n, :], stats[:, n, :])
                last.then_inc(aggregated, 1)
                dve.wait_ge(aggregated, 1)
                nc.vector.tensor_scalar(var_eps[:], mean_var[:, :, 1], LN_EPS, None, ALU.add).then_inc(var_ready, 1)
                dve.wait_ge(rstd_ready, 1)
                for i in range(2):
                    dve.sem_inc(x_hat_ready[i], 1)
                with dve.Fori(1, PAIRS + 1) as pair:
                    for i in range(2):
                        dve.wait_ge(turned_ready[i], pair)
                        for t in range(TILES):
                            row = pair * (2 * TILES) + ((i - 2) * TILES + t)
                            last = nc.vector.tensor_scalar(
                                x_hat[:, i, t * P:(t + 1) * P], g.X[:, bass.ds(pair * 2 + (i - 2), 1), t * P:(t + 1) * P],
                                mean_var[:, bass.ds(row, 1), 0], rstd[:, bass.ds(row, 1)], ALU.subtract, ALU.mult)
                        last.then_inc(x_hat_ready[i], 1)

            @block.gpsimd
            def _(pool):
                pool.wait_ge(var_ready, 1)
                nc.gpsimd.tensor_tensor(rstd[:], var_eps[:], g.minus_half[:, 0:SEQS * TILES], ALU.pow).then_inc(rstd_ready, 1)

            @block.tensor
            def _(pe):
                for i in range(2):
                    pe.sem_inc(turned_ready[i], 1)
                with pe.Fori(1, PAIRS + 1) as pair:
                    for i in range(2):
                        pe.wait_ge(x_hat_ready[i], pair + 1)
                        pe.wait_ge(turned_used[i], pair)
                        for t in range(TILES):
                            last = nc.tensor.transpose(turned[i][:, t * P:(t + 1) * P], x_hat[:, i, t * P:(t + 1) * P], g.ident[:])
                        last.then_inc(turned_ready[i], 1)

            @block.scalar
            def _(act):
                for i in range(2):
                    act.sem_inc(turned_used[i], 1)
                with act.Fori(1, PAIRS + 1) as pair:
                    for i in range(2):
                        act.wait_ge(turned_ready[i], pair + 1)
                        nc.scalar.copy(g.XH[:, bass.ds(pair * 2 + (i - 2), 1), :], turned[i][:]).then_inc(turned_used[i], 1)

    run_phase(nc, name, body)


def moe_phase(nc, g, name, w, gelu, top2):
    E, FC = 8, 4

    def body(ph):
        w1 = ph.sb("w1", [P, E, FC, P])
        w2 = ph.sb("w2", [P, E, FC, P])
        b1 = ph.sb("b1", [P, E, FC])
        b2 = ph.sb("b2", [E, P])
        wg = ph.sb("wg", [P, E])
        wg_rows = ph.sb("wg_rows", [E, P])
        bg = ph.sb("bg", [P, E])
        xs = ph.sb("xs", [P, TOKENS])
        hid = ph.sb("hid", [P, 2, FC, TOKENS])
        score = ph.sb("score", [P, TILES, E])
        tmp = ph.sb("tmp", [P, TILES, E])
        tmp2 = ph.sb("tmp2", [P, TILES, E])
        pick = ph.sb("pick", [P, 2, TILES, E])
        combine = ph.sb("combine", [P, TILES, E])
        small = ph.sb("small", [P, 8, TILES])
        combine_t = ph.sb("combine_t", [E, TOKENS])
        acc = ph.sb("acc", [P, TOKENS])
        hid_ps = [ph.ps(f"hid_ps{i}", [P, TOKENS]) for i in range(4)]
        y_ps = [ph.ps(f"y_ps{i}", [P, TOKENS]) for i in range(2)]
        small_ps = ph.ps("small_ps", [P, TOKENS])
        bias_ps = ph.ps("bias_ps", [P, TOKENS])
        loaded = ph.sem("loaded")
        router_turned = ph.sem("router_turned")
        router_ready = ph.sem("router_ready")
        xs_ready = ph.sem("xs_ready")
        logits_ready = ph.sem("logits_ready")
        step = ph.sem("routing_step")
        probs_ready = ph.sem("probs_ready")
        combine_ready = ph.sem("combine_ready")
        combine_turned = ph.sem("combine_turned")
        combine_t_ready = ph.sem("combine_t_ready")
        bias_ready = ph.sem("bias_ready")
        hid_done = ph.sem("hid_done")
        gelu_done = ph.sem("gelu_done")
        y_done = ph.sem("y_done")
        y_added = ph.sem("y_added")
        acc_started = ph.sem("acc_started")
        STEPS = 25 if top2 else 6
        has_gbias = w["bg"] is not None
        wg_by_expert = w["wg_t"] is not None
        LOADS = 16 * (4 + 1 + (1 if has_gbias else 0))

        with nc.Block() as block:

            @block.sync
            def _(sp):
                if wg_by_expert:
                    sp.dma_start(wg_rows[:], w["wg_t"]).then_inc(loaded, 16)
                else:
                    sp.dma_start(wg[:], w["wg"]).then_inc(loaded, 16)
                sp.dma_start(w1[:].rearrange("p e b f -> p e (b f)"), w["w1"].rearrange("e d f -> d e f")).then_inc(loaded, 16)
                sp.dma_start(w2[:], w["w2"].rearrange("e (b f) d -> f e b d", f=P)).then_inc(loaded, 16)
                sp.dma_start(b1[:], w["b1"].rearrange("e (b f) -> f e b", f=P), allow_slow_non_contiguous=True).then_inc(loaded, 16)
                sp.dma_start(b2[:], w["b2"]).then_inc(loaded, 16)
                if has_gbias:
                    sp.dma_start(bg[:], w["bg"].partition_broadcast(P)).then_inc(loaded, 16)

            @block.scalar
            def _(act):
                act.sem_inc(gelu_done, E * FC)
                act.wait_ge(loaded, LOADS)
                with act.Fori(1, SEQS + 1) as s:
                    act.wait_ge(hid_done, s * (E * FC))
                    nc.scalar.copy(xs[:], g.XH[:, bass.ds(s - 1, 1), :]).then_inc(xs_ready, 1)
                    if top2:
                        act.wait_ge(step, s * STEPS + 3)
                        nc.scalar.activation(score[:], tmp[:], ACT.Exp).then_inc(probs_ready, 1)
                    for e in range(E):
                        for b in range(FC):
                            n = e * FC + b
                            act.wait_ge(hid_done, s * (E * FC) + (n + 1))
                            if b == 0:
                                act.wait_ge(y_done, s * E + (e - 1) if e >= 2 else (s - 1) * E + (e + E - 1))
                            nc.scalar.activation(hid[:, e % 2, b, :], hid_ps[n % 4][:], gelu, bias=b1[:, e, b:b + 1]).then_inc(gelu_done, 1)
                        if e == 1:
                            act.wait_ge(combine_turned, s)
                            nc.scalar.copy(combine_t[:], small_ps[0:E, :]).then_inc(combine_t_ready, 1)

            @block.tensor
            def _(pe):
                pe.sem_inc(hid_done, E * FC)
                pe.sem_inc(y_done, E)
                pe.wait_ge(loaded, LOADS)
                if wg_by_expert:
                    nc.tensor.transpose(small_ps[:, 0:E], wg_rows[:], g.ident[0:E, 0:E]).then_inc(router_turned, 1)
                    pe.wait_ge(router_ready, 1)
                with pe.Fori(1, SEQS + 1) as s:

                    def down(e):
                        pe.wait_ge(gelu_done, s * (E * FC) + FC * (e + 1))
                        pe.wait_ge(y_added, s * E + (e - 1) if e >= 2 else (s - 1) * E + (e + E - 1))
                        for t in range(TILES):
                            for b in range(FC):
                                last = nc.tensor.matmul(y_ps[e % 2][:, t * P:(t + 1) * P], hid[:, e % 2, b, t * P:(t + 1) * P],
                                                        w2[:, e, b, :], start=(b == 0), stop=(b == FC - 1))
                        last.then_inc(y_done, 1)

                    pe.wait_ge(xs_ready, s)
                    for t in range(TILES):
                        last = nc.tensor.matmul(small_ps[:, t * E:(t + 1) * E], xs[:, t * P:(t + 1) * P], wg[:], start=True, stop=True)
                    last.then_inc(logits_ready, 1)
                    for e in range(E):
                        for b in range(FC):
                            n = e * FC + b
                            pe.wait_ge(gelu_done, s * (E * FC) + (n - 3) if n >= 4 else (s - 1) * (E * FC) + (n + E * FC - 3))
                            nc.tensor.matmul(hid_ps[n % 4][:], w1[:, e, b, :], xs[:], start=True, stop=True).then_inc(hid_done, 1)
                        if e == 1:
                            pe.wait_ge(combine_ready, s)
                            for t in range(TILES):
                                last = nc.tensor.transpose(small_ps[0:E, t * P:(t + 1) * P], combine[:, t, :], g.ident[:])
                            last.then_inc(combine_turned, 1)
                        if e == 2:
                            pe.wait_ge(combine_t_ready, s)
                            for t in range(TILES):
                                last = nc.tensor.matmul(bias_ps[:, t * P:(t + 1) * P], combine_t[:, t * P:(t + 1) * P], b2[:], start=True, stop=True)
                            last.then_inc(bias_ready, 1)
                        if e >= 1:
                            down(e - 1)
                    down(E - 1)

            @block.vector
            def _(dve):
                dve.sem_inc(step, STEPS)
                dve.sem_inc(y_added, E)
                dve.wait_ge(loaded, LOADS)
                if wg_by_expert:
                    dve.wait_ge(router_turned, 1)
                    nc.vector.tensor_copy(wg[:], small_ps[:, 0:E]).then_inc(router_ready, 1)
                with dve.Fori(1, SEQS + 1) as s:
                    made = 0

                    def done(ins):
                        nonlocal made
                        made += 1
                        ins.then_inc(step, 1)
                        dve.wait_ge(step, s * STEPS + made)

                    def spread(row):
                        return small[:, row, :].unsqueeze(2).to_broadcast([P, TILES, E])

                    def first_of(src, row, onehot):
                        done(nc.vector.tensor_tensor(tmp[:], src, spread(row), ALU.is_equal))
                        done(nc.vector.tensor_tensor(tmp[:], tmp[:], g.rank8[:].unsqueeze(1).to_broadcast([P, TILES, E]), ALU.mult))
                        done(nc.vector.tensor_reduce(small[:, row + 2, :], tmp[:], AX, ALU.max))
                        done(nc.vector.tensor_tensor(onehot, tmp[:], spread(row + 2), ALU.is_equal))

                    dve.wait_ge(logits_ready, s)
                    logits = small_ps[:, 0:TILES * E].rearrange("p (t e) -> p t e", e=E)
                    if has_gbias:
                        done(nc.vector.tensor_tensor(score[:], logits, bg[:].unsqueeze(1).to_broadcast([P, TILES, E]), ALU.add))
                    else:
                        done(nc.vector.tensor_copy(score[:], logits))
                    done(nc.vector.tensor_reduce(small[:, 0, :], score[:], AX, ALU.max))
                    if top2:
                        done(nc.vector.tensor_tensor(tmp[:], score[:], spread(0), ALU.subtract))
                        dve.wait_ge(probs_ready, s)
                        done(nc.vector.tensor_reduce(small[:, 4, :], score[:], AX, ALU.add))
                        done(nc.vector.reciprocal(small[:, 5, :], small[:, 4, :]))
                        done(nc.vector.tensor_tensor(score[:], score[:], spread(5), ALU.mult))
                        done(nc.vector.tensor_reduce(small[:, 0, :], score[:], AX, ALU.max))
                        first_of(score[:], 0, pick[:, 0])
                        done(nc.vector.scalar_tensor_tensor(tmp2[:], pick[:, 0], -4.0, score[:], ALU.mult, ALU.add))
                        done(nc.vector.tensor_reduce(small[:, 1, :], tmp2[:], AX, ALU.max))
                        first_of(tmp2[:], 1, pick[:, 1])
                        done(nc.vector.tensor_tensor(small[:, 4, :], small[:, 0, :], small[:, 1, :], ALU.add))
                        done(nc.vector.tensor_scalar(small[:, 5, :], small[:, 4, :], 1e-8, None, ALU.add))
                        done(nc.vector.reciprocal(small[:, 4, :], small[:, 5, :]))
                        for k in range(2):
                            done(nc.vector.tensor_tensor(small[:, 6 + k, :], small[:, k, :], small[:, 4, :], ALU.mult))
                            done(nc.vector.tensor_tensor(pick[:, k], pick[:, k], spread(6 + k), ALU.mult))
                        done(nc.vector.tensor_tensor(combine[:], pick[:, 0], pick[:, 1], ALU.add))
                    else:
                        first_of(score[:], 0, combine[:])
                    assert made == STEPS
                    dve.sem_inc(combine_ready, 1)
                    dve.wait_ge(bias_ready, s)
                    nc.vector.tensor_tensor(acc[:], bias_ps[:], g.X[:, bass.ds(s - 1, 1), :].rearrange("p a t -> p (a t)"), ALU.add).then_inc(acc_started, 1)
                    dve.wait_ge(acc_started, s)
                    for e in range(E):
                        dve.wait_ge(y_done, s * E + (e + 1))
                        if e:
                            dve.wait_ge(y_added, s * E + e)
                        for t in range(TILES):
                            cols = slice(t * P, (t + 1) * P)
                            out = acc[:, cols] if e < E - 1 else g.X[:, bass.ds(s - 1, 1), cols].rearrange("p a t -> p (a t)")
                            last = nc.vector.scalar_tensor_tensor(out, y_ps[e % 2][:, cols], combine[:, t, e:e + 1], acc[:, cols], ALU.mult, ALU.add)
                        last.then_inc(y_added, 1)

    run_phase(nc, name, body)


def softmax_attention_phase(nc, g, name, w, causal_only):
    rope = causal_only

    def body(ph):
        wq = ph.sb("wq", [P, P])
        wk = ph.sb("wk", [P, P])
        wv = ph.sb("wv", [P, P])
        wo = ph.sb("wo", [P, P])
        mask = ph.sb("mask", [P, 7 * P])
        if rope:
            wq_rot = ph.sb("wq_rot", [P, 64])
            wk_rot = ph.sb("wk_rot", [P, 64])
            cos = ph.sb("cos", [P, TOKENS])
            sin = ph.sb("sin", [64, TOKENS])
            rotated = ph.sb("rotated", [64, TOKENS])
        else:
            bias = ph.sb("bias", [P, 3])
            bo = ph.sb("bo", [P, P])
            y = ph.sb("y", [P, P])
        xs = ph.sb("xs", [P, TOKENS])
        q_t = ph.sb("q_t", [P, TOKENS])
        k_t = ph.sb("k_t", [P, TOKENS])
        v_t = ph.sb("v_t", [P, TOKENS])
        vo = ph.sb("vo", [P, TILES, P])
        masked = ph.sb("masked", [P, 2, TOKENS])
        probs = ph.sb("probs", [P, 2, TOKENS])
        probs_t = ph.sb("probs_t", [P, 2, TOKENS])
        neg_max = ph.sb("neg_max", [P, TILES])
        row_sum = ph.sb("row_sum", [P, TILES])
        inv_sum = ph.sb("inv_sum", [P, TILES])
        proj_ps = [ph.ps(f"proj_ps{i}", [P, TOKENS]) for i in range(4)]
        score_ps = [ph.ps(f"score_ps{i}", [P, TOKENS]) for i in range(2)]
        turn_ps = ph.ps("turn_ps", [P, TOKENS])
        out_ps = [ph.ps("out_ps", [P, TOKENS]), proj_ps[3]]
        names = ["loaded", "rot_ready", "xs_ready", "q_projected", "k_projected", "v_projected", "q_scaled", "q_rotated", "q_ready",
                 "k_scaled", "k_rotated", "k_ready", "v_ready", "vo_done", "vo_ready", "scores_done", "masked_ready",
                 "max_ready", "probs_ready", "turned", "probs_t_ready", "out_done", "inv_ready", "y_ready", "x_added"]
        q = {n: ph.sem(n) for n in names}
        LOADS = 16 * (7 if rope else 9)
        SCALE = 1.0 if rope else float(P) ** -0.5
        def keys(t):
            return t + 1 if causal_only else TILES

        with nc.Block() as block:

            @block.sync
            def _(sp):
                for dst, key in ((wq, "wq"), (wk, "wk"), (wv, "wv"), (wo, "wo"), (mask, "mask")):
                    sp.dma_start(dst[:], w[key]).then_inc(q["loaded"], 16)
                if rope:
                    sp.dma_start(cos[:], w["cos"]).then_inc(q["loaded"], 16)
                    sp.dma_start(sin[:], w["sin"]).then_inc(q["loaded"], 16)
                else:
                    for i, key in enumerate(("bq", "bk", "bv")):
                        sp.dma_start(bias[:, i:i + 1], w[key].unsqueeze(1)).then_inc(q["loaded"], 16)
                    sp.dma_start(bo[:], w["bo"].partition_broadcast(P)).then_inc(q["loaded"], 16)

            @block.scalar
            def _(act):
                act.sem_inc(q["probs_ready"], TILES)
                act.wait_ge(q["loaded"], LOADS)
                with act.Fori(1, SEQS + 1) as s:

                    def copy_probs_t(t):
                        act.wait_ge(q["turned"], (s - 1) * TILES + (t + 1))
                        act.wait_ge(q["out_done"], s * TILES + (t - 1) if t >= 2 else (s - 1) * TILES + (t + 3))
                        n = keys(t) * P
                        nc.scalar.copy(probs_t[:, t % 2, 0:n], turn_ps[:, 0:n]).then_inc(q["probs_t_ready"], 1)

                    nc.scalar.copy(xs[:], g.XH[:, bass.ds(s - 1, 1), :]).then_inc(q["xs_ready"], 1)
                    if not rope:
                        act.wait_ge(q["q_projected"], s)
                        nc.scalar.activation(q_t[:], proj_ps[0][:], ACT.Relu, bias=bias[:, 0:1]).then_inc(q["q_ready"], 1)
                        act.wait_ge(q["k_projected"], s)
                        nc.scalar.activation(k_t[:], proj_ps[2][:], ACT.Relu, bias=bias[:, 1:2]).then_inc(q["k_ready"], 1)
                    act.wait_ge(q["v_projected"], s)
                    if rope:
                        nc.scalar.copy(v_t[:], turn_ps[:]).then_inc(q["v_ready"], 1)
                    else:
                        nc.scalar.activation(v_t[:], turn_ps[:], ACT.Relu, bias=bias[:, 2:3]).then_inc(q["v_ready"], 1)
                    act.wait_ge(q["vo_done"], s)
                    nc.scalar.copy(vo[:].rearrange("p t d -> p (t d)"), out_ps[0][:]).then_inc(q["vo_ready"], 1)
                    for t in range(TILES):
                        act.wait_ge(q["max_ready"], (s - 1) * TILES + (t + 1))
                        n = keys(t) * P
                        nc.scalar.activation(probs[:, t % 2, 0:n], masked[:, t % 2, 0:n], ACT.Exp, bias=neg_max[:, t:t + 1],
                                             accum_out=row_sum[:, t:t + 1]).then_inc(q["probs_ready"], 1)
                        if t:
                            copy_probs_t(t - 1)
                    copy_probs_t(TILES - 1)

            @block.tensor
            def _(pe):
                pe.sem_inc(q["out_done"], TILES)
                pe.wait_ge(q["loaded"], LOADS)
                if rope:
                    pe.wait_ge(q["rot_ready"], 1)
                with pe.Fori(1, SEQS + 1) as s:

                    def scores(t):
                        pe.wait_ge(q["masked_ready"], s * TILES + (t - 1) if t >= 2 else (s - 1) * TILES + (t + 3))
                        nc.tensor.matmul(score_ps[t % 2][:, 0:keys(t) * P], q_t[:, t * P:(t + 1) * P], k_t[:, 0:keys(t) * P],
                                         start=True, stop=True).then_inc(q["scores_done"], 1)

                    pe.wait_ge(q["xs_ready"], s)
                    if rope:
                        nc.tensor.matmul(proj_ps[0][:], wq[:], xs[:], start=True, stop=True)
                        nc.tensor.matmul(proj_ps[1][0:64, :], wq_rot[:], xs[:], start=True, stop=True).then_inc(q["q_projected"], 1)
                        nc.tensor.matmul(proj_ps[2][:], wk[:], xs[:], start=True, stop=True)
                        pe.wait_ge(q["x_added"], s * TILES)
                        nc.tensor.matmul(proj_ps[3][0:64, :], wk_rot[:], xs[:], start=True, stop=True).then_inc(q["k_projected"], 1)
                    else:
                        nc.tensor.matmul(proj_ps[0][:], wq[:], xs[:], start=True, stop=True).then_inc(q["q_projected"], 1)
                        nc.tensor.matmul(proj_ps[2][:], wk[:], xs[:], start=True, stop=True).then_inc(q["k_projected"], 1)
                    nc.tensor.matmul(turn_ps[:], wv[:], xs[:], start=True, stop=True).then_inc(q["v_projected"], 1)
                    pe.wait_ge(q["q_ready"], s)
                    pe.wait_ge(q["k_ready"], s)
                    scores(0)
                    scores(1)
                    pe.wait_ge(q["v_ready"], s)
                    if not rope:
                        pe.wait_ge(q["x_added"], s * TILES)
                    for t in range(TILES):
                        last = nc.tensor.matmul(out_ps[0][:, t * P:(t + 1) * P], v_t[:, t * P:(t + 1) * P], wo[:], start=True, stop=True)
                    last.then_inc(q["vo_done"], 1)
                    pe.wait_ge(q["vo_ready"], s)
                    for t in range(TILES):
                        pe.wait_ge(q["probs_ready"], s * TILES + (t + 1))
                        for k in range(keys(t)):
                            last = nc.tensor.transpose(turn_ps[:, k * P:(k + 1) * P], probs[:, t % 2, k * P:(k + 1) * P], g.ident[:])
                        last.then_inc(q["turned"], 1)
                        if t + 2 < TILES:
                            scores(t + 2)
                        pe.wait_ge(q["probs_t_ready"], (s - 1) * TILES + (t + 1))
                        if t >= 2:
                            pe.wait_ge(q["x_added"], s * TILES + (t - 1))
                        for k in range(keys(t)):
                            last = nc.tensor.matmul(out_ps[t % 2][:, 0:P], probs_t[:, t % 2, k * P:(k + 1) * P], vo[:, k, :],
                                                    start=(k == 0), stop=(k == keys(t) - 1))
                        last.then_inc(q["out_done"], 1)

            @block.vector
            def _(dve):
                dve.sem_inc(q["masked_ready"], TILES)
                dve.sem_inc(q["x_added"], TILES)
                dve.wait_ge(q["loaded"], LOADS)
                if rope:
                    for src, dst in ((wq, wq_rot), (wk, wk_rot)):
                        nc.vector.tensor_scalar(dst[:, 0:32], src[:, 32:64], -1.0, None, ALU.mult)
                        last = nc.vector.tensor_copy(dst[:, 32:64], src[:, 0:32])
                    last.then_inc(q["rot_ready"], 1)
                with dve.Fori(1, SEQS + 1) as s:

                    def add_output(t):
                        cols = slice(t * P, (t + 1) * P)
                        xt = g.X[:, bass.ds(s - 1, 1), cols].rearrange("p a t -> p (a t)")
                        out = out_ps[t % 2][:, 0:P]
                        dve.wait_ge(q["out_done"], s * TILES + (t + 1))
                        nc.vector.reciprocal(inv_sum[:, t:t + 1], row_sum[:, t:t + 1]).then_inc(q["inv_ready"], 1)
                        dve.wait_ge(q["inv_ready"], (s - 1) * TILES + (t + 1))
                        if rope:
                            nc.vector.scalar_tensor_tensor(xt, out, inv_sum[:, t:t + 1], xt, ALU.mult, ALU.add).then_inc(q["x_added"], 1)
                        else:
                            nc.vector.scalar_tensor_tensor(y[:], out, inv_sum[:, t:t + 1], bo[:], ALU.mult, ALU.add).then_inc(q["y_ready"], 1)
                            dve.wait_ge(q["y_ready"], (s - 1) * TILES + (t + 1))
                            nc.vector.scalar_tensor_tensor(xt, y[:], 0.0, xt, ALU.max, ALU.add).then_inc(q["x_added"], 1)

                    if rope:
                        for side, dst, a in (("q", q_t, 0), ("k", k_t, 2)):
                            dve.wait_ge(q[side + "_projected"], s)
                            if side == "k":
                                dve.wait_ge(q["q_ready"], s)
                            nc.vector.tensor_tensor(dst[:], proj_ps[a][:], cos[:], ALU.mult).then_inc(q[side + "_scaled"], 1)
                            nc.vector.tensor_tensor(rotated[:], proj_ps[a + 1][0:64, :], sin[:], ALU.mult).then_inc(q[side + "_rotated"], 1)
                            dve.wait_ge(q[side + "_scaled"], s)
                            dve.wait_ge(q[side + "_rotated"], s)
                            nc.vector.tensor_tensor(dst[0:64, :], dst[0:64, :], rotated[:], ALU.add).then_inc(q[side + "_ready"], 1)
                    for t in range(TILES):
                        n = keys(t) * P
                        dve.wait_ge(q["scores_done"], (s - 1) * TILES + (t + 1))
                        dve.wait_ge(q["probs_ready"], s * TILES + (t - 1) if t >= 2 else (s - 1) * TILES + (t + 3))
                        at = (TILES - 1 - t) * P
                        nc.vector.scalar_tensor_tensor(masked[:, t % 2, 0:n], score_ps[t % 2][:, 0:n], SCALE, mask[:, at:at + n],
                                                       ALU.mult, ALU.add).then_inc(q["masked_ready"], 1)
                        dve.wait_ge(q["masked_ready"], s * TILES + (t + 1))
                        nc.vector.tensor_reduce(neg_max[:, t:t + 1], masked[:, t % 2, 0:n], AX, ALU.max, negate=True).then_inc(q["max_ready"], 1)
                        if t:
                            add_output(t - 1)
                    add_output(TILES - 1)

    run_phase(nc, name, body)


def chunk_attention_phase(nc, g, name, w):
    PAIRS = SEQS // 2
    SPAN = 2 * P - 1

    def body(ph):
        wqk = ph.sb("wqk", [P, P])
        wv = ph.sb("wv", [P, P])
        bqk = ph.sb("bqk", [P, 1])
        bv = ph.sb("bv", [P, P])
        gamma = ph.sb("gamma", [P, 2])
        beta = ph.sb("beta", [P, 2])
        rel = ph.sb("rel", [32, 1])
        rel_wide = ph.sb("rel_wide", [32, P])
        bucket = ph.sb("bucket", [32, SPAN])
        by_distance = ph.sb("by_distance", [P, SPAN])
        mask = ph.sb("mask", [P, P])
        bias = ph.sb("bias", [P, P])
        xs = ph.sb("xs", [P, 2, TOKENS])
        qk = ph.sb("qk", [P, 2, TOKENS])
        q_t = ph.sb("q_t", [P, 2, TOKENS])
        k_t = ph.sb("k_t", [P, 2, TOKENS])
        v_raw = ph.sb("v_raw", [P, 2, TOKENS])
        v = ph.sb("v", [P, 2, TOKENS])
        masked = ph.sb("masked", [P, 2, TOKENS])
        probs = ph.sb("probs", [P, 2, TOKENS])
        probs_t = ph.sb("probs_t", [P, 2, TOKENS])
        top = ph.sb("top", [P, 2, TILES])
        total = ph.sb("total", [P, 2, TILES])
        inv = ph.sb("inv", [P, 2, TILES])
        a_ps = [ph.ps(f"a_ps{i}", [P, TOKENS]) for i in range(2)]
        v_ps = [ph.ps(f"v_ps{i}", [P, TOKENS]) for i in range(2)]
        s_ps = [ph.ps(f"s_ps{i}", [P, TOKENS]) for i in range(2)]
        o_ps = [ph.ps(f"o_ps{i}", [P, TOKENS]) for i in range(2)]
        skew = nc.dram_tensor(f"{name}_skew", [P, SPAN], F32, kind="Internal").ap()
        names = ["loaded", "rel_ready", "distance_ready", "distance_copied", "skew_written", "skew_read", "bias_ready",
                 "xs_ready", "qk_projected", "v_projected", "qk_ready", "v_raw_ready", "v_ready", "q_ready",
                 "scores_done", "masked_ready", "max_ready", "centred", "probs_ready", "sum_ready", "inv_ready", "turned",
                 "probs_t_ready", "out_done", "x_added"]
        q = {n: ph.sem(n) for n in names}
        LOADS = 16 * 9

        with nc.Block() as block:

            @block.sync
            def _(sp):
                for dst, src in ((wqk[:], w["Wqk"]), (wv[:], w["Wv"]), (bqk[:], w["bqk"].unsqueeze(1)),
                                 (bv[:], w["bv"].partition_broadcast(P)), (rel[:], w["rel_emb"]),
                                 (bucket[:], w["bucket"]), (mask[:], w["chunk_mask"])):
                    sp.dma_start(dst, src).then_inc(q["loaded"], 16)
                sp.dma_start(gamma[:], w["gamma"].rearrange("a d -> d a"), allow_slow_non_contiguous=True).then_inc(q["loaded"], 16)
                sp.dma_start(beta[:], w["beta"].rearrange("a d -> d a"), allow_slow_non_contiguous=True).then_inc(q["loaded"], 16)
                sp.wait_ge(q["distance_copied"], 1)
                sp.dma_start(skew, by_distance[:]).then_inc(q["skew_written"], 16)
                sp.wait_ge(q["skew_written"], 16)
                skewed = bass.AP(skew.tensor, P - 1, [[SPAN - 1, P], [1, P]])
                sp.dma_start(bias[:], skewed).then_inc(q["skew_read"], 16)

            @block.scalar
            def _(act):
                act.wait_ge(q["loaded"], LOADS)
                act.wait_ge(q["distance_ready"], 1)
                nc.scalar.mul(by_distance[:], o_ps[0][:, 0:SPAN], float(P) ** 0.5).then_inc(q["distance_copied"], 1)
                with act.Fori(1, PAIRS + 1) as pair:
                    def at(i):
                        return (pair - 1) * 2 + (i + 1)

                    for i in range(2):
                        nc.scalar.copy(xs[:, i], g.XH[:, bass.ds(pair * 2 + (i - 2), 1), :].rearrange("p a t -> p (a t)")).then_inc(q["xs_ready"], 1)
                    for i in range(2):
                        act.wait_ge(q["qk_projected"], at(i))
                        nc.scalar.activation(qk[:, i], a_ps[i][:], ACT.Silu, bias=bqk[:]).then_inc(q["qk_ready"], 1)
                    for i in range(2):
                        act.wait_ge(q["v_raw_ready"], at(i))
                        nc.scalar.activation(v[:, i], v_raw[:, i], ACT.Silu).then_inc(q["v_ready"], 1)
                    for i in range(2):
                        act.wait_ge(q["centred"], at(i))
                        nc.scalar.activation(probs[:, i], masked[:, i], ACT.Exp).then_inc(q["probs_ready"], 1)
                    for i in range(2):
                        act.wait_ge(q["turned"], at(i))
                        nc.scalar.copy(probs_t[:, i], a_ps[i][:]).then_inc(q["probs_t_ready"], 1)

            @block.tensor
            def _(pe):
                pe.sem_inc(q["out_done"], 2)
                pe.wait_ge(q["loaded"], LOADS)
                pe.wait_ge(q["rel_ready"], 1)
                nc.tensor.matmul(o_ps[0][:, 0:SPAN], rel_wide[:], bucket[:], start=True, stop=True).then_inc(q["distance_ready"], 1)
                pe.wait_ge(q["distance_copied"], 1)
                with pe.Fori(1, PAIRS + 1) as pair:
                    def at(i):
                        return (pair - 1) * 2 + (i + 1)

                    for i in range(2):
                        pe.wait_ge(q["xs_ready"], at(i))
                        nc.tensor.matmul(a_ps[i][:], wqk[:], xs[:, i], start=True, stop=True).then_inc(q["qk_projected"], 1)
                        for t in range(TILES):
                            last = nc.tensor.matmul(v_ps[i][:, t * P:(t + 1) * P], xs[:, i, t * P:(t + 1) * P], wv[:], start=True, stop=True)
                        last.then_inc(q["v_projected"], 1)
                    for i in range(2):
                        pe.wait_ge(q["q_ready"], at(i))
                        for t in range(TILES):
                            last = nc.tensor.matmul(s_ps[i][:, t * P:(t + 1) * P], q_t[:, i, t * P:(t + 1) * P], k_t[:, i, t * P:(t + 1) * P],
                                                    start=True, stop=True)
                        last.then_inc(q["scores_done"], 1)
                    for i in range(2):
                        pe.wait_ge(q["probs_ready"], at(i))
                        for t in range(TILES):
                            last = nc.tensor.transpose(a_ps[i][:, t * P:(t + 1) * P], probs[:, i, t * P:(t + 1) * P], g.ident[:])
                        last.then_inc(q["turned"], 1)
                    for i in range(2):
                        pe.wait_ge(q["probs_t_ready"], at(i))
                        pe.wait_ge(q["v_ready"], at(i))
                        pe.wait_ge(q["x_added"], at(i))
                        for t in range(TILES):
                            last = nc.tensor.matmul(o_ps[i][:, t * P:(t + 1) * P], probs_t[:, i, t * P:(t + 1) * P], v[:, i, t * P:(t + 1) * P],
                                                    start=True, stop=True)
                        last.then_inc(q["out_done"], 1)

            @block.vector
            def _(dve):
                dve.sem_inc(q["x_added"], 2)
                dve.wait_ge(q["loaded"], LOADS)
                nc.vector.tensor_copy(rel_wide[:], rel[:].to_broadcast([32, P])).then_inc(q["rel_ready"], 1)
                dve.wait_ge(q["skew_read"], 16)
                nc.vector.tensor_tensor(bias[:], bias[:], mask[:], ALU.add).then_inc(q["bias_ready"], 1)
                dve.wait_ge(q["bias_ready"], 1)
                with dve.Fori(1, PAIRS + 1) as pair:
                    def at(i):
                        return (pair - 1) * 2 + (i + 1)

                    def tiles(buf, i):
                        return buf[:, i].rearrange("p (t k) -> p t k", k=P)

                    def spread(col, i):
                        return col[:, i, :].unsqueeze(2).to_broadcast([P, TILES, P])

                    for i in range(2):
                        dve.wait_ge(q["v_projected"], at(i))
                        nc.vector.tensor_tensor(tiles(v_raw, i), v_ps[i][:].rearrange("p (t d) -> p t d", d=P),
                                                bv[:].unsqueeze(1).to_broadcast([P, TILES, P]), ALU.add).then_inc(q["v_raw_ready"], 1)
                        dve.wait_ge(q["qk_ready"], at(i))
                        nc.vector.tensor_scalar(q_t[:, i], qk[:, i], gamma[:, 0:1], beta[:, 0:1], ALU.mult, ALU.add)
                        nc.vector.tensor_scalar(k_t[:, i], qk[:, i], gamma[:, 1:2], beta[:, 1:2], ALU.mult, ALU.add).then_inc(q["q_ready"], 1)
                    for i in range(2):
                        dve.wait_ge(q["scores_done"], at(i))
                        nc.vector.scalar_tensor_tensor(tiles(masked, i), s_ps[i][:].rearrange("p (t k) -> p t k", k=P), float(P) ** -0.5,
                                                       bias[:].unsqueeze(1).to_broadcast([P, TILES, P]), ALU.mult, ALU.add).then_inc(q["masked_ready"], 1)
                        dve.wait_ge(q["masked_ready"], at(i))
                        nc.vector.tensor_reduce(top[:, i], tiles(masked, i), AX, ALU.max).then_inc(q["max_ready"], 1)
                        dve.wait_ge(q["max_ready"], at(i))
                        nc.vector.tensor_tensor(tiles(masked, i), tiles(masked, i), spread(top, i), ALU.subtract).then_inc(q["centred"], 1)
                    for i in range(2):
                        dve.wait_ge(q["probs_ready"], at(i))
                        nc.vector.tensor_reduce(total[:, i], tiles(probs, i), AX, ALU.add).then_inc(q["sum_ready"], 1)
                        dve.wait_ge(q["sum_ready"], at(i))
                        nc.vector.reciprocal(inv[:, i], total[:, i]).then_inc(q["inv_ready"], 1)
                    for i in range(2):
                        dve.wait_ge(q["inv_ready"], at(i))
                        dve.wait_ge(q["out_done"], at(i) + 2)
                        for t in range(TILES):
                            xt = g.X[:, bass.ds(pair * 2 + (i - 2), 1), t * P:(t + 1) * P].rearrange("p a t -> p (a t)")
                            last = nc.vector.scalar_tensor_tensor(xt, o_ps[i][:, t * P:(t + 1) * P], inv[:, i, t:t + 1], xt, ALU.mult, ALU.add)
                        last.then_inc(q["x_added"], 1)

    run_phase(nc, name, body)


def local_transformer_phase(nc, g, name, w):
    LAYERS, HEADS, HD, BLOCK, WIN, BACK = 6, 16, 64, 64, 96, 32
    INNER = HEADS * HD
    CH = INNER // P
    GROUPS = 4
    HPG = HEADS // GROUPS
    HIDDEN = 341
    HCH = [(0, P), (P, P), (2 * P, HIDDEN - 2 * P)]
    PV_HEADS = [(0, 6), (6, 11), (11, 16)]

    def s_banks(t):
        return (0, 1, 2, 3) if t % 2 == 0 else (2, 3, 0, 1)

    def pv_banks(t):
        b = s_banks(t)
        return b[3], b[0], b[1]

    FFN_TURN, FFN_BACK, FFN_GATE, FFN_A, FFN_OUT = 1, 2, (3, 1, 3), (0, 2, 0), 2

    def body(ph):
        sb = ph.sb
        stage = sb("stage", [P, 3 * INNER])
        wqkv_hi, wqkv_lo = (sb(n, [P, 3 * INNER], F32R) for n in ("wqkv_hi", "wqkv_lo"))
        ys_hi, ys_lo = (sb(n, [P, BACK + TOKENS], F32R) for n in ("ys_hi", "ys_lo"))
        head_hi, head_lo = (sb(n, [P, P], F32R) for n in ("head_hi", "head_lo"))
        wo = sb("wo", [P, CH, P])
        w1 = sb("w1", [P, 2 * HIDDEN])
        w2 = sb("w2", [P, 3, P])
        b1 = sb("b1", [P, 6])
        ln = sb("ln", [P, 3])
        scales = sb("scales", [P, 2, LAYERS, HD])
        base = sb("base", [P, TILES, 4, HD])
        table = sb("table", [P, TILES, 4, HD])
        band = sb("band", [P, 2, WIN])
        squares = sb("squares", [P, 2 * INNER])
        normed = sb("normed", [P, 2 * INNER])
        rot = sb("rot", [P, 2 * INNER])
        norm2 = sb("norm2", [P, 2 * HEADS])
        norm2c = sb("norm2c", [P, 2 * HEADS])
        inv_norm = sb("inv_norm", [P, 2 * HEADS])
        q_t = sb("q_t", [P, CH, P])
        k_t = sb("k_t", [P, CH, BACK + TOKENS])
        scores = sb("scores", [P, HEADS, WIN])
        top = sb("top", [P, HEADS])
        probs_t = sb("probs_t", [WIN, HEADS, P])
        vals = sb("vals", [WIN, 2, HEADS, HD + 1])
        inv_sum = sb("inv_sum", [P, HEADS])
        att = sb("att", [P, INNER])
        att_t = sb("att_t", [P, CH, P])
        y1 = sb("y1", [P, TOKENS])
        y1s = sb("y1s", [P, TOKENS])
        stats = sb("stats", [P, TILES, 6])
        mean_var = sb("mean_var", [P, TILES, 2])
        var_eps = sb("var_eps", [P, TILES])
        rstd = sb("rstd", [P, TILES])
        y_hat = sb("y_hat", [P, TOKENS])
        xn = sb("xn", [P, TOKENS])
        gates = sb("gates", [P, 3, TOKENS])
        table_pick = sb("table_pick", [P, 2])
        A = [ph.ps(f"A{i}", [P, TOKENS]) for i in range(4)]
        B = [ph.ps(f"B{i}", [P, TOKENS]) for i in range(4)]

        per_tile = {"qk_projected": 4, "scores_done": 4, "v_projected": 4, "probs_turned": 4, "pv_done": 3, "qk_turned": 4,
                    "out_turned": 2, "wo_done": 1,
                    "squared": 4, "v_copied": 4, "exp_done": 2, "probs_t_ready": 4, "qkt_copied": 4, "out_copied": 2,
                    "masked": 4, "max_ready": 2, "norms_ready": 2, "qk_normed": 4, "cos_ready": 2, "sums_inverted": 1,
                    "att_ready": 3, "y_added": 1,
                    "centred": 2, "norms_guarded": 2, "inv_norms_ready": 2, "sin_ready": 2, "rotated": 2}
        per_seq = {"ffn_turned": 1, "ffn_back": 1, "gate_done": 3, "a_done": 3, "w2_done": 1,
                   "head_hi_ready": 1, "head_ready": 1, "ys_hi_ready": 1, "ys_ready": 1, "y1s_ready": 1, "xn_ready": 1, "gelu_done": 3,
                   "stats_ready": 1, "aggregated": 1, "var_ready": 1, "y_hat_ready": 1, "prod_ready": 3, "seq_done": 1,
                   "rstd_ready": 1}
        q = {k: ph.sem(k) for k in (*per_tile, *per_seq)}
        consts_loaded, wqkv_loaded, wo_loaded, ffn_loaded = (ph.sem(k) for k in ("consts_loaded", "wqkv_loaded", "wo_loaded", "ffn_loaded"))
        wait_taken = ph.sem("wait_taken")
        split_hi, split_done = ph.sem("split_hi"), ph.sem("split_done")
        tables_ready, pads_ready = ph.sem("tables_ready"), ph.sem("pads_ready")
        CONST_LOADS, FFN_LOADS = 16 * 4, 16 * 11
        PE_MADE = ("qk_projected", "scores_done", "v_projected", "probs_turned", "pv_done", "qk_turned", "out_turned", "wo_done",
                   "ffn_turned", "ffn_back", "gate_done", "a_done", "w2_done")
        ACT_MADE = ("squared", "v_copied", "exp_done", "probs_t_ready", "qkt_copied", "out_copied", "head_hi_ready", "ys_hi_ready", "y1s_ready",
                    "xn_ready", "gelu_done")
        DVE_MADE = ("masked", "max_ready", "centred", "rotated", "norms_ready", "norms_guarded", "qk_normed", "cos_ready", "sums_inverted", "att_ready", "y_added",
                    "stats_ready", "aggregated", "var_ready", "y_hat_ready", "prod_ready", "seq_done")
        POOL_MADE = ("head_ready", "ys_ready", "inv_norms_ready", "sin_ready", "rstd_ready")

        def credit(eng, made):
            for k in made:
                eng.sem_inc(q[k], per_tile[k] * TILES if k in per_tile else per_seq[k])

        def of_tile(n, key, t, k):
            c = per_tile[key]
            return n * (TILES * c) + (t * c + k)

        def of_seq(n, key, k=1):
            return n * per_seq[key] + k

        def place(h):
            return 8 * (h // 8) + HPG * (h % 2) + (h % 8) // 2

        def y_of(s, c0=0, c1=TOKENS, rows=slice(0, P)):
            return g.XH[rows, bass.ds(s - 1, 1), c0:c1].rearrange("p a t -> p (a t)")

        def of_heads(buf, a):
            return buf[:, a * INNER:(a + 1) * INNER].rearrange("p (h d) -> p h d", d=HD)

        def sine_product(engine, t, a, half):
            to, of = slice(32 * half, 32 * half + 32), slice(32 - 32 * half, 64 - 32 * half)
            return engine.tensor_tensor(of_heads(squares, a)[:, :, to], of_heads(normed, a)[:, :, of],
                                        table[:, t % TILES, 2 * a + 1, to].unsqueeze(1).to_broadcast([P, HEADS, 32]), ALU.mult)

        with nc.Block() as block:

            @block.sync
            def _(sp):
                sp.dma_start(base[:], w["rotary"]).then_inc(consts_loaded, 16)
                sp.dma_start(band[:], w["band"]).then_inc(consts_loaded, 16)
                for i, key in enumerate(("q_scale", "k_scale")):
                    sp.dma_start(scales[:, i].rearrange("p l d -> p (l d)"), w[key].rearrange("l d -> (l d)").partition_broadcast(P)).then_inc(consts_loaded, 16)
                with sp.Fori(1, LAYERS + 1) as layer:
                    one = bass.ds(layer - 1, 1)
                    sp.wait_ge(split_done, layer)
                    sp.dma_start(stage[:], w["Wqkv"][one].rearrange("a d n -> (a d) n")).then_inc(wqkv_loaded, 16)
                    sp.wait_ge(q["wo_done"], layer * (SEQS * TILES) - (SEQS - 1) * TILES)
                    sp.dma_start(wo[:], w["Wo"][one].rearrange("a (c p) d -> p (a c) d", p=P)).then_inc(wo_loaded, 16)
                    sp.wait_ge(q["seq_done"], layer * SEQS - (SEQS - 1))
                    sp.dma_start(w1[:], w["W1"][one].rearrange("a d n -> (a d) n")).then_inc(ffn_loaded, 16)
                    sp.dma_start(w2[:, 0:2], w["W2"][one, 0:2 * P].rearrange("a (c p) d -> p (a c) d", p=P)).then_inc(ffn_loaded, 16)
                    sp.dma_start(w2[0:HIDDEN - 2 * P, 2], w["W2"][one, 2 * P:HIDDEN].rearrange("a p d -> (a p) d")).then_inc(ffn_loaded, 16)
                    for i, key in enumerate(("ln_g", "ln_b", "b2")):
                        sp.dma_start(ln[:, i:i + 1], w[key][one].rearrange("a d -> d a")).then_inc(ffn_loaded, 16)
                    for side in range(2):
                        at = side * HIDDEN
                        sp.dma_start(b1[:, 3 * side:3 * side + 2], w["b1"][one, at:at + 2 * P].rearrange("a (c p) -> p (a c)", p=P),
                                     allow_slow_non_contiguous=True).then_inc(ffn_loaded, 16)
                        sp.dma_start(b1[0:HIDDEN - 2 * P, 3 * side + 2:3 * side + 3], w["b1"][one, at + 2 * P:at + HIDDEN].rearrange("a p -> p a")).then_inc(ffn_loaded, 16)
                    sp.nop().then_inc(ffn_loaded, 16)

            @block.tensor
            def _(pe):
                credit(pe, PE_MADE)
                pe.wait_ge(pads_ready, 3)

                def product(out, hi, lo, d0, d1):
                    nc.tensor.matmul(out, hi, wqkv_hi[:, d0:d1], start=True, stop=False)
                    nc.tensor.matmul(out, hi, wqkv_lo[:, d0:d1], start=False, stop=False)
                    return nc.tensor.matmul(out, lo, wqkv_hi[:, d0:d1], start=False, stop=True)

                def project_qk(n, t):
                    first = t % TILES == 0
                    if first:
                        pe.wait_ge(q["head_ready"], of_seq(n, "head_ready", 1 + t // TILES))
                        hi, lo = head_hi[:], head_lo[:]
                    else:
                        if t == 1:
                            pe.wait_ge(q["ys_ready"], of_seq(n, "ys_ready"))
                        hi, lo = (y[:, BACK + t * P:BACK + (t + 1) * P] for y in (ys_hi, ys_lo))
                    for i in range(4):
                        pe.wait_ge(q["qkt_copied"], of_tile(n, "qkt_copied", t - 1, i + 1))
                        product(A[i][:], hi, lo, i * 512, (i + 1) * 512).then_inc(q["qk_projected"], 1)

                def turn_qk(n, t):
                    for i in range(4):
                        if i % 2 == 0:
                            pe.wait_ge(q["rotated"], of_tile(n, "rotated", t, i // 2 + 1))
                        if i == 0:
                            pe.wait_ge(q["qk_normed"], of_tile(n, "qk_normed", t, 4))
                        for j in range(4):
                            last = nc.tensor.transpose(A[i][:, j * P:(j + 1) * P], rot[:, (4 * i + j) * P:(4 * i + j + 1) * P], g.ident[:])
                        last.then_inc(q["qk_turned"], 1)

                def make_scores(n, t):
                    pe.wait_ge(q["qkt_copied"], of_tile(n, "qkt_copied", t, 4))
                    for half in range(2):
                        if half == 0 and t >= 2:
                            pe.wait_ge(q["y_added"], of_tile(n, "y_added", t - 2, 1))
                        if half == 0 and t >= 1:
                            pe.wait_ge(q["att_ready"], of_tile(n, "att_ready", t - 1, 3))
                        if half == 1 and t == 0:
                            pe.wait_ge(q["seq_done"], n)
                        pe.sem_inc(wait_taken, 1)
                        for j in range(HPG):
                            for odd in range(2):
                                rows, c = slice(HD * odd, HD * odd + HD), 4 * half + j
                                bank = B[s_banks(t)[2 * half + odd]]
                                for b in range(2):
                                    c0 = t * P + b * BLOCK
                                    last = nc.tensor.matmul(bank[b * BLOCK:(b + 1) * BLOCK, j * WIN:(j + 1) * WIN],
                                                            q_t[rows, c, b * BLOCK:(b + 1) * BLOCK], k_t[rows, c, c0:c0 + WIN],
                                                            start=True, stop=True)
                                if j == HPG - 1:
                                    last.then_inc(q["scores_done"], 1)

                def project_v(n, t):
                    for i in range(4):
                        b, half = i // 2, i % 2
                        c0 = t * P + b * BLOCK
                        pe.wait_ge(q["masked"], of_tile(n, "masked", t, i + 1))
                        product(B[s_banks(t)[i]][0:WIN, :], ys_hi[:, c0:c0 + WIN], ys_lo[:, c0:c0 + WIN], 2 * INNER + half * 512, 2 * INNER + (half + 1) * 512).then_inc(q["v_projected"], 1)

                def turn_probs(n, t, ahead):
                    for i in range(GROUPS):
                        if i % 2 == 0:
                            pe.wait_ge(q["exp_done"], of_tile(n, "exp_done", t, i // 2 + 1))
                        if ahead:
                            pe.wait_ge(q["qk_normed"], of_tile(n, "qk_normed", t + 1, i + 1))
                        for h in range(HPG * i, HPG * (i + 1)):
                            last = nc.tensor.transpose(A[i][0:WIN, (h % HPG) * P:(h % HPG + 1) * P], scores[:, h, :], g.ident[:])
                        last.then_inc(q["probs_turned"], 1)

                def weigh_values(n, t):
                    pe.wait_ge(q["v_copied"], of_tile(n, "v_copied", t, 4))
                    if t >= 1:
                        pe.wait_ge(q["out_copied"], of_tile(n, "out_copied", t - 1, 2))
                    for i, (h0, h1) in enumerate(PV_HEADS):
                        pe.wait_ge(q["probs_t_ready"], of_tile(n, "probs_t_ready", t, 2 if h1 <= 8 else 4))
                        for h in range(h0, h1):
                            for b in range(2):
                                last = nc.tensor.matmul(B[pv_banks(t)[i]][b * BLOCK:(b + 1) * BLOCK, (h - h0) * (HD + 1):(h - h0 + 1) * (HD + 1)],
                                                        probs_t[:, place(h), b * BLOCK:(b + 1) * BLOCK], vals[:, b, h, :], start=True, stop=True)
                        last.then_inc(q["pv_done"], 1)

                def project_out(n, t, banks, between=None):
                    pe.wait_ge(q["att_ready"], of_tile(n, "att_ready", t, 3))
                    for i in range(2):
                        if t + 1 < TILES:
                            pe.wait_ge(q["v_copied"], of_tile(n, "v_copied", t + 1, i + 1))
                        for j in range(4):
                            c = 4 * i + j
                            last = nc.tensor.transpose(B[banks[i]][:, j * P:(j + 1) * P], att[:, c * P:(c + 1) * P], g.ident[:])
                        last.then_inc(q["out_turned"], 1)
                    if t + 1 < TILES:
                        pe.wait_ge(q["v_copied"], of_tile(n, "v_copied", t + 1, 3))
                    if between:
                        between()
                    pe.wait_ge(q["out_copied"], of_tile(n, "out_copied", t, 2))
                    for c in range(CH):
                        last = nc.tensor.matmul(B[banks[2]][:, 0:P], wo[:, c, :], att_t[:, c, :], start=(c == 0), stop=(c == CH - 1))
                    last.then_inc(q["wo_done"], 1)

                def sequence(layer, n, more):
                    for t in range(TILES):
                        ahead = t + 1 < TILES or more
                        if ahead and t:
                            project_qk(n, t + 1)
                        make_scores(n, t)
                        project_v(n, t)
                        if t:
                            project_out(n, t - 1, s_banks(t)[0:3])
                        else:
                            pe.wait_ge(wo_loaded, layer * 16)
                        turn_probs(n, t, ahead)
                        weigh_values(n, t)
                        if ahead:
                            turn_qk(n, t + 1)
                    project_out(n, TILES - 1, out_banks_last, (lambda: project_qk(n + 1, 1)) if more else None)

                    pe.wait_ge(q["y1s_ready"], of_seq(n, "y1s_ready"))
                    for t in range(TILES):
                        last = nc.tensor.transpose(B[FFN_TURN][:, t * P:(t + 1) * P], y1s[:, t * P:(t + 1) * P], g.ident[:])
                    last.then_inc(q["ffn_turned"], 1)
                    pe.wait_ge(q["y_hat_ready"], of_seq(n, "y_hat_ready"))
                    for t in range(TILES):
                        last = nc.tensor.transpose(B[FFN_BACK][:, t * P:(t + 1) * P], y_hat[:, t * P:(t + 1) * P], g.ident[:])
                    last.then_inc(q["ffn_back"], 1)
                    pe.wait_ge(ffn_loaded, layer * FFN_LOADS)
                    pe.wait_ge(q["xn_ready"], of_seq(n, "xn_ready"))
                    for i, (h0, hn) in enumerate(HCH):
                        if i == 2:
                            pe.wait_ge(q["gelu_done"], of_seq(n, "gelu_done", 1))
                        nc.tensor.matmul(B[FFN_GATE[i]][0:hn, :], w1[:, HIDDEN + h0:HIDDEN + h0 + hn], xn[:], start=True, stop=True).then_inc(q["gate_done"], 1)
                        if i == 2:
                            pe.wait_ge(q["prod_ready"], of_seq(n, "prod_ready", 1))
                        nc.tensor.matmul(B[FFN_A[i]][0:hn, :], w1[:, h0:h0 + hn], xn[:], start=True, stop=True).then_inc(q["a_done"], 1)
                    for i, (h0, hn) in enumerate(HCH):
                        pe.wait_ge(q["prod_ready"], of_seq(n, "prod_ready", max(i + 1, 2)))
                        last = nc.tensor.matmul(B[FFN_OUT][:], w2[0:hn, i, :], gates[0:hn, i, :], start=(i == 0), stop=(i == 2))
                    last.then_inc(q["w2_done"], 1)

                out_banks_last = (2, 3, 0)
                with pe.Fori(1, LAYERS + 1) as layer:
                    pe.wait_ge(split_done, layer + 1)
                    first = pe.snap(layer * SEQS - (SEQS - 1))
                    project_qk(first, 0)
                    turn_qk(first, 0)
                    project_qk(first, 1)
                    pe.sem_inc(wait_taken, 1)
                    with pe.Fori(1, SEQS) as s:
                        sequence(layer, pe.snap(layer * SEQS + (s - SEQS)), True)
                    sequence(layer, layer * SEQS, False)

            @block.scalar
            def _(act):
                credit(act, ACT_MADE)
                act.wait_ge(pads_ready, 3)

                def square(n, t):
                    for i in range(4):
                        act.wait_ge(q["qk_projected"], of_tile(n, "qk_projected", t, i + 1))
                        if i % 2 == 0:
                            act.wait_ge(q["rotated"], of_tile(n, "rotated", t - 1, i // 2 + 1))
                        nc.scalar.activation(squares[:, i * 512:(i + 1) * 512], A[i][:], ACT.Square).then_inc(q["squared"], 1)

                def copy_qk(n, t):
                    for i in range(4):
                        act.wait_ge(q["qk_turned"], of_tile(n, "qk_turned", t, i + 1))
                        src = A[i][:].rearrange("p (c t) -> p c t", t=P)
                        c0 = BACK + t % TILES * P
                        dst = q_t[:, 4 * i:4 * i + 4, :] if i < 2 else k_t[:, 4 * i - 8:4 * i - 4, c0:c0 + P]
                        nc.scalar.copy(dst, src).then_inc(q["qkt_copied"], 1)

                def copy_v(n, t):
                    for i in range(4):
                        act.wait_ge(q["v_projected"], of_tile(n, "v_projected", t, i + 1))
                        nc.scalar.copy(vals[:, i // 2, 8 * (i % 2):8 * (i % 2) + 8, 0:HD],
                                       B[s_banks(t)[i]][0:WIN, :].rearrange("p (h d) -> p h d", d=HD)).then_inc(q["v_copied"], 1)

                def copy_out(n, t, banks):
                    for i in range(2):
                        act.wait_ge(q["out_turned"], of_tile(n, "out_turned", t, i + 1))
                        nc.scalar.copy(att_t[:, 4 * i:4 * i + 4, :], B[banks[i]][:].rearrange("p (c t) -> p c t", t=P)).then_inc(q["out_copied"], 1)

                def exponentials(n, t, half):
                    act.wait_ge(q["centred"], of_tile(n, "centred", t, half + 1))
                    nc.scalar.activation(scores[:, 8 * half:8 * half + 8, :], scores[:, 8 * half:8 * half + 8, :], ACT.Exp).then_inc(q["exp_done"], 1)

                def read_head(n, s):
                    act.sem_inc(wait_taken, 1)
                    nc.scalar.copy(head_hi[0:HD, :], y_of(s, 0, P, rows=slice(0, HD)))
                    nc.scalar.copy(head_hi[HD:P, 1:], y_of(s, 0, P - 1, rows=slice(HD, P))).then_inc(q["head_hi_ready"], 1)

                def read_sequence(n, s):
                    act.sem_inc(wait_taken, 1)
                    nc.scalar.copy(ys_hi[0:HD, BACK:], y_of(s, rows=slice(0, HD)))
                    nc.scalar.copy(ys_hi[HD:P, BACK + 1:], y_of(s, 0, TOKENS - 1, rows=slice(HD, P))).then_inc(q["ys_hi_ready"], 1)

                def sequence(layer, n, s, more):
                    for t in range(TILES):
                        ahead = t + 1 < TILES or more
                        if ahead and t:
                            square(n, t + 1)
                        exponentials(n, t, 0)
                        copy_v(n, t)
                        if t:
                            copy_out(n, t - 1, s_banks(t))
                        exponentials(n, t, 1)
                        if t == 1 and more:
                            act.wait_ge(q["head_ready"], of_seq(n, "head_ready"))
                            read_head(n + 1, s + 1)
                        if t + 1 == TILES and more:
                            act.wait_ge(q["ys_ready"], of_seq(n, "ys_ready"))
                            read_sequence(n + 1, s + 1)
                        for i in range(GROUPS):
                            act.wait_ge(q["probs_turned"], of_tile(n, "probs_turned", t, i + 1))
                            nc.scalar.copy(probs_t[:, HPG * i:HPG * (i + 1), :], A[i][0:WIN, :].rearrange("p (h t) -> p h t", t=P)).then_inc(q["probs_t_ready"], 1)
                        if ahead:
                            copy_qk(n, t + 1)
                    copy_out(n, TILES - 1, (2, 3))

                    act.wait_ge(q["y_added"], of_tile(n, "y_added", TILES - 1, 1))
                    nc.scalar.copy(y1s[0:HD, :], y1[0:HD, :])
                    nc.scalar.copy(y1s[HD:P, 1:], y1[HD:P, 0:TOKENS - 1]).then_inc(q["y1s_ready"], 1)
                    if more:
                        square(n + 1, 1)
                    nc.scalar.activation(table_pick[:, 1:2], table_pick[:, 0:1], ACT.Gelu)
                    act.wait_ge(ffn_loaded, layer * FFN_LOADS)
                    act.wait_ge(q["ffn_back"], of_seq(n, "ffn_back"))
                    nc.scalar.activation(xn[:], B[FFN_BACK][:], ACT.Identity, bias=ln[:, 1:2], scale=ln[:, 0:1]).then_inc(q["xn_ready"], 1)
                    for i, (h0, hn) in enumerate(HCH):
                        act.wait_ge(q["gate_done"], of_seq(n, "gate_done", i + 1))
                        nc.scalar.activation(gates[0:hn, i, :], B[FFN_GATE[i]][0:hn, :], ACT.Gelu, bias=b1[0:hn, 3 + i:4 + i]).then_inc(q["gelu_done"], 1)
                    nc.scalar.activation(table_pick[:, 1:2], table_pick[:, 0:1], ACT.Exp)

                with act.Fori(1, LAYERS + 1) as layer:
                    first = act.snap(layer * SEQS - (SEQS - 1))
                    act.wait_ge(q["seq_done"], first)
                    read_head(first, 1)
                    read_sequence(first, 1)
                    square(first, 0)
                    copy_qk(first, 0)
                    square(first, 1)
                    with act.Fori(1, SEQS) as s:
                        sequence(layer, act.snap(layer * SEQS + (s - SEQS)), s, True)
                    sequence(layer, layer * SEQS, SEQS, False)

            @block.gpsimd
            def _(pool):
                nc.gpsimd.memset(k_t[:, :, 0:BACK], 0.0)
                nc.gpsimd.memset(vals[:, :, :, HD:HD + 1], 1.0).then_inc(pads_ready, 1)
                credit(pool, POOL_MADE)

                def read_head(n, s):
                    pool.wait_ge(q["head_hi_ready"], of_seq(n, "head_hi_ready"))
                    pool.sem_inc(wait_taken, 1)
                    nc.gpsimd.tensor_tensor(head_lo[0:HD, :], y_of(s, 0, P, rows=slice(0, HD)), head_hi[0:HD, :].bitcast(F32), ALU.subtract)
                    nc.gpsimd.tensor_tensor(head_lo[HD:P, 1:], y_of(s, 0, P - 1, rows=slice(HD, P)), head_hi[HD:P, 1:].bitcast(F32),
                                            ALU.subtract).then_inc(q["head_ready"], 1)
                    pool.wait_ge(q["head_ready"], of_seq(n, "head_ready"))

                def read_sequence(n, s):
                    pool.wait_ge(q["ys_hi_ready"], of_seq(n, "ys_hi_ready"))
                    pool.sem_inc(wait_taken, 1)
                    nc.gpsimd.tensor_tensor(ys_lo[0:HD, BACK:], y_of(s, rows=slice(0, HD)), ys_hi[0:HD, BACK:].bitcast(F32), ALU.subtract)
                    nc.gpsimd.tensor_tensor(ys_lo[HD:P, BACK + 1:], y_of(s, 0, TOKENS - 1, rows=slice(HD, P)), ys_hi[HD:P, BACK + 1:].bitcast(F32),
                                            ALU.subtract).then_inc(q["ys_ready"], 1)
                    pool.wait_ge(q["ys_ready"], of_seq(n, "ys_ready"))

                def invert_norms(n, t):
                    for a in range(2):
                        cols = slice(a * HEADS, (a + 1) * HEADS)
                        pool.wait_ge(q["norms_guarded"], of_tile(n, "norms_guarded", t, a + 1))
                        nc.gpsimd.tensor_tensor(inv_norm[:, cols], norm2c[:, cols], g.minus_half[:, cols], ALU.pow).then_inc(q["inv_norms_ready"], 1)

                def sine_products(n, t):
                    for a in range(2):
                        pool.wait_ge(q["qk_normed"], of_tile(n, "qk_normed", t, 2 * a + 2))
                        for half in range(2 - a):
                            last = sine_product(nc.gpsimd, t, a, half)
                        last.then_inc(q["sin_ready"], 1)

                def sequence(layer, n, s, more):
                    for t in range(TILES):
                        if t + 1 < TILES or more:
                            if t:
                                invert_norms(n, t + 1)
                            sine_products(n, t + 1)
                        if t == 1 and more:
                            pool.wait_ge(q["sin_ready"], of_tile(n, "sin_ready", t + 1, 2))
                            read_head(n + 1, s + 1)
                    if more:
                        pool.wait_ge(q["sin_ready"], of_tile(n, "sin_ready", TILES, 2))
                        read_sequence(n + 1, s + 1)
                    pool.wait_ge(q["var_ready"], of_seq(n, "var_ready"))
                    nc.gpsimd.tensor_tensor(rstd[:], var_eps[:], g.minus_half[:, 0:TILES], ALU.pow).then_inc(q["rstd_ready"], 1)
                    if more:
                        invert_norms(n + 1, 1)

                with pool.Fori(1, LAYERS + 1) as layer:
                    first = pool.snap(layer * SEQS - (SEQS - 1))
                    read_head(first, 1)
                    read_sequence(first, 1)
                    pool.wait_ge(tables_ready, layer)
                    invert_norms(first, 0)
                    sine_products(first, 0)
                    invert_norms(first, 1)
                    with pool.Fori(1, SEQS) as s:
                        sequence(layer, pool.snap(layer * SEQS + (s - SEQS)), s, True)
                    sequence(layer, layer * SEQS, SEQS, False)

            @block.vector
            def _(dve):
                nc.vector.memset(ys_hi[:].bitcast(F32), 0.0).then_inc(pads_ready, 1)
                nc.vector.memset(ys_lo[:].bitcast(F32), 0.0)
                nc.vector.memset(head_hi[:].bitcast(F32), 0.0)
                nc.vector.memset(head_lo[:].bitcast(F32), 0.0)
                nc.vector.memset(table_pick[:], 0.0)
                nc.vector.memset(y1s[:], 0.0).then_inc(pads_ready, 1)
                credit(dve, DVE_MADE)
                dve.sem_inc(split_done, 1)
                dve.wait_ge(consts_loaded, CONST_LOADS)

                def sum_squares(n, t):
                    for a in range(2):
                        for i in (2 * a, 2 * a + 1):
                            dve.wait_ge(q["squared"], of_tile(n, "squared", t, i + 1))
                            last = nc.vector.tensor_reduce(norm2[:, 8 * i:8 * i + 8], squares[:, i * 512:(i + 1) * 512].rearrange("p (h d) -> p h d", d=HD), AX, ALU.add)
                        last.then_inc(q["norms_ready"], 1)
                        dve.wait_ge(q["norms_ready"], of_tile(n, "norms_ready", t, a + 1))
                        cols = slice(a * HEADS, (a + 1) * HEADS)
                        nc.vector.tensor_scalar(norm2c[:, cols], norm2[:, cols], 1e-24, None, ALU.max).then_inc(q["norms_guarded"], 1)

                def normalise(n, t):
                    for i in range(4):
                        if i % 2 == 0:
                            dve.wait_ge(q["inv_norms_ready"], of_tile(n, "inv_norms_ready", t, i // 2 + 1))
                        nc.vector.tensor_tensor(normed[:, i * 512:(i + 1) * 512].rearrange("p (h d) -> p h d", d=HD), A[i][:].rearrange("p (h d) -> p h d", d=HD),
                                                inv_norm[:, 8 * i:8 * i + 8].unsqueeze(2).to_broadcast([P, 8, HD]), ALU.mult).then_inc(q["qk_normed"], 1)

                def cosine_products(n, t):
                    for a in range(2):
                        dve.wait_ge(q["qk_normed"], of_tile(n, "qk_normed", t, 2 * a + 2))
                        dve.wait_ge(q["qk_turned"], of_tile(n, "qk_turned", t - 1, 2 * a + 2))
                        last = nc.vector.tensor_tensor(of_heads(rot, a), of_heads(normed, a), table[:, t % TILES, 2 * a, :].unsqueeze(1).to_broadcast([P, HEADS, HD]), ALU.mult)
                        if a:
                            last = sine_product(nc.vector, t, 1, 1)
                        last.then_inc(q["cos_ready"], 1)

                def add_rotated(n, t):
                    for a in range(2):
                        dve.wait_ge(q["cos_ready"], of_tile(n, "cos_ready", t, a + 1))
                        dve.wait_ge(q["sin_ready"], of_tile(n, "sin_ready", t, a + 1))
                        nc.vector.tensor_tensor(of_heads(rot, a), of_heads(rot, a), of_heads(squares, a), ALU.add).then_inc(q["rotated"], 1)

                def mask(n, t, half):
                    for i in (2 * half, 2 * half + 1):
                        dve.wait_ge(q["scores_done"], of_tile(n, "scores_done", t, i + 1))
                        src = B[s_banks(t)[i]][:, 0:HPG * WIN].rearrange("p (h k) -> p h k", k=WIN)
                        nc.vector.tensor_tensor(scores[:, HPG * i:HPG * (i + 1), :], src, band[:, min(t, 1), :].unsqueeze(1).to_broadcast([P, HPG, WIN]),
                                                ALU.add).then_inc(q["masked"], 1)

                def centre(n, t, half):
                    rows = scores[:, 8 * half:8 * half + 8, :]
                    dve.wait_ge(q["masked"], of_tile(n, "masked", t, 2 * half + 2))
                    nc.vector.tensor_reduce(top[:, 8 * half:8 * half + 8], rows, AX, ALU.max).then_inc(q["max_ready"], 1)
                    dve.wait_ge(q["max_ready"], of_tile(n, "max_ready", t, half + 1))
                    nc.vector.tensor_tensor(rows, rows, top[:, 8 * half:8 * half + 8].unsqueeze(2).to_broadcast([P, 8, WIN]), ALU.subtract).then_inc(q["centred"], 1)

                def divide(n, t):
                    for i, (h0, h1) in enumerate(PV_HEADS):
                        dve.wait_ge(q["pv_done"], of_tile(n, "pv_done", t, i + 1))
                        src = B[pv_banks(t)[i]][:, 0:(h1 - h0) * (HD + 1)].rearrange("p (h d) -> p h d", d=HD + 1)
                        last = nc.vector.reciprocal(inv_sum[:, h0:h1].unsqueeze(2), src[:, :, HD:HD + 1])
                    last.then_inc(q["sums_inverted"], 1)
                    dve.wait_ge(q["sums_inverted"], of_tile(n, "sums_inverted", t, 1))
                    dve.wait_ge(q["out_turned"], of_tile(n, "out_turned", t - 1, 2))
                    for i, (h0, h1) in enumerate(PV_HEADS):
                        src = B[pv_banks(t)[i]][:, 0:(h1 - h0) * (HD + 1)].rearrange("p (h d) -> p h d", d=HD + 1)
                        nc.vector.tensor_tensor(att[:, h0 * HD:h1 * HD].rearrange("p (h d) -> p h d", d=HD), src[:, :, 0:HD],
                                                inv_sum[:, h0:h1].unsqueeze(2).to_broadcast([P, h1 - h0, HD]), ALU.mult).then_inc(q["att_ready"], 1)

                def add_output(n, s, t, bank):
                    dve.wait_ge(q["wo_done"], of_tile(n, "wo_done", t, 1))
                    nc.vector.tensor_tensor(y1[:, t * P:(t + 1) * P], B[bank][:, 0:P], y_of(s, t * P, (t + 1) * P), ALU.add).then_inc(q["y_added"], 1)

                def sequence(layer, n, s, more):
                    for t in range(TILES):
                        ahead = t + 1 < TILES or more
                        if ahead and t:
                            sum_squares(n, t + 1)
                        for half in range(2):
                            mask(n, t, half)
                            centre(n, t, half)
                        if ahead:
                            if t:
                                normalise(n, t + 1)
                            cosine_products(n, t + 1)
                        if t:
                            add_output(n, s, t - 1, s_banks(t)[2])
                        if ahead:
                            add_rotated(n, t + 1)
                        divide(n, t)
                    add_output(n, s, TILES - 1, 0)
                    if more:
                        sum_squares(n + 1, 1)

                    dve.wait_ge(q["ffn_turned"], of_seq(n, "ffn_turned"))
                    for t in range(TILES):
                        last = nc.vector.bn_stats(stats[:, t, :], B[FFN_TURN][:, t * P:(t + 1) * P])
                    last.then_inc(q["stats_ready"], 1)
                    dve.wait_ge(q["stats_ready"], of_seq(n, "stats_ready"))
                    dve.sem_inc(wait_taken, 1)
                    for t in range(TILES):
                        last = nc.vector.bn_aggr(mean_var[:, t, :], stats[:, t, :])
                    last.then_inc(q["aggregated"], 1)
                    dve.wait_ge(q["aggregated"], of_seq(n, "aggregated"))
                    nc.vector.tensor_scalar(var_eps[:], mean_var[:, :, 1], LN_EPS, None, ALU.add).then_inc(q["var_ready"], 1)
                    dve.wait_ge(q["rstd_ready"], of_seq(n, "rstd_ready"))
                    for t in range(TILES):
                        last = nc.vector.tensor_scalar(y_hat[:, t * P:(t + 1) * P], B[FFN_TURN][:, t * P:(t + 1) * P], mean_var[:, t, 0:1], rstd[:, t:t + 1],
                                                       ALU.subtract, ALU.mult)
                    last.then_inc(q["y_hat_ready"], 1)
                    dve.wait_ge(ffn_loaded, layer * FFN_LOADS)
                    for i, (h0, hn) in enumerate(HCH):
                        dve.wait_ge(q["gelu_done"], of_seq(n, "gelu_done", i + 1))
                        dve.wait_ge(q["a_done"], of_seq(n, "a_done", i + 1))
                        nc.vector.scalar_tensor_tensor(gates[0:hn, i, :], B[FFN_A[i]][0:hn, :], b1[0:hn, i:i + 1], gates[0:hn, i, :],
                                                       ALU.add, ALU.mult).then_inc(q["prod_ready"], 1)
                    if more:
                        normalise(n + 1, 1)
                    dve.wait_ge(q["w2_done"], of_seq(n, "w2_done"))
                    nc.vector.scalar_tensor_tensor(y_of(s), B[FFN_OUT][:], ln[:, 2:3], y1[:], ALU.add, ALU.add).then_inc(q["seq_done"], 1)

                with dve.Fori(1, LAYERS + 1) as layer:
                    first = dve.snap(layer * SEQS - (SEQS - 1))
                    for a in range(2):
                        def scale_of(cols, width):
                            return scales[:, a, bass.ds(layer - 1, 1), cols].to_broadcast([P, TILES, width])
                        nc.vector.tensor_tensor(table[:, :, 2 * a, :], base[:, :, 2 * a, :], scale_of(slice(0, 64), 64), ALU.mult)
                        nc.vector.tensor_tensor(table[:, :, 2 * a + 1, 0:32], base[:, :, 2 * a + 1, 0:32], scale_of(slice(32, 64), 32), ALU.mult)
                        last = nc.vector.tensor_tensor(table[:, :, 2 * a + 1, 32:64], base[:, :, 2 * a + 1, 32:64], scale_of(slice(0, 32), 32), ALU.mult)
                    last.then_inc(tables_ready, 1)
                    dve.wait_ge(wqkv_loaded, layer * 16)
                    nc.vector.tensor_copy(wqkv_hi[:], stage[:]).then_inc(split_hi, 1)
                    dve.wait_ge(split_hi, layer)
                    nc.vector.tensor_tensor(wqkv_lo[:], stage[:], wqkv_hi[:].bitcast(F32), ALU.subtract).then_inc(split_done, 1)
                    dve.wait_ge(tables_ready, layer)
                    sum_squares(first, 0)
                    normalise(first, 0)
                    cosine_products(first, 0)
                    add_rotated(first, 0)
                    sum_squares(first, 1)
                    normalise(first, 1)
                    dve.sem_inc(wait_taken, 1)
                    with dve.Fori(1, SEQS) as s:
                        sequence(layer, dve.snap(layer * SEQS + (s - SEQS)), s, True)
                    sequence(layer, layer * SEQS, SEQS, False)

    run_phase(nc, name, body)


def add_back_phase(nc, g, name):

    def body(ph):
        xs = ph.sb("xs", [P, 2, TOKENS])
        turned = [ph.ps(f"turned{i}", [P, TOKENS]) for i in range(2)]
        xs_ready, done, added = ph.sem("xs_ready"), ph.sem("turned_ready"), ph.sem("added")
        PAIRS = SEQS // 2

        with nc.Block() as block:

            @block.scalar
            def _(act):
                with act.Fori(1, PAIRS + 1) as pair:
                    for i in range(2):
                        act.wait_ge(done, (pair - 1) * 2 + (i + 1))
                        nc.scalar.copy(xs[:, i], g.XH[:, bass.ds(pair * 2 + (i - 2), 1), :].rearrange("p a t -> p (a t)")).then_inc(xs_ready, 1)

            @block.tensor
            def _(pe):
                pe.sem_inc(done, 2)
                with pe.Fori(1, PAIRS + 1) as pair:
                    for i in range(2):
                        pe.wait_ge(xs_ready, (pair - 1) * 2 + (i + 1))
                        pe.wait_ge(added, (pair - 1) * 2 + (i + 1))
                        for t in range(TILES):
                            last = nc.tensor.transpose(turned[i][:, t * P:(t + 1) * P], xs[:, i, t * P:(t + 1) * P], g.ident[:])
                        last.then_inc(done, 1)

            @block.vector
            def _(dve):
                dve.sem_inc(added, 2)
                with dve.Fori(1, PAIRS + 1) as pair:
                    for i in range(2):
                        dve.wait_ge(done, pair * 2 + (i + 1))
                        xt = g.X[:, bass.ds(pair * 2 + (i - 2), 1), :].rearrange("p a t -> p (a t)")
                        nc.vector.tensor_tensor(xt, xt, turned[i][:], ALU.add).then_inc(added, 1)

    run_phase(nc, name, body)


def delta_rule_phase(nc, g, name, w):
    PAIRS, CHUNK, LEVELS = SEQS // 2, 64, 6
    CHUNKS = TOKENS // CHUNK

    def body(ph):
        wwrite = ph.sb("wwrite", [P, P])
        wwrite_t = ph.sb("wwrite_t", [P, P])
        wout = ph.sb("wout", [P, P])
        wout_t = ph.sb("wout_t", [P, P])
        wgates = ph.sb("wgates", [P, 3])
        dt_bias = ph.sb("dt_bias", [P, 1])
        a_log = ph.sb("a_log", [P, 1])
        rate = ph.sb("rate", [P, 1])
        until = ph.sb("until", [P, P])
        within = ph.sb("within", [P, P])
        ends = ph.sb("ends", [P, 2])
        ceiling = ph.sb("ceiling", [P, P])
        corner = ph.sb("corner", [P, LEVELS, P])
        big = {n: ph.sb(n, [P, 2, TOKENS]) for n in (
            "xs", "xt", "rk", "wk", "wkb", "vb", "rkd", "wkbd", "wkdw", "wkb_t", "rkd_t", "decayed", "m_t", "attn_t",
            "t1", "inv", "inv_t", "vp", "wkcd_t", "v_new", "o_t", "y")}
        off_t = ph.sb("off_t", [P, 2, LEVELS, TOKENS])
        keys_t = ph.sb("keys_t", [P, 2, TOKENS + 1])
        state = ph.sb("state", [P, 2, P])
        sm = {n: ph.sb(n, [P, 2, TILES]) for n in ("norm2", "norm2c", "inv_norm", "u", "abs_u", "e_u", "ln_u", "sp", "decay", "dec", "to_end", "e_dec", "e_to_end")}
        e_gates = ph.sb("e_gates", [P, 2, TILES, 2])
        e_gates1 = ph.sb("e_gates1", [P, 2, TILES, 2])
        gates = ph.sb("gates", [P, 2, TILES, 2])
        carry = ph.sb("carry", [P, 2, CHUNKS])
        bank = [[ph.ps(f"bank{i}{k}", [P, TOKENS]) for k in range(4)] for i in range(2)]

        pe_made = ["x_turned", "z_done", "v_done", "rk_turned", "decs_done", "dec_rows_done", "wk_turned", "wkb_turned", "rkd_turned",
                   "gram_done", "attn_done", "t1_done", "u_done", "ut_done", "vp_done", "wkcd_done", "vs_done", "update_done", "o_done", "out_done"]
        act_made = ["xs_ready", "xt_ready", "e_gates_ready", "abs_ready", "e_u_ready", "ln_ready", "rk_t_ready", "dec_ready", "e_dec_ready", "carry_ready",
                    "e_to_end_ready", "decayed_ready", "wk_ready", "wkb_t_ready", "rkd_t_ready", "t1_ready", "vp_ready", "wkcd_ready", "o_ready"]
        dve_made = ["squares_ready", "norm2_ready", "norm2c_ready", "rk_ready", "e_gates1_ready", "gates_ready", "u_ready", "sp_ready", "sp_sum_ready", "decay_ready",
                    "to_end_ready", "floor_ready", "wkb_ready", "vb_ready", "m_ready", "attn_ready", "inv_ready", "inv_t_ready",
                    "v_new_ready", "state_ready", "y_ready", "x_added"]
        pool_made = ["inv_norm_ready", "rkd_ready", "wkbd_ready", "wkdw_ready", "off_ready"]
        count = {k: 1 for k in pe_made + act_made + dve_made + pool_made}
        count.update(t1_done=LEVELS, t1_ready=LEVELS - 1, u_done=LEVELS - 2, ut_done=LEVELS - 1, inv_ready=LEVELS, inv_t_ready=LEVELS, off_ready=LEVELS,
                     vs_done=CHUNKS, update_done=CHUNKS, v_new_ready=CHUNKS, state_ready=CHUNKS + 1)
        q = {k: [ph.sem(f"{k}{i}") for i in range(2)] for k in ("t1_done", "t1_ready", "u_done", "ut_done", "inv_ready", "inv_t_ready", "off_ready",
                                                                 "vs_done", "update_done", "v_new_ready", "state_ready")}
        q.update({k: ph.sem(k) for k in count if k not in q})
        loaded, weights_turned, weights_ready, rate_ready, pads_ready, wait_taken = (
            ph.sem(k) for k in ("loaded", "weights_turned", "weights_ready", "rate_ready", "pads_ready", "wait_taken"))
        LOADS = 16 * 12

        def credit(eng, made):
            for k in made:
                if isinstance(q[k], list):
                    for one in q[k]:
                        eng.sem_inc(one, count[k])
                else:
                    eng.sem_inc(q[k], 2)

        def wait(eng, pair, key, i, k=1):
            if isinstance(q[key], list):
                eng.wait_ge(q[key][i], pair * count[key] + k)
            else:
                eng.wait_ge(q[key], pair * 2 + (i + 1))

        def done(ins, key, i):
            ins.then_inc(q[key][i] if isinstance(q[key], list) else q[key], 1)

        def tiled(buf, i):
            return buf[:, i].rearrange("p (t d) -> p t d", d=P)

        def banked(i, k):
            return bank[i][k][:].rearrange("p (t d) -> p t d", d=P)

        def spread(col):
            return col.unsqueeze(2).to_broadcast([P, TILES, P])

        def every(table):
            return table.unsqueeze(1).to_broadcast([P, TILES, P])

        def seq_of(buf, pair, i, c0=0, c1=TOKENS):
            return buf[:, bass.ds(pair * 2 + (i - 2), 1), c0:c1].rearrange("p a t -> p (a t)")

        cols = [slice(t * P, (t + 1) * P) for t in range(TILES)]

        with nc.Block() as block:

            @block.sync
            def _(sp):
                for dst, src in ((wwrite[:], w["W_write"]), (wout[:], w["W_out"]), (wgates[:, 0:1], w["W_gate"].rearrange("a d -> d a")),
                                 (wgates[:, 1:2], w["W_beta"].rearrange("a d -> d a")), (wgates[:, 2:3], w["W_alpha"].rearrange("a d -> d a")),
                                 (dt_bias[:], w["dt_bias"].partition_broadcast(P)), (a_log[:], w["A_log"].partition_broadcast(P)),
                                 (until[:], w["until"]), (within[:], w["within"]), (ends[:], w["ends"]), (ceiling[:], w["ceiling"]),
                                 (corner[:], w["corner"])):
                    sp.dma_start(dst, src).then_inc(loaded, 16)

            @block.tensor
            def _(pe):
                credit(pe, pe_made)
                pe.wait_ge(loaded, LOADS)
                nc.tensor.transpose(bank[0][0][:, 0:P], wwrite[:], g.ident[:])
                nc.tensor.transpose(bank[0][0][:, P:2 * P], wout[:], g.ident[:]).then_inc(weights_turned, 1)
                pe.wait_ge(weights_ready, 1)
                pe.wait_ge(pads_ready, 1)
                with pe.Fori(1, PAIRS + 1) as pair:

                    def products(i, k, lhs, rhs, key):
                        for t in range(TILES):
                            last = nc.tensor.matmul(bank[i][k][:, cols[t]], lhs(t), rhs(t), start=True, stop=True)
                        done(last, key, i)

                    def turns(i, k, src, key):
                        for t in range(TILES):
                            last = nc.tensor.transpose(bank[i][k][:, cols[t]], src(t), g.ident[:])
                        done(last, key, i)

                    for i in range(2):
                        wait(pe, pair, "xs_ready", i)
                        wait(pe, pair - 1, "x_added", i)
                        turns(i, 0, lambda t: big["xs"][:, i, cols[t]], "x_turned")
                        for t in range(TILES):
                            last = nc.tensor.matmul(bank[i][1][:, 3 * t:3 * t + 3], big["xs"][:, i, cols[t]], wgates[:], start=True, stop=True)
                        done(last, "z_done", i)
                        products(i, 2, lambda t: big["xs"][:, i, cols[t]], lambda t: wwrite_t[:], "v_done")
                    for i in range(2):
                        wait(pe, pair, "rk_ready", i)
                        turns(i, 3, lambda t: big["rk"][:, i, cols[t]], "rk_turned")
                    for i in range(2):
                        wait(pe, pair, "decay_ready", i)
                        nc.tensor.matmul(bank[i][1][:, 16:20], until[:], sm["decay"][:, i], start=True, stop=True)
                        nc.tensor.matmul(bank[i][1][:, 20:24], within[:], sm["decay"][:, i], start=True, stop=True)
                        for t in range(TILES):
                            last = nc.tensor.matmul(bank[i][1][:, 24 + 2 * t:26 + 2 * t], sm["decay"][:, i, t:t + 1].to_broadcast([P, P]), ends[:],
                                                    start=True, stop=True)
                        done(last, "decs_done", i)
                        wait(pe, pair, "xt_ready", i)
                        products(i, 0, lambda t: sm["decay"][:, i, t:t + 1].to_broadcast([P, P]), lambda t: until[:], "dec_rows_done")
                    for i in range(2):
                        wait(pe, pair, "rk_t_ready", i)
                        turns(i, 3, lambda t: keys_t[:, i, t * P:(t + 1) * P], "wk_turned")
                    for i in range(2):
                        wait(pe, pair, "rkd_ready", i)
                        wait(pe, pair, "vb_ready", i)
                        turns(i, 2, lambda t: big["rkd"][:, i, cols[t]], "rkd_turned")
                        wait(pe, pair, "wkb_ready", i)
                        wait(pe, pair, "e_to_end_ready", i)
                        wait(pe, pair, "carry_ready", i)
                        turns(i, 1, lambda t: big["wkb"][:, i, cols[t]], "wkb_turned")
                    for i in range(2):
                        wait(pe, pair, "floor_ready", i)
                        products(i, 0, lambda t: keys_t[:, i, t * P:(t + 1) * P], lambda t: keys_t[:, i, t * P + 1:(t + 1) * P + 1], "attn_done")
                        wait(pe, pair, "wkb_t_ready", i)
                        products(i, 3, lambda t: keys_t[:, i, t * P:(t + 1) * P], lambda t: big["wkb_t"][:, i, cols[t]], "gram_done")
                    for level in range(LEVELS):
                        for i in range(2):
                            wait(pe, pair, "off_ready", i, level + 1)
                            if level == 0:
                                wait(pe, pair, "attn_ready", i)
                                wait(pe, pair, "m_ready", i)
                                products(i, 0, lambda t: off_t[:, i, 0, cols[t]], lambda t: g.ident[:], "t1_done")
                                continue
                            wait(pe, pair, "inv_ready", i, level)
                            products(i, 0, lambda t: off_t[:, i, level, cols[t]], lambda t: big["inv"][:, i, cols[t]], "t1_done")
                        if level == 0:
                            continue
                        for i in range(2):
                            wait(pe, pair, "t1_ready", i, level)
                            wait(pe, pair, "inv_t_ready", i, level)
                            if level < LEVELS - 1:
                                products(i, 1, lambda t: big["inv_t"][:, i, cols[t]], lambda t: big["t1"][:, i, cols[t]], "u_done")
                            if level == 1:
                                wait(pe, pair, "rkd_t_ready", i)
                            products(i, 2, lambda t: big["t1"][:, i, cols[t]], lambda t: big["inv_t"][:, i, cols[t]], "ut_done")
                    for i in range(2):
                        wait(pe, pair, "inv_t_ready", i, LEVELS)
                        products(i, 0, lambda t: big["inv_t"][:, i, cols[t]], lambda t: big["vb"][:, i, cols[t]], "vp_done")
                        wait(pe, pair, "wkbd_ready", i)
                        products(i, 1, lambda t: big["wkbd"][:, i, cols[t]], lambda t: big["inv_t"][:, i, cols[t]], "wkcd_done")
                    for c in range(CHUNKS):
                        t, rows, own = c // 2, slice(CHUNK * (c % 2), CHUNK * (c % 2) + CHUNK), slice(c * CHUNK, (c + 1) * CHUNK)
                        for i in range(2):
                            if c == 0:
                                wait(pe, pair, "wkcd_ready", i)
                                wait(pe, pair, "vp_ready", i)
                            wait(pe, pair, "state_ready", i, c + 1)
                            done(nc.tensor.matmul(bank[i][2][rows, 0:P], big["wkcd_t"][:, i, own], state[:, i], start=True, stop=True), "vs_done", i)
                            nc.tensor.matmul(bank[i][3][:, own], state[:, i], big["rkd_t"][:, i, own], start=True, stop=False)
                        for i in range(2):
                            wait(pe, pair, "v_new_ready", i, c + 1)
                            if c == 0:
                                wait(pe, pair, "wkdw_ready", i)
                            last = nc.tensor.matmul(bank[i][3][:, own], big["v_new"][rows, i, cols[t]], big["attn_t"][rows, i, own], start=False, stop=True)
                            if c == CHUNKS - 1:
                                done(last, "o_done", i)
                            done(nc.tensor.matmul(bank[i][0][:, 0:P], big["wkdw"][rows, i, cols[t]], big["v_new"][rows, i, cols[t]], start=True, stop=True), "update_done", i)
                    for i in range(2):
                        wait(pe, pair, "o_ready", i)
                        products(i, 1, lambda t: big["o_t"][:, i, cols[t]], lambda t: wout_t[:], "out_done")

            @block.scalar
            def _(act):
                credit(act, act_made)
                act.wait_ge(loaded, LOADS)
                nc.scalar.activation(rate[:], a_log[:], ACT.Exp).then_inc(rate_ready, 1)
                act.wait_ge(weights_turned, 1)
                nc.scalar.copy(wwrite_t[:], bank[0][0][:, 0:P])
                nc.scalar.copy(wout_t[:], bank[0][0][:, P:2 * P]).then_inc(weights_ready, 1)
                with act.Fori(1, PAIRS + 1) as pair:

                    def copy(i, k, dst, key, done_key):
                        wait(act, pair, done_key, i)
                        done(nc.scalar.copy(dst, bank[i][k][:]), key, i)

                    for i in range(2):
                        wait(act, pair - 1, "out_done", i)
                        done(nc.scalar.copy(big["xs"][:, i], seq_of(g.XH, pair, i)), "xs_ready", i)
                    for i in range(2):
                        wait(act, pair - 1, "x_added", i)
                        copy(i, 0, big["xt"][:, i], "xt_ready", "x_turned")
                        z = bank[i][1][:, 0:12].rearrange("p (t k) -> p t k", k=3)
                        wait(act, pair, "z_done", i)
                        done(nc.scalar.activation(e_gates[:, i], z[:, :, 0:2], ACT.Exp, scale=-1.0), "e_gates_ready", i)
                    for i in range(2):
                        wait(act, pair, "u_ready", i)
                        done(nc.scalar.activation(sm["abs_u"][:, i], sm["u"][:, i], ACT.Abs), "abs_ready", i)
                        wait(act, pair, "abs_ready", i)
                        done(nc.scalar.activation(sm["e_u"][:, i], sm["abs_u"][:, i], ACT.Exp, scale=-1.0), "e_u_ready", i)
                        wait(act, pair, "e_u_ready", i)
                        done(nc.scalar.activation(sm["ln_u"][:, i], sm["e_u"][:, i], ACT.Ln, bias=1.0), "ln_ready", i)
                    for i in range(2):
                        copy(i, 3, keys_t[:, i, 1:TOKENS + 1], "rk_t_ready", "rk_turned")
                    for i in range(2):
                        wait(act, pair, "decs_done", i)
                        done(nc.scalar.copy(sm["dec"][:, i], bank[i][1][:, 16:20]), "dec_ready", i)
                        done(nc.scalar.activation(sm["e_dec"][:, i], bank[i][1][:, 16:20], ACT.Exp), "e_dec_ready", i)
                        done(nc.scalar.activation(carry[:, i], bank[i][1][:, 24:32], ACT.Exp), "carry_ready", i)
                        wait(act, pair, "to_end_ready", i)
                        done(nc.scalar.activation(sm["e_to_end"][:, i], sm["to_end"][:, i], ACT.Exp), "e_to_end_ready", i)
                    for i in range(2):
                        wait(act, pair, "floor_ready", i)
                        done(nc.scalar.activation(big["decayed"][:, i], big["decayed"][:, i], ACT.Exp), "decayed_ready", i)
                        copy(i, 3, big["wk"][:, i], "wk_ready", "wk_turned")
                    for i in range(2):
                        copy(i, 2, big["rkd_t"][:, i], "rkd_t_ready", "rkd_turned")
                        copy(i, 1, big["wkb_t"][:, i], "wkb_t_ready", "wkb_turned")
                    for level in range(1, LEVELS):
                        for i in range(2):
                            wait(act, pair, "t1_done", i, level + 1)
                            done(nc.scalar.copy(big["t1"][:, i], bank[i][0][:]), "t1_ready", i)
                    for i in range(2):
                        copy(i, 0, big["vp"][:, i], "vp_ready", "vp_done")
                        copy(i, 1, big["wkcd_t"][:, i], "wkcd_ready", "wkcd_done")
                    for i in range(2):
                        copy(i, 3, big["o_t"][:, i], "o_ready", "o_done")

            @block.gpsimd
            def _(pool):
                credit(pool, pool_made)
                pool.wait_ge(loaded, LOADS)
                with pool.Fori(1, PAIRS + 1) as pair:
                    for i in range(2):
                        wait(pool, pair, "norm2c_ready", i)
                        done(nc.gpsimd.tensor_tensor(sm["inv_norm"][:, i], sm["norm2c"][:, i], g.minus_half[:, 0:TILES], ALU.pow), "inv_norm_ready", i)
                    for i in range(2):
                        wait(pool, pair, "rk_ready", i)
                        wait(pool, pair, "e_dec_ready", i)
                        done(nc.gpsimd.tensor_tensor(tiled(big["rkd"], i), tiled(big["rk"], i), spread(sm["e_dec"][:, i]), ALU.mult), "rkd_ready", i)
                    for level in range(LEVELS):
                        for i in range(2):
                            wait(pool, pair, "m_ready", i)
                            done(nc.gpsimd.tensor_tensor(off_t[:, i, level].rearrange("p (t d) -> p t d", d=P), tiled(big["m_t"], i), every(corner[:, level]), ALU.mult), "off_ready", i)
                    for i in range(2):
                        wait(pool, pair, "wkb_ready", i)
                        done(nc.gpsimd.tensor_tensor(tiled(big["wkbd"], i), tiled(big["wkb"], i), spread(sm["e_dec"][:, i]), ALU.mult), "wkbd_ready", i)
                        wait(pool, pair, "wk_ready", i)
                        wait(pool, pair, "e_to_end_ready", i)
                        done(nc.gpsimd.tensor_tensor(tiled(big["wkdw"], i), tiled(big["wk"], i), spread(sm["e_to_end"][:, i]), ALU.mult), "wkdw_ready", i)

            @block.vector
            def _(dve):
                nc.vector.memset(keys_t[:], 0.0).then_inc(pads_ready, 1)
                credit(dve, dve_made)
                dve.wait_ge(loaded, LOADS)
                dve.wait_ge(rate_ready, 1)
                with dve.Fori(1, PAIRS + 1) as pair:
                    for i in range(2):
                        wait(dve, pair, "xt_ready", i)
                        done(nc.vector.tensor_tensor(big["y"][:, i], big["xt"][:, i], big["xt"][:, i], ALU.mult), "squares_ready", i)
                        wait(dve, pair, "squares_ready", i)
                        done(nc.vector.tensor_reduce(sm["norm2"][:, i], tiled(big["y"], i), AX, ALU.add), "norm2_ready", i)
                        wait(dve, pair, "norm2_ready", i)
                        done(nc.vector.tensor_scalar(sm["norm2c"][:, i], sm["norm2"][:, i], 1e-24, None, ALU.max), "norm2c_ready", i)
                    for i in range(2):
                        z = bank[i][1][:, 0:12].rearrange("p (t k) -> p t k", k=3)
                        wait(dve, pair, "z_done", i)
                        wait(dve, pair, "e_gates_ready", i)
                        done(nc.vector.tensor_scalar(sm["u"][:, i], z[:, :, 2], dt_bias[:], None, ALU.add), "u_ready", i)
                        done(nc.vector.tensor_scalar(e_gates1[:, i], e_gates[:, i], 1.0, None, ALU.add), "e_gates1_ready", i)
                        wait(dve, pair, "e_gates1_ready", i)
                        done(nc.vector.reciprocal(gates[:, i], e_gates1[:, i]), "gates_ready", i)
                    for i in range(2):
                        wait(dve, pair, "inv_norm_ready", i)
                        done(nc.vector.tensor_tensor(tiled(big["rk"], i), tiled(big["xt"], i), spread(sm["inv_norm"][:, i]), ALU.mult), "rk_ready", i)
                    for i in range(2):
                        wait(dve, pair, "ln_ready", i)
                        done(nc.vector.scalar_tensor_tensor(sm["sp"][:, i], sm["u"][:, i], 0.0, sm["ln_u"][:, i], ALU.max, ALU.add), "sp_ready", i)
                        wait(dve, pair, "sp_ready", i)
                        done(nc.vector.tensor_scalar(sm["decay"][:, i], sm["sp"][:, i], rate[:], -1.0, ALU.mult, ALU.mult), "decay_ready", i)
                    for i in range(2):
                        wait(dve, pair, "v_done", i)
                        wait(dve, pair, "gates_ready", i)
                        done(nc.vector.tensor_tensor(tiled(big["vb"], i), banked(i, 2), spread(gates[:, i, :, 1]), ALU.mult), "vb_ready", i)
                    for i in range(2):
                        wait(dve, pair, "carry_ready", i)
                        done(nc.vector.tensor_tensor(sm["to_end"][:, i], bank[i][1][:, 20:24], sm["dec"][:, i], ALU.subtract), "to_end_ready", i)
                        wait(dve, pair, "dec_rows_done", i)
                        for t in range(TILES):
                            last = nc.vector.scalar_tensor_tensor(big["decayed"][:, i, cols[t]], bank[i][0][:, cols[t]], sm["dec"][:, i, t:t + 1], ceiling[:],
                                                                  ALU.subtract, ALU.min)
                        done(last, "floor_ready", i)
                    for i in range(2):
                        wait(dve, pair, "wk_ready", i)
                        done(nc.vector.tensor_tensor(tiled(big["wkb"], i), tiled(big["wk"], i), spread(gates[:, i, :, 1]), ALU.mult), "wkb_ready", i)
                    for i in range(2):
                        wait(dve, pair, "decayed_ready", i)
                        wait(dve, pair, "attn_done", i)
                        done(nc.vector.tensor_tensor(big["attn_t"][:, i], bank[i][0][:], big["decayed"][:, i], ALU.mult), "attn_ready", i)
                        wait(dve, pair, "gram_done", i)
                        done(nc.vector.tensor_tensor(big["m_t"][:, i], bank[i][3][:], big["decayed"][:, i], ALU.mult), "m_ready", i)
                    for level in range(LEVELS):
                        for i in range(2):
                            if level == 0:
                                wait(dve, pair, "off_ready", i, 1)
                                done(nc.vector.tensor_tensor(tiled(big["inv_t"], i), every(g.ident[:]), off_t[:, i, 0].rearrange("p (t d) -> p t d", d=P), ALU.subtract), "inv_t_ready", i)
                                wait(dve, pair, "t1_done", i, 1)
                                done(nc.vector.tensor_tensor(tiled(big["inv"], i), every(g.ident[:]), banked(i, 0), ALU.subtract), "inv_ready", i)
                                continue
                            if level < LEVELS - 1:
                                wait(dve, pair, "u_done", i, level)
                                wait(dve, pair, "inv_ready", i, level)
                                done(nc.vector.tensor_tensor(big["inv"][:, i], big["inv"][:, i], bank[i][1][:], ALU.subtract), "inv_ready", i)
                            wait(dve, pair, "ut_done", i, level)
                            wait(dve, pair, "inv_t_ready", i, level)
                            done(nc.vector.tensor_tensor(big["inv_t"][:, i], big["inv_t"][:, i], bank[i][2][:], ALU.subtract), "inv_t_ready", i)
                    for i in range(2):
                        done(nc.vector.memset(state[:, i], 0.0), "state_ready", i)
                        dve.sem_inc(q["inv_ready"][i], 1)
                    for c in range(CHUNKS):
                        t, rows = c // 2, slice(CHUNK * (c % 2), CHUNK * (c % 2) + CHUNK)
                        for i in range(2):
                            if c == 0:
                                wait(dve, pair, "vp_ready", i)
                            wait(dve, pair, "vs_done", i, c + 1)
                            done(nc.vector.tensor_tensor(big["v_new"][rows, i, cols[t]], big["vp"][rows, i, cols[t]], bank[i][2][rows, 0:P], ALU.subtract), "v_new_ready", i)
                        for i in range(2):
                            wait(dve, pair, "update_done", i, c + 1)
                            wait(dve, pair, "state_ready", i, c + 1)
                            done(nc.vector.scalar_tensor_tensor(state[:, i], state[:, i], carry[:, i, c:c + 1], bank[i][0][:, 0:P], ALU.mult, ALU.add), "state_ready", i)
                    for i in range(2):
                        wait(dve, pair, "out_done", i)
                        for t in range(TILES):
                            last = nc.vector.scalar_tensor_tensor(big["y"][:, i, cols[t]], bank[i][1][:, cols[t]], gates[:, i, t, 0:1], big["xt"][:, i, cols[t]], ALU.mult, ALU.add)
                        done(last, "y_ready", i)
                        wait(dve, pair, "y_ready", i)
                        xt = seq_of(g.X, pair, i)
                        done(nc.vector.tensor_tensor(xt, xt, big["y"][:, i], ALU.add), "x_added", i)

    run_phase(nc, name, body)


class Kept:

    def __init__(self, nc, ctx):
        def sb(name, shape):
            return ctx.enter_context(nc.sbuf_tensor(name, shape, F32))

        self.X = sb("X", [P, SEQS, TOKENS])
        self.XH = sb("XH", [P, SEQS, TOKENS])
        self.ident = sb("ident", [P, P])
        self.minus_half = sb("minus_half", [P, 64])
        self.rank8 = sb("rank8", [P, 8])


def load_phase(nc, g, x, a):
    def body(ph):
        loaded = ph.sem("loaded")
        with nc.Block() as block:

            @block.sync
            def _(sp):
                sp.dma_start(g.X[:].rearrange("p s (t d) -> p (s t) d", d=P), x.rearrange("s (t p) d -> p (s t) d", p=P)).then_inc(loaded, 16)
                sp.dma_start(g.ident[:], a["ident"]).then_inc(loaded, 16)
                sp.dma_start(g.rank8[:], a["rank8"]).then_inc(loaded, 16)
                sp.wait_ge(loaded, 16 * 3)

            @block.vector
            def _(dve):
                nc.vector.memset(g.minus_half[:], -0.5)

    run_phase(nc, "load", body)


def store_phase(nc, g, out):
    def body(ph):
        stored = ph.sem("stored")
        with nc.Block() as block:

            @block.sync
            def _(sp):
                sp.dma_start(out.rearrange("s (t p) d -> p (s t) d", p=P), g.X[:].rearrange("p s (t d) -> p (s t) d", d=P)).then_inc(stored, 16)
                sp.wait_ge(stored, 16)

    run_phase(nc, "store", body)


def build_program(nc, a, out):
    def of(layer, *names):
        return {n: a[f"{layer}_{n}"] for n in names}

    with ExitStack() as ctx:
        g = Kept(nc, ctx)
        load_phase(nc, g, a["L0_attn_x"], a)

        layernorm_pass(nc, g, "norm0")
        delta_rule_phase(nc, g, "delta", of("L0_attn", "W_write", "W_gate", "W_out", "W_beta", "W_alpha", "dt_bias", "A_log")
                         | {n: a[n] for n in ("until", "within", "ends", "ceiling", "corner")})

        layernorm_pass(nc, g, "norm1")
        local_transformer_phase(nc, g, "local", of("L0_ffn", "Wqkv", "q_scale", "k_scale", "Wo", "ln_g", "ln_b", "W1", "b1", "W2", "b2")
                                | {n: a[n] for n in ("rotary", "band")})
        add_back_phase(nc, g, "back")

        layernorm_pass(nc, g, "norm2")
        l1 = of("L1_attn", "wq", "wk", "wv", "wo")
        softmax_attention_phase(nc, g, "causal", {
            "wq": l1["wq"].rearrange("m h d -> m (h d)"), "wk": l1["wk"].rearrange("m h d -> m (h d)"), "wv": l1["wv"].rearrange("m h d -> m (h d)"),
            "wo": l1["wo"].rearrange("h d m -> (h d) m"), "cos": a["rope_cos"], "sin": a["rope_sin"], "mask": a["never_later"]}, causal_only=True)

        layernorm_pass(nc, g, "norm3")
        moe_phase(nc, g, "moe1", {"wg": a["L1_ffn_Wg"], "wg_t": None, "bg": a["L1_ffn_bg"], "w1": a["L1_ffn_W1"], "b1": a["L1_ffn_b1"],
                                  "w2": a["L1_ffn_W2"], "b2": a["L1_ffn_b2"]}, ACT.Gelu_apprx_tanh, top2=True)

        layernorm_pass(nc, g, "norm4")
        chunk_attention_phase(nc, g, "chunked", of("L2_attn", "Wqk", "bqk", "Wv", "bv", "gamma", "beta", "rel_emb")
                              | {n: a[n] for n in ("bucket", "chunk_mask")})

        layernorm_pass(nc, g, "norm5")
        moe_phase(nc, g, "moe2", {"wg": a["L2_ffn_router_w"], "wg_t": None, "bg": a["L2_ffn_router_b"], "w1": a["L2_ffn_W1"], "b1": a["L2_ffn_b1"],
                                  "w2": a["L2_ffn_W2"], "b2": a["L2_ffn_b2"]}, ACT.Gelu, top2=False)

        layernorm_pass(nc, g, "norm6")
        softmax_attention_phase(nc, g, "relu", {n.lower(): ap for n, ap in of("L3_attn", "Wq", "Wk", "Wv", "Wo", "bq", "bk", "bv", "bo").items()}
                                | {"mask": a["less_later"]}, causal_only=False)

        layernorm_pass(nc, g, "norm7")
        moe_phase(nc, g, "moe3", {"wg": None, "wg_t": a["L3_ffn_Wg"], "bg": None, "w1": a["L3_ffn_W1"], "b1": a["L3_ffn_b1"],
                                  "w2": a["L3_ffn_W2"], "b2": a["L3_ffn_b2"]}, ACT.Gelu, top2=False)

        store_phase(nc, g, out)


def shape_constants():
    f = np.float32
    c = {"ident": np.eye(P, dtype=f), "rank8": np.tile(np.arange(8, 0, -1, dtype=f), (P, 1))}

    j, i = np.arange(P)[:, None], np.arange(P)[None]
    same = j // 64 == i // 64
    c["until"] = (same & (j <= i)).astype(f)
    c["within"] = same.astype(f)
    c["ends"] = (j // 64 == np.arange(2)[None]).astype(f)
    c["ceiling"] = np.where(same & (j <= i), f(-NEVER), f(NEVER))
    c["corner"] = np.stack([((i >> b) % 2 == 1) & (j >> b == (i >> b) - 1) for b in range(6)], 1).astype(f)
    c["chunk_mask"] = np.where(same & (i <= j), f(0), f(NEVER))

    half = np.arange(0, 64, 2, dtype=f)
    angle = np.arange(TOKENS, dtype=f)[:, None] * (f(1) / f(10000) ** (half / f(64)))[None]
    scale = ((half + f(25.6)) / f(89.6))[None] ** ((np.arange(TOKENS, dtype=f) - f(256)) / f(16))[:, None]
    angle, scale = np.tile(angle, 2).astype(np.float64), np.tile(scale, 2)
    cos, sin = np.cos(angle), np.sin(angle) * np.where(np.arange(64) < 32, -1, 1)
    rotary = np.stack([cos * scale * 8, sin * scale * 8, cos / scale, sin / scale], 1).astype(f)
    c["rotary"] = rotary.reshape(TILES, P, 4, 64).transpose(1, 0, 2, 3)
    r, k = np.arange(P)[:, None], np.arange(96)[None]
    near = (k >= r % 64) & (k <= r % 64 + 32)
    c["band"] = np.stack([np.where(near & ((r >= 64) | (k >= 32)), 0, NEVER), np.where(near, 0, NEVER)], 1).astype(f)

    angle = np.arange(TOKENS, dtype=f)[:, None] * (f(10000) ** (-(np.arange(32) / 32)).astype(f))[None]
    cos, sin = np.cos(angle.astype(np.float64)).T, np.sin(angle.astype(np.float64)).T
    root = P ** -0.5
    c["rope_cos"] = (np.concatenate([cos, cos, np.ones((64, TOKENS))]) * root).astype(f)
    c["rope_sin"] = (np.concatenate([sin, sin]) * root).astype(f)
    later = np.arange(7 * P)[None] - 3 * P > np.arange(P)[:, None]
    c["never_later"] = np.where(later, f(-1e30), f(0))
    c["less_later"] = np.where(later, f(-1e4), f(0))

    n = np.arange(64)
    large = 16 + np.log(np.maximum(n, 1).astype(f) / 16) / math.log(8) * 16
    bucket = np.where(n < 16, n, np.minimum(large, 31)).astype(np.int32)
    c["bucket"] = np.zeros((32, 2 * P - 1), f)
    c["bucket"][bucket, P - 1 - n] = 1
    return {name: np.ascontiguousarray(table) for name, table in c.items()}


def kernel(**inputs):
    import concourse.bacc as bacc
    from concourse.bass_utils import run_bass_kernel_spmd

    nc = bacc.Bacc("TRN2", target_bir_lowering=False, num_devices=1)
    arrays, aps = {}, {}
    for name, array in [*inputs.items(), *shape_constants().items()]:
        array = np.ascontiguousarray(array)
        arrays[f"in_{name}"] = array
        aps[name] = nc.dram_tensor(f"in_{name}", array.shape, mybir.dt.from_np(array.dtype), kind="ExternalInput").ap()
    out = nc.dram_tensor("out_x", (SEQS, TOKENS, P), F32, kind="ExternalOutput").ap()
    build_program(nc, aps, out)
    return run_bass_kernel_spmd(nc, [arrays], core_ids=[0]).results[0]["out_x"]
```

```python
import math

import numpy as np

import concourse.bass as bass
from concourse import mybir
from contextlib import ExitStack

F32 = mybir.dt.float32
F32R = mybir.dt.float32r
ALU = mybir.AluOpType
ACT = mybir.ActivationFunctionType
AX = mybir.AxisListType.X

P = 128
SEQS = 8
TOKENS = 512
TILES = TOKENS // P
LN_EPS = 1e-5
NEVER = -3.0e38


class Phase:

    def __init__(self, nc, name, ctx):
        self.nc, self.name, self.ctx = nc, name, ctx
        self.sems = []

    def sb(self, name, shape, dtype=F32):
        return self.ctx.enter_context(self.nc.sbuf_tensor(f"{self.name}_{name}", shape, dtype))

    def ps(self, name, shape, dtype=F32):
        return self.ctx.enter_context(self.nc.psum_tensor(f"{self.name}_{name}", shape, dtype))

    def sem(self, name):
        s = self.nc.alloc_semaphore(f"{self.name}_{name}")
        self.sems.append(s)
        return s


def run_phase(nc, name, body):
    with ExitStack() as ctx:
        ph = Phase(nc, name, ctx)
        body(ph)
    nc.clear_and_free_semaphores(ph.sems)
    nc.all_engine_barrier()


class Normaliser:

    def __init__(self, nc, ph, g, banks, x_hat=None):
        self.nc, self.g, self.turned = nc, g, banks
        self.x_hat = ph.sb("x_hat", [P, 2, TOKENS])[:] if x_hat is None else x_hat
        self.stats = ph.sb("ln_stats", [P, 2, TILES, 6])
        self.mean_var = ph.sb("ln_mean_var", [P, 2, TILES, 2])
        self.var_eps = ph.sb("ln_var_eps", [P, 2, TILES])
        self.rstd = ph.sb("ln_rstd", [P, 2, TILES])
        self.wait_taken, self.stats_ready, self.aggregated, self.var_ready, self.rstd_ready, self.x_hat_ready, self.turned_ready, self.xh_ready = (
            ph.sem(f"ln_{n}") for n in ("wait_taken", "stats_ready", "aggregated", "var_ready", "rstd_ready", "x_hat_ready", "turned_ready", "xh_ready"))

    @staticmethod
    def at(pair, i):
        return pair * 2 + (i - 1)

    def finished(self, eng):
        eng.wait_ge(self.xh_ready, SEQS + 2)

    def vector(self, dve):
        nc, g, at = self.nc, self.g, self.at
        with dve.Fori(1, SEQS // 2 + 1) as pair:
            def tile(i, t):
                return g.X[:, bass.ds(pair * 2 + (i - 2), 1), t * P:(t + 1) * P]

            for i in range(2):
                for t in range(TILES):
                    last = nc.vector.bn_stats(self.stats[:, i, t, :].unsqueeze(1), tile(i, t))
                last.then_inc(self.stats_ready, 1)
            for i in range(2):
                dve.wait_ge(self.stats_ready, at(pair, i))
                dve.sem_inc(self.wait_taken, 1)
                for t in range(TILES):
                    last = nc.vector.bn_aggr(self.mean_var[:, i, t, :], self.stats[:, i, t, :])
                last.then_inc(self.aggregated, 1)
                dve.wait_ge(self.aggregated, at(pair, i))
                nc.vector.tensor_scalar(self.var_eps[:, i], self.mean_var[:, i, :, 1], LN_EPS, None, ALU.add).then_inc(self.var_ready, 1)
            for i in range(2):
                dve.wait_ge(self.rstd_ready, at(pair, i))
                dve.wait_ge(self.turned_ready, at(pair, i))
                dve.sem_inc(self.wait_taken, 1)
                for t in range(TILES):
                    last = nc.vector.tensor_scalar(self.x_hat[:, i, t * P:(t + 1) * P].unsqueeze(1), tile(i, t),
                                                   self.mean_var[:, i, t, 0:1], self.rstd[:, i, t:t + 1], ALU.subtract, ALU.mult)
                last.then_inc(self.x_hat_ready, 1)
        self.finished(dve)

    def gpsimd(self, pool):
        nc, g, at = self.nc, self.g, self.at
        with pool.Fori(1, SEQS // 2 + 1) as pair:
            for i in range(2):
                pool.wait_ge(self.var_ready, at(pair, i))
                nc.gpsimd.tensor_tensor(self.rstd[:, i], self.var_eps[:, i], g.minus_half[:, 0:TILES], ALU.pow).then_inc(self.rstd_ready, 1)
        self.finished(pool)

    def tensor(self, pe):
        nc, g, at = self.nc, self.g, self.at
        pe.sem_inc(self.turned_ready, 2)
        with pe.Fori(1, SEQS // 2 + 1) as pair:
            for i in range(2):
                pe.wait_ge(self.x_hat_ready, at(pair, i))
                pe.wait_ge(self.xh_ready, at(pair, i))
                for t in range(TILES):
                    last = nc.tensor.transpose(self.turned[i][:, t * P:(t + 1) * P], self.x_hat[:, i, t * P:(t + 1) * P], g.ident[:])
                last.then_inc(self.turned_ready, 1)
        self.finished(pe)

    def scalar(self, act):
        nc, g, at = self.nc, self.g, self.at
        act.sem_inc(self.xh_ready, 2)
        with act.Fori(1, SEQS // 2 + 1) as pair:
            for i in range(2):
                act.wait_ge(self.turned_ready, at(pair, i) + 2)
                act.sem_inc(self.wait_taken, 1)
                nc.scalar.copy(g.XH[:, bass.ds(pair * 2 + (i - 2), 1), :], self.turned[i][:].unsqueeze(1)).then_inc(self.xh_ready, 1)
        self.finished(act)


def moe_phase(nc, g, name, w, gelu, top2):
    E, FC = 8, 4

    def body(ph):
        w1 = ph.sb("w1", [P, E, FC, P])
        w1_hi, w1_lo = (ph.sb(n, [P, E, FC, P], F32R) for n in ("w1_hi", "w1_lo"))
        xs_hi, xs_lo = (ph.sb(n, [P, TOKENS], F32R) for n in ("xs_hi", "xs_lo"))
        w2 = ph.sb("w2", [P, E, FC, P])
        b1 = ph.sb("b1", [P, E, FC])
        b2 = ph.sb("b2", [E, P])
        wg = ph.sb("wg", [P, E])
        wg_rows = ph.sb("wg_rows", [E, P])
        bg = ph.sb("bg", [P, E])
        xs = ph.sb("xs", [P, TOKENS])
        hid = ph.sb("hid", [P, 2, FC, TOKENS])
        score = ph.sb("score", [P, TILES, E])
        tmp = ph.sb("tmp", [P, TILES, E])
        tmp2 = ph.sb("tmp2", [P, TILES, E])
        pick = ph.sb("pick", [P, 2, TILES, E])
        combine = ph.sb("combine", [P, TILES, E])
        small = ph.sb("small", [P, 8, TILES])
        combine_t = ph.sb("combine_t", [E, TOKENS])
        acc = ph.sb("acc", [P, TOKENS])
        hid_ps = [ph.ps(f"hid_ps{i}", [P, TOKENS]) for i in range(4)]
        y_ps = [ph.ps(f"y_ps{i}", [P, TOKENS]) for i in range(2)]
        small_ps = ph.ps("small_ps", [P, TOKENS])
        bias_ps = ph.ps("bias_ps", [P, TOKENS])
        loaded = ph.sem("loaded")
        router_turned = ph.sem("router_turned")
        router_ready = ph.sem("router_ready")
        xs_ready = ph.sem("xs_ready")
        xs_hi_ready = ph.sem("xs_hi_ready")
        xs_lo_ready = ph.sem("xs_lo_ready")
        w1_hi_ready = ph.sem("w1_hi_ready")
        w1_split = ph.sem("w1_split")
        wait_taken = ph.sem("wait_taken")
        logits_ready = ph.sem("logits_ready")
        step = ph.sem("routing_step")
        probs_ready = ph.sem("probs_ready")
        combine_ready = ph.sem("combine_ready")
        combine_turned = ph.sem("combine_turned")
        combine_t_ready = ph.sem("combine_t_ready")
        bias_ready = ph.sem("bias_ready")
        hid_done = ph.sem("hid_done")
        gelu_done = ph.sem("gelu_done")
        y_done = ph.sem("y_done")
        y_added = ph.sem("y_added")
        acc_started = ph.sem("acc_started")
        STEPS = 25 if top2 else 6
        has_gbias = w["bg"] is not None
        wg_by_expert = w["wg_t"] is not None
        LOADS = 16 * (4 + 1 + (1 if has_gbias else 0))

        norm = Normaliser(nc, ph, g, (small_ps, bias_ps))

        with nc.Block() as block:

            @block.sync
            def _(sp):
                if wg_by_expert:
                    sp.dma_start(wg_rows[:], w["wg_t"]).then_inc(loaded, 16)
                else:
                    sp.dma_start(wg[:], w["wg"]).then_inc(loaded, 16)
                sp.dma_start(w1[:].rearrange("p e b f -> p e (b f)"), w["w1"].rearrange("e d f -> d e f")).then_inc(loaded, 16)
                sp.dma_start(w2[:], w["w2"].rearrange("e (b f) d -> f e b d", f=P)).then_inc(loaded, 16)
                sp.dma_start(b1[:], w["b1"].rearrange("e (b f) -> f e b", f=P), allow_slow_non_contiguous=True).then_inc(loaded, 16)
                sp.dma_start(b2[:], w["b2"]).then_inc(loaded, 16)
                if has_gbias:
                    sp.dma_start(bg[:], w["bg"].partition_broadcast(P)).then_inc(loaded, 16)

            @block.scalar
            def _(act):
                norm.scalar(act)
                act.sem_inc(gelu_done, E * FC)
                act.wait_ge(loaded, LOADS)
                for e in range(E):
                    nc.scalar.copy(w1_hi[:, e], w1[:, e]).then_inc(w1_hi_ready, 1)
                with act.Fori(1, SEQS + 1) as s:
                    act.wait_ge(hid_done, s * (E * FC))
                    act.wait_ge(xs_lo_ready, s)
                    act.sem_inc(wait_taken, 1)
                    nc.scalar.copy(xs_hi[:], g.XH[:, bass.ds(s - 1, 1), :]).then_inc(xs_hi_ready, 1)
                    nc.scalar.copy(xs[:], g.XH[:, bass.ds(s - 1, 1), :]).then_inc(xs_ready, 1)
                    if top2:
                        act.wait_ge(step, s * STEPS + 3)
                        nc.scalar.activation(score[:], tmp[:], ACT.Exp).then_inc(probs_ready, 1)
                    for e in range(E):
                        for b in range(FC):
                            n = e * FC + b
                            act.wait_ge(hid_done, s * (E * FC) + (n + 1))
                            if b == 0:
                                act.wait_ge(y_done, s * E + (e - 1) if e >= 2 else (s - 1) * E + (e + E - 1))
                            nc.scalar.activation(hid[:, e % 2, b, :], hid_ps[n % 4][:], gelu, bias=b1[:, e, b:b + 1]).then_inc(gelu_done, 1)
                        if e == 1:
                            act.wait_ge(combine_turned, s)
                            nc.scalar.copy(combine_t[:], small_ps[0:E, :]).then_inc(combine_t_ready, 1)

            @block.tensor
            def _(pe):
                norm.tensor(pe)
                pe.sem_inc(hid_done, E * FC)
                pe.sem_inc(y_done, E)
                pe.wait_ge(loaded, LOADS)
                if wg_by_expert:
                    nc.tensor.transpose(small_ps[:, 0:E], wg_rows[:], g.ident[0:E, 0:E]).then_inc(router_turned, 1)
                    pe.wait_ge(router_ready, 1)
                with pe.Fori(1, SEQS + 1) as s:

                    def down(e):
                        pe.wait_ge(gelu_done, s * (E * FC) + FC * (e + 1))
                        pe.wait_ge(y_added, s * E + (e - 1) if e >= 2 else (s - 1) * E + (e + E - 1))
                        for t in range(TILES):
                            for b in range(FC):
                                last = nc.tensor.matmul(y_ps[e % 2][:, t * P:(t + 1) * P], hid[:, e % 2, b, t * P:(t + 1) * P],
                                                        w2[:, e, b, :], start=(b == 0), stop=(b == FC - 1))
                        last.then_inc(y_done, 1)

                    pe.wait_ge(xs_ready, s)
                    for t in range(TILES):
                        last = nc.tensor.matmul(small_ps[:, t * E:(t + 1) * E], xs[:, t * P:(t + 1) * P], wg[:], start=True, stop=True)
                    last.then_inc(logits_ready, 1)
                    pe.wait_ge(xs_lo_ready, s + 1)
                    for e in range(E):
                        pe.wait_ge(w1_split, e + 1)
                        for b in range(FC):
                            n = e * FC + b
                            pe.wait_ge(gelu_done, s * (E * FC) + (n - 3) if n >= 4 else (s - 1) * (E * FC) + (n + E * FC - 3))
                            nc.tensor.matmul(hid_ps[n % 4][:], w1_hi[:, e, b, :], xs_hi[:], start=True, stop=False)
                            nc.tensor.matmul(hid_ps[n % 4][:], w1_lo[:, e, b, :], xs_hi[:], start=False, stop=False)
                            nc.tensor.matmul(hid_ps[n % 4][:], w1_hi[:, e, b, :], xs_lo[:], start=False, stop=True).then_inc(hid_done, 1)
                        if e == 1:
                            pe.wait_ge(combine_ready, s)
                            for t in range(TILES):
                                last = nc.tensor.transpose(small_ps[0:E, t * P:(t + 1) * P], combine[:, t, :], g.ident[:])
                            last.then_inc(combine_turned, 1)
                        if e == 2:
                            pe.wait_ge(combine_t_ready, s)
                            for t in range(TILES):
                                last = nc.tensor.matmul(bias_ps[:, t * P:(t + 1) * P], combine_t[:, t * P:(t + 1) * P], b2[:], start=True, stop=True)
                            last.then_inc(bias_ready, 1)
                        if e >= 1:
                            down(e - 1)
                    down(E - 1)

            @block.gpsimd
            def _(pool):
                norm.gpsimd(pool)
                pool.sem_inc(xs_lo_ready, 1)
                with pool.Fori(1, SEQS + 1) as s:
                    pool.wait_ge(xs_hi_ready, s)
                    pool.sem_inc(wait_taken, 1)
                    nc.gpsimd.tensor_tensor(xs_lo[:], g.XH[:, bass.ds(s - 1, 1), :].rearrange("p a t -> p (a t)"), xs_hi[:].bitcast(F32),
                                            ALU.subtract).then_inc(xs_lo_ready, 1)

            @block.vector
            def _(dve):
                norm.vector(dve)
                dve.sem_inc(step, STEPS)
                dve.sem_inc(y_added, E)
                dve.wait_ge(loaded, LOADS)
                for e in range(E):
                    dve.wait_ge(w1_hi_ready, e + 1)
                    nc.vector.tensor_tensor(w1_lo[:, e], w1[:, e], w1_hi[:, e].bitcast(F32), ALU.subtract).then_inc(w1_split, 1)
                if wg_by_expert:
                    dve.wait_ge(router_turned, 1)
                    nc.vector.tensor_copy(wg[:], small_ps[:, 0:E]).then_inc(router_ready, 1)
                with dve.Fori(1, SEQS + 1) as s:
                    made = 0

                    def done(ins):
                        nonlocal made
                        made += 1
                        ins.then_inc(step, 1)
                        dve.wait_ge(step, s * STEPS + made)

                    def spread(row):
                        return small[:, row, :].unsqueeze(2).to_broadcast([P, TILES, E])

                    def first_of(src, row, onehot):
                        done(nc.vector.tensor_tensor(tmp[:], src, spread(row), ALU.is_equal))
                        done(nc.vector.tensor_tensor(tmp[:], tmp[:], g.rank8[:].unsqueeze(1).to_broadcast([P, TILES, E]), ALU.mult))
                        done(nc.vector.tensor_reduce(small[:, row + 2, :], tmp[:], AX, ALU.max))
                        done(nc.vector.tensor_tensor(onehot, tmp[:], spread(row + 2), ALU.is_equal))

                    dve.wait_ge(logits_ready, s)
                    logits = small_ps[:, 0:TILES * E].rearrange("p (t e) -> p t e", e=E)
                    if has_gbias:
                        done(nc.vector.tensor_tensor(score[:], logits, bg[:].unsqueeze(1).to_broadcast([P, TILES, E]), ALU.add))
                    else:
                        done(nc.vector.tensor_copy(score[:], logits))
                    done(nc.vector.tensor_reduce(small[:, 0, :], score[:], AX, ALU.max))
                    if top2:
                        done(nc.vector.tensor_tensor(tmp[:], score[:], spread(0), ALU.subtract))
                        dve.wait_ge(probs_ready, s)
                        done(nc.vector.tensor_reduce(small[:, 4, :], score[:], AX, ALU.add))
                        done(nc.vector.reciprocal(small[:, 5, :], small[:, 4, :]))
                        done(nc.vector.tensor_tensor(score[:], score[:], spread(5), ALU.mult))
                        done(nc.vector.tensor_reduce(small[:, 0, :], score[:], AX, ALU.max))
                        first_of(score[:], 0, pick[:, 0])
                        done(nc.vector.scalar_tensor_tensor(tmp2[:], pick[:, 0], -4.0, score[:], ALU.mult, ALU.add))
                        done(nc.vector.tensor_reduce(small[:, 1, :], tmp2[:], AX, ALU.max))
                        first_of(tmp2[:], 1, pick[:, 1])
                        done(nc.vector.tensor_tensor(small[:, 4, :], small[:, 0, :], small[:, 1, :], ALU.add))
                        done(nc.vector.tensor_scalar(small[:, 5, :], small[:, 4, :], 1e-8, None, ALU.add))
                        done(nc.vector.reciprocal(small[:, 4, :], small[:, 5, :]))
                        for k in range(2):
                            done(nc.vector.tensor_tensor(small[:, 6 + k, :], small[:, k, :], small[:, 4, :], ALU.mult))
                            done(nc.vector.tensor_tensor(pick[:, k], pick[:, k], spread(6 + k), ALU.mult))
                        done(nc.vector.tensor_tensor(combine[:], pick[:, 0], pick[:, 1], ALU.add))
                    else:
                        first_of(score[:], 0, combine[:])
                    assert made == STEPS
                    dve.sem_inc(combine_ready, 1)
                    dve.wait_ge(bias_ready, s)
                    nc.vector.tensor_tensor(acc[:], bias_ps[:], g.X[:, bass.ds(s - 1, 1), :].rearrange("p a t -> p (a t)"), ALU.add).then_inc(acc_started, 1)
                    dve.wait_ge(acc_started, s)
                    for e in range(E):
                        dve.wait_ge(y_done, s * E + (e + 1))
                        if e:
                            dve.wait_ge(y_added, s * E + e)
                        for t in range(TILES):
                            cols = slice(t * P, (t + 1) * P)
                            out = acc[:, cols] if e < E - 1 else g.X[:, bass.ds(s - 1, 1), cols].rearrange("p a t -> p (a t)")
                            last = nc.vector.scalar_tensor_tensor(out, y_ps[e % 2][:, cols], combine[:, t, e:e + 1], acc[:, cols], ALU.mult, ALU.add)
                        last.then_inc(y_added, 1)

    run_phase(nc, name, body)


def softmax_attention_phase(nc, g, name, w, causal_only):
    rope = causal_only

    def body(ph):
        wq = ph.sb("wq", [P, P])
        wk = ph.sb("wk", [P, P])
        wv = ph.sb("wv", [P, P])
        wo = ph.sb("wo", [P, P])
        mask = ph.sb("mask", [P, 7 * P])
        if rope:
            wq_rot = ph.sb("wq_rot", [P, 64])
            wk_rot = ph.sb("wk_rot", [P, 64])
            cos = ph.sb("cos", [P, TOKENS])
            sin = ph.sb("sin", [64, TOKENS])
            rotated = ph.sb("rotated", [64, TOKENS])
        else:
            bias = ph.sb("bias", [P, 3])
            bo = ph.sb("bo", [P, P])
            y = ph.sb("y", [P, P])
        xs = ph.sb("xs", [P, TOKENS])
        q_t = ph.sb("q_t", [P, TOKENS])
        k_t = ph.sb("k_t", [P, TOKENS])
        v_t = ph.sb("v_t", [P, TOKENS])
        vo = ph.sb("vo", [P, TILES, P])
        masked = ph.sb("masked", [P, 2, TOKENS])
        probs = ph.sb("probs", [P, 2, TOKENS])
        probs_t = ph.sb("probs_t", [P, 2, TOKENS])
        neg_max = ph.sb("neg_max", [P, TILES])
        row_sum = ph.sb("row_sum", [P, TILES])
        inv_sum = ph.sb("inv_sum", [P, TILES])
        proj_ps = [ph.ps(f"proj_ps{i}", [P, TOKENS]) for i in range(4)]
        score_ps = [ph.ps(f"score_ps{i}", [P, TOKENS]) for i in range(2)]
        turn_ps = ph.ps("turn_ps", [P, TOKENS])
        out_ps = [ph.ps("out_ps", [P, TOKENS]), proj_ps[3]]
        turned_ps = [turn_ps, proj_ps[1]]
        names = ["loaded", "rot_ready", "xs_ready", "q_projected", "k_projected", "v_projected", "q_scaled", "q_rotated", "q_ready",
                 "k_scaled", "k_rotated", "k_ready", "v_ready", "vo_done", "vo_ready", "scores_done", "masked_ready",
                 "max_ready", "probs_ready", "turned", "probs_t_ready", "out_done", "inv_ready", "y_ready", "x_added"]
        q = {n: ph.sem(n) for n in names}
        LOADS = 16 * (7 if rope else 9)
        SCALE = 1.0 if rope else float(P) ** -0.5
        def keys(t):
            return t + 1 if causal_only else TILES

        norm = Normaliser(nc, ph, g, score_ps)

        with nc.Block() as block:

            @block.sync
            def _(sp):
                for dst, key in ((wq, "wq"), (wk, "wk"), (wv, "wv"), (wo, "wo"), (mask, "mask")):
                    sp.dma_start(dst[:], w[key]).then_inc(q["loaded"], 16)
                if rope:
                    sp.dma_start(cos[:], w["cos"]).then_inc(q["loaded"], 16)
                    sp.dma_start(sin[:], w["sin"]).then_inc(q["loaded"], 16)
                else:
                    for i, key in enumerate(("bq", "bk", "bv")):
                        sp.dma_start(bias[:, i:i + 1], w[key].unsqueeze(1)).then_inc(q["loaded"], 16)
                    sp.dma_start(bo[:], w["bo"].partition_broadcast(P)).then_inc(q["loaded"], 16)

            @block.scalar
            def _(act):
                norm.scalar(act)
                act.sem_inc(q["probs_ready"], TILES)
                act.wait_ge(q["loaded"], LOADS)
                with act.Fori(1, SEQS + 1) as s:

                    def copy_probs_t(t):
                        act.wait_ge(q["turned"], (s - 1) * TILES + (t + 1))
                        act.wait_ge(q["out_done"], s * TILES + (t - 1) if t >= 2 else (s - 1) * TILES + (t + 3))
                        n = keys(t) * P
                        nc.scalar.copy(probs_t[:, t % 2, 0:n], turned_ps[t % 2][:, 0:n]).then_inc(q["probs_t_ready"], 1)

                    nc.scalar.copy(xs[:], g.XH[:, bass.ds(s - 1, 1), :]).then_inc(q["xs_ready"], 1)
                    if not rope:
                        act.wait_ge(q["q_projected"], s)
                        nc.scalar.activation(q_t[:], proj_ps[0][:], ACT.Relu, bias=bias[:, 0:1]).then_inc(q["q_ready"], 1)
                        act.wait_ge(q["k_projected"], s)
                        nc.scalar.activation(k_t[:], proj_ps[2][:], ACT.Relu, bias=bias[:, 1:2]).then_inc(q["k_ready"], 1)
                    act.wait_ge(q["v_projected"], s)
                    if rope:
                        nc.scalar.copy(v_t[:], turn_ps[:]).then_inc(q["v_ready"], 1)
                    else:
                        nc.scalar.activation(v_t[:], turn_ps[:], ACT.Relu, bias=bias[:, 2:3]).then_inc(q["v_ready"], 1)
                    act.wait_ge(q["vo_done"], s)
                    nc.scalar.copy(vo[:].rearrange("p t d -> p (t d)"), out_ps[0][:]).then_inc(q["vo_ready"], 1)
                    for t in range(TILES):
                        act.wait_ge(q["max_ready"], (s - 1) * TILES + (t + 1))
                        n = keys(t) * P
                        nc.scalar.activation(probs[:, t % 2, 0:n], masked[:, t % 2, 0:n], ACT.Exp, bias=neg_max[:, t:t + 1],
                                             accum_out=row_sum[:, t:t + 1]).then_inc(q["probs_ready"], 1)
                        if t:
                            copy_probs_t(t - 1)
                    copy_probs_t(TILES - 1)

            @block.tensor
            def _(pe):
                norm.tensor(pe)
                pe.sem_inc(q["out_done"], TILES)
                pe.wait_ge(q["loaded"], LOADS)
                if rope:
                    pe.wait_ge(q["rot_ready"], 1)
                with pe.Fori(1, SEQS + 1) as s:

                    def scores(t):
                        pe.wait_ge(q["masked_ready"], s * TILES + (t - 1) if t >= 2 else (s - 1) * TILES + (t + 3))
                        nc.tensor.matmul(score_ps[t % 2][:, 0:keys(t) * P], q_t[:, t * P:(t + 1) * P], k_t[:, 0:keys(t) * P],
                                         start=True, stop=True).then_inc(q["scores_done"], 1)

                    pe.wait_ge(q["xs_ready"], s)
                    if rope:
                        nc.tensor.matmul(proj_ps[0][:], wq[:], xs[:], start=True, stop=True)
                        nc.tensor.matmul(proj_ps[1][0:64, :], wq_rot[:], xs[:], start=True, stop=True).then_inc(q["q_projected"], 1)
                        nc.tensor.matmul(proj_ps[2][:], wk[:], xs[:], start=True, stop=True)
                        pe.wait_ge(q["x_added"], s * TILES)
                        nc.tensor.matmul(proj_ps[3][0:64, :], wk_rot[:], xs[:], start=True, stop=True).then_inc(q["k_projected"], 1)
                    else:
                        nc.tensor.matmul(proj_ps[0][:], wq[:], xs[:], start=True, stop=True).then_inc(q["q_projected"], 1)
                        nc.tensor.matmul(proj_ps[2][:], wk[:], xs[:], start=True, stop=True).then_inc(q["k_projected"], 1)
                    nc.tensor.matmul(turn_ps[:], wv[:], xs[:], start=True, stop=True).then_inc(q["v_projected"], 1)
                    def values():
                        pe.wait_ge(q["v_ready"], s)
                        if not rope:
                            pe.wait_ge(q["x_added"], s * TILES)
                        for t in range(TILES):
                            last = nc.tensor.matmul(out_ps[0][:, t * P:(t + 1) * P], v_t[:, t * P:(t + 1) * P], wo[:], start=True, stop=True)
                        last.then_inc(q["vo_done"], 1)

                    if rope:
                        values()
                    pe.wait_ge(q["q_ready"], s)
                    pe.wait_ge(q["k_ready"], s)
                    scores(0)
                    scores(1)
                    if not rope:
                        values()
                    pe.wait_ge(q["vo_ready"], s)

                    def turn(t):
                        pe.wait_ge(q["probs_ready"], s * TILES + (t + 1))
                        for k in range(keys(t)):
                            last = nc.tensor.transpose(turned_ps[t % 2][:, k * P:(k + 1) * P], probs[:, t % 2, k * P:(k + 1) * P], g.ident[:])
                        last.then_inc(q["turned"], 1)

                    turn(0)
                    scores(2)
                    turn(1)
                    scores(3)
                    for t in range(TILES):
                        pe.wait_ge(q["probs_t_ready"], (s - 1) * TILES + (t + 1))
                        if t >= 2:
                            pe.wait_ge(q["x_added"], s * TILES + (t - 1))
                        for k in range(keys(t)):
                            last = nc.tensor.matmul(out_ps[t % 2][:, 0:P], probs_t[:, t % 2, k * P:(k + 1) * P], vo[:, k, :],
                                                    start=(k == 0), stop=(k == keys(t) - 1))
                        last.then_inc(q["out_done"], 1)
                        if t + 2 < TILES:
                            turn(t + 2)

            @block.gpsimd
            def _(pool):
                norm.gpsimd(pool)

            @block.vector
            def _(dve):
                norm.vector(dve)
                dve.sem_inc(q["masked_ready"], TILES)
                dve.sem_inc(q["x_added"], TILES)
                dve.wait_ge(q["loaded"], LOADS)
                if rope:
                    for src, dst in ((wq, wq_rot), (wk, wk_rot)):
                        nc.vector.tensor_scalar(dst[:, 0:32], src[:, 32:64], -1.0, None, ALU.mult)
                        last = nc.vector.tensor_copy(dst[:, 32:64], src[:, 0:32])
                    last.then_inc(q["rot_ready"], 1)
                with dve.Fori(1, SEQS + 1) as s:

                    def add_output(t):
                        cols = slice(t * P, (t + 1) * P)
                        xt = g.X[:, bass.ds(s - 1, 1), cols].rearrange("p a t -> p (a t)")
                        out = out_ps[t % 2][:, 0:P]
                        dve.wait_ge(q["out_done"], s * TILES + (t + 1))
                        nc.vector.reciprocal(inv_sum[:, t:t + 1], row_sum[:, t:t + 1]).then_inc(q["inv_ready"], 1)
                        dve.wait_ge(q["inv_ready"], (s - 1) * TILES + (t + 1))
                        if rope:
                            nc.vector.scalar_tensor_tensor(xt, out, inv_sum[:, t:t + 1], xt, ALU.mult, ALU.add).then_inc(q["x_added"], 1)
                        else:
                            nc.vector.scalar_tensor_tensor(y[:], out, inv_sum[:, t:t + 1], bo[:], ALU.mult, ALU.add).then_inc(q["y_ready"], 1)
                            dve.wait_ge(q["y_ready"], (s - 1) * TILES + (t + 1))
                            nc.vector.scalar_tensor_tensor(xt, y[:], 0.0, xt, ALU.max, ALU.add).then_inc(q["x_added"], 1)

                    if rope:
                        for side, dst, a in (("q", q_t, 0), ("k", k_t, 2)):
                            dve.wait_ge(q[side + "_projected"], s)
                            if side == "k":
                                dve.wait_ge(q["q_ready"], s)
                            nc.vector.tensor_tensor(dst[:], proj_ps[a][:], cos[:], ALU.mult).then_inc(q[side + "_scaled"], 1)
                            nc.vector.tensor_tensor(rotated[:], proj_ps[a + 1][0:64, :], sin[:], ALU.mult).then_inc(q[side + "_rotated"], 1)
                            dve.wait_ge(q[side + "_scaled"], s)
                            dve.wait_ge(q[side + "_rotated"], s)
                            nc.vector.tensor_tensor(dst[0:64, :], dst[0:64, :], rotated[:], ALU.add).then_inc(q[side + "_ready"], 1)
                    for t in range(TILES):
                        n = keys(t) * P
                        dve.wait_ge(q["scores_done"], (s - 1) * TILES + (t + 1))
                        dve.wait_ge(q["probs_ready"], s * TILES + (t - 1) if t >= 2 else (s - 1) * TILES + (t + 3))
                        at = (TILES - 1 - t) * P
                        nc.vector.scalar_tensor_tensor(masked[:, t % 2, 0:n], score_ps[t % 2][:, 0:n], SCALE, mask[:, at:at + n],
                                                       ALU.mult, ALU.add).then_inc(q["masked_ready"], 1)
                        dve.wait_ge(q["masked_ready"], s * TILES + (t + 1))
                        nc.vector.tensor_reduce(neg_max[:, t:t + 1], masked[:, t % 2, 0:n], AX, ALU.max, negate=True).then_inc(q["max_ready"], 1)
                        if t >= 2:
                            add_output(t - 2)
                    add_output(TILES - 2)
                    add_output(TILES - 1)

    run_phase(nc, name, body)


def chunk_attention_phase(nc, g, name, w):
    PAIRS = SEQS // 2
    SPAN = 2 * P - 1

    def body(ph):
        wqk = ph.sb("wqk", [P, P])
        wv = ph.sb("wv", [P, P])
        bqk = ph.sb("bqk", [P, 1])
        bv = ph.sb("bv", [P, P])
        gamma = ph.sb("gamma", [P, 2])
        beta = ph.sb("beta", [P, 2])
        rel = ph.sb("rel", [32, 1])
        rel_wide = ph.sb("rel_wide", [32, P])
        bucket = ph.sb("bucket", [32, SPAN])
        by_distance = ph.sb("by_distance", [P, SPAN])
        mask = ph.sb("mask", [P, P])
        bias = ph.sb("bias", [P, P])
        xs = ph.sb("xs", [P, 2, TOKENS])
        qk = ph.sb("qk", [P, 2, TOKENS])
        q_t = ph.sb("q_t", [P, 2, TOKENS])
        k_t = ph.sb("k_t", [P, 2, TOKENS])
        v_raw = ph.sb("v_raw", [P, 2, TOKENS])
        v = ph.sb("v", [P, 2, TOKENS])
        masked = ph.sb("masked", [P, 2, TOKENS])
        probs = ph.sb("probs", [P, 2, TOKENS])
        probs_t = ph.sb("probs_t", [P, 2, TOKENS])
        top = ph.sb("top", [P, 2, TILES])
        total = ph.sb("total", [P, 2, TILES])
        inv = ph.sb("inv", [P, 2, TILES])
        a_ps = [ph.ps(f"a_ps{i}", [P, TOKENS]) for i in range(2)]
        v_ps = [ph.ps(f"v_ps{i}", [P, TOKENS]) for i in range(2)]
        s_ps = [ph.ps(f"s_ps{i}", [P, TOKENS]) for i in range(2)]
        o_ps = [ph.ps(f"o_ps{i}", [P, TOKENS]) for i in range(2)]
        skew = nc.dram_tensor(f"{name}_skew", [P, SPAN], F32, kind="Internal").ap()
        names = ["loaded", "rel_ready", "distance_ready", "distance_copied", "skew_written", "skew_read", "bias_ready",
                 "xs_ready", "qk_projected", "v_projected", "qk_ready", "v_raw_ready", "v_ready", "q_ready",
                 "scores_done", "masked_ready", "max_ready", "centred", "probs_ready", "sum_ready", "inv_ready", "turned",
                 "probs_t_ready", "out_done", "x_added"]
        q = {n: ph.sem(n) for n in names}
        LOADS = 16 * 9

        norm = Normaliser(nc, ph, g, s_ps)

        with nc.Block() as block:

            @block.sync
            def _(sp):
                for dst, src in ((wqk[:], w["Wqk"]), (wv[:], w["Wv"]), (bqk[:], w["bqk"].unsqueeze(1)),
                                 (bv[:], w["bv"].partition_broadcast(P)), (rel[:], w["rel_emb"]),
                                 (bucket[:], w["bucket"]), (mask[:], w["chunk_mask"])):
                    sp.dma_start(dst, src).then_inc(q["loaded"], 16)
                sp.dma_start(gamma[:], w["gamma"].rearrange("a d -> d a"), allow_slow_non_contiguous=True).then_inc(q["loaded"], 16)
                sp.dma_start(beta[:], w["beta"].rearrange("a d -> d a"), allow_slow_non_contiguous=True).then_inc(q["loaded"], 16)
                sp.wait_ge(q["distance_copied"], 1)
                sp.dma_start(skew, by_distance[:]).then_inc(q["skew_written"], 16)
                sp.wait_ge(q["skew_written"], 16)
                skewed = bass.AP(skew.tensor, P - 1, [[SPAN - 1, P], [1, P]])
                sp.dma_start(bias[:], skewed).then_inc(q["skew_read"], 16)

            @block.scalar
            def _(act):
                norm.scalar(act)
                act.wait_ge(q["loaded"], LOADS)
                act.wait_ge(q["distance_ready"], 1)
                nc.scalar.mul(by_distance[:], o_ps[0][:, 0:SPAN], float(P) ** 0.5).then_inc(q["distance_copied"], 1)
                with act.Fori(1, PAIRS + 1) as pair:
                    def at(i):
                        return (pair - 1) * 2 + (i + 1)

                    for i in range(2):
                        nc.scalar.copy(xs[:, i], g.XH[:, bass.ds(pair * 2 + (i - 2), 1), :].rearrange("p a t -> p (a t)")).then_inc(q["xs_ready"], 1)
                    for i in range(2):
                        act.wait_ge(q["qk_projected"], at(i))
                        nc.scalar.activation(qk[:, i], a_ps[i][:], ACT.Silu, bias=bqk[:]).then_inc(q["qk_ready"], 1)
                    for i in range(2):
                        act.wait_ge(q["v_raw_ready"], at(i))
                        nc.scalar.activation(v[:, i], v_raw[:, i], ACT.Silu).then_inc(q["v_ready"], 1)
                    for i in range(2):
                        act.wait_ge(q["centred"], at(i))
                        nc.scalar.activation(probs[:, i], masked[:, i], ACT.Exp).then_inc(q["probs_ready"], 1)
                    for i in range(2):
                        act.wait_ge(q["turned"], at(i))
                        nc.scalar.copy(probs_t[:, i], a_ps[i][:]).then_inc(q["probs_t_ready"], 1)

            @block.tensor
            def _(pe):
                norm.tensor(pe)
                pe.sem_inc(q["out_done"], 2)
                pe.wait_ge(q["loaded"], LOADS)
                pe.wait_ge(q["rel_ready"], 1)
                nc.tensor.matmul(o_ps[0][:, 0:SPAN], rel_wide[:], bucket[:], start=True, stop=True).then_inc(q["distance_ready"], 1)
                pe.wait_ge(q["distance_copied"], 1)
                with pe.Fori(1, PAIRS + 1) as pair:
                    def at(i):
                        return (pair - 1) * 2 + (i + 1)

                    for i in range(2):
                        pe.wait_ge(q["xs_ready"], at(i))
                        nc.tensor.matmul(a_ps[i][:], wqk[:], xs[:, i], start=True, stop=True).then_inc(q["qk_projected"], 1)
                        for t in range(TILES):
                            last = nc.tensor.matmul(v_ps[i][:, t * P:(t + 1) * P], xs[:, i, t * P:(t + 1) * P], wv[:], start=True, stop=True)
                        last.then_inc(q["v_projected"], 1)
                    for i in range(2):
                        pe.wait_ge(q["q_ready"], at(i))
                        for t in range(TILES):
                            last = nc.tensor.matmul(s_ps[i][:, t * P:(t + 1) * P], q_t[:, i, t * P:(t + 1) * P], k_t[:, i, t * P:(t + 1) * P],
                                                    start=True, stop=True)
                        last.then_inc(q["scores_done"], 1)
                    for i in range(2):
                        pe.wait_ge(q["probs_ready"], at(i))
                        for t in range(TILES):
                            last = nc.tensor.transpose(a_ps[i][:, t * P:(t + 1) * P], probs[:, i, t * P:(t + 1) * P], g.ident[:])
                        last.then_inc(q["turned"], 1)
                    for i in range(2):
                        pe.wait_ge(q["probs_t_ready"], at(i))
                        pe.wait_ge(q["v_ready"], at(i))
                        pe.wait_ge(q["x_added"], at(i))
                        for t in range(TILES):
                            last = nc.tensor.matmul(o_ps[i][:, t * P:(t + 1) * P], probs_t[:, i, t * P:(t + 1) * P], v[:, i, t * P:(t + 1) * P],
                                                    start=True, stop=True)
                        last.then_inc(q["out_done"], 1)

            @block.gpsimd
            def _(pool):
                norm.gpsimd(pool)

            @block.vector
            def _(dve):
                norm.vector(dve)
                dve.sem_inc(q["x_added"], 2)
                dve.wait_ge(q["loaded"], LOADS)
                nc.vector.tensor_copy(rel_wide[:], rel[:].to_broadcast([32, P])).then_inc(q["rel_ready"], 1)
                dve.wait_ge(q["skew_read"], 16)
                nc.vector.tensor_tensor(bias[:], bias[:], mask[:], ALU.add).then_inc(q["bias_ready"], 1)
                dve.wait_ge(q["bias_ready"], 1)
                with dve.Fori(1, PAIRS + 1) as pair:
                    def at(i):
                        return (pair - 1) * 2 + (i + 1)

                    def tiles(buf, i):
                        return buf[:, i].rearrange("p (t k) -> p t k", k=P)

                    def spread(col, i):
                        return col[:, i, :].unsqueeze(2).to_broadcast([P, TILES, P])

                    for i in range(2):
                        dve.wait_ge(q["v_projected"], at(i))
                        nc.vector.tensor_tensor(tiles(v_raw, i), v_ps[i][:].rearrange("p (t d) -> p t d", d=P),
                                                bv[:].unsqueeze(1).to_broadcast([P, TILES, P]), ALU.add).then_inc(q["v_raw_ready"], 1)
                        dve.wait_ge(q["qk_ready"], at(i))
                        nc.vector.tensor_scalar(q_t[:, i], qk[:, i], gamma[:, 0:1], beta[:, 0:1], ALU.mult, ALU.add)
                        nc.vector.tensor_scalar(k_t[:, i], qk[:, i], gamma[:, 1:2], beta[:, 1:2], ALU.mult, ALU.add).then_inc(q["q_ready"], 1)
                    for i in range(2):
                        dve.wait_ge(q["scores_done"], at(i))
                        nc.vector.scalar_tensor_tensor(tiles(masked, i), s_ps[i][:].rearrange("p (t k) -> p t k", k=P), float(P) ** -0.5,
                                                       bias[:].unsqueeze(1).to_broadcast([P, TILES, P]), ALU.mult, ALU.add).then_inc(q["masked_ready"], 1)
                        dve.wait_ge(q["masked_ready"], at(i))
                        nc.vector.tensor_reduce(top[:, i], tiles(masked, i), AX, ALU.max).then_inc(q["max_ready"], 1)
                        dve.wait_ge(q["max_ready"], at(i))
                        nc.vector.tensor_tensor(tiles(masked, i), tiles(masked, i), spread(top, i), ALU.subtract).then_inc(q["centred"], 1)
                    for i in range(2):
                        dve.wait_ge(q["probs_ready"], at(i))
                        nc.vector.tensor_reduce(total[:, i], tiles(probs, i), AX, ALU.add).then_inc(q["sum_ready"], 1)
                        dve.wait_ge(q["sum_ready"], at(i))
                        nc.vector.reciprocal(inv[:, i], total[:, i]).then_inc(q["inv_ready"], 1)
                    for i in range(2):
                        dve.wait_ge(q["inv_ready"], at(i))
                        dve.wait_ge(q["out_done"], at(i) + 2)
                        for t in range(TILES):
                            xt = g.X[:, bass.ds(pair * 2 + (i - 2), 1), t * P:(t + 1) * P].rearrange("p a t -> p (a t)")
                            last = nc.vector.scalar_tensor_tensor(xt, o_ps[i][:, t * P:(t + 1) * P], inv[:, i, t:t + 1], xt, ALU.mult, ALU.add)
                        last.then_inc(q["x_added"], 1)

    run_phase(nc, name, body)


def local_transformer_phase(nc, g, name, w):
    LAYERS, HEADS, HD, BLOCK, WIN, BACK = 6, 16, 64, 64, 96, 32
    INNER = HEADS * HD
    CH = INNER // P
    GROUPS = 4
    HPG = HEADS // GROUPS
    HIDDEN = 341
    HCH = [(0, P), (P, P), (2 * P, HIDDEN - 2 * P)]
    PV_HEADS = [(0, 6), (6, 11), (11, 16)]


    def s_banks(t):
        return (0, 1, 2, 3) if t % 2 == 0 else (2, 3, 0, 1)

    def pv_banks(t):
        b = s_banks(t)
        return b[3], b[0], b[1]

    LAST_OUT = (2, 3, 0)
    FFN_TURN, FFN_BACK, FFN_GATE, FFN_A, FFN_OUT = 3, 2, (3, 0, 3), (2, 1, 2), 0

    def body(ph):
        sb = ph.sb
        stage = sb("stage", [P, 3 * INNER])
        wqkv_hi, wqkv_lo = (sb(n, [P, 3 * INNER], F32R) for n in ("wqkv_hi", "wqkv_lo"))
        ys_hi, ys_lo = (sb(n, [P, BACK + TOKENS], F32R) for n in ("ys_hi", "ys_lo"))
        head_hi, head_lo = (sb(n, [P, P], F32R) for n in ("head_hi", "head_lo"))
        wo = sb("wo", [P, CH, P])
        w1 = sb("w1", [P, 2 * HIDDEN])
        w2 = sb("w2", [P, 3, P])
        b1 = sb("b1", [P, 6])
        ln = sb("ln", [P, 3])
        scales = sb("scales", [P, 2, LAYERS, HD])
        base = sb("base", [P, TILES, 4, HD])
        table = sb("table", [P, TILES, 4, HD])
        band = sb("band", [P, 2, WIN])
        squares = sb("squares", [P, 2 * INNER])
        normed = sb("normed", [P, 2 * INNER])
        rot = sb("rot", [P, 2 * INNER])
        norm2 = sb("norm2", [P, 2 * HEADS])
        norm2c = sb("norm2c", [P, 2 * HEADS])
        inv_norm = sb("inv_norm", [P, 2 * HEADS])
        q_t = sb("q_t", [P, CH, P])
        k_t = sb("k_t", [P, CH, BACK + TOKENS])
        scores = sb("scores", [P, HEADS, WIN])
        top = sb("top", [P, HEADS])
        probs_t = sb("probs_t", [WIN, HEADS, P])
        vals = sb("vals", [WIN, 2, HEADS, HD + 1])
        inv_sum = sb("inv_sum", [P, HEADS])
        att = sb("att", [P, INNER])
        att_t = sb("att_t", [P, CH, P])
        y1 = sb("y1", [P, TOKENS])
        y1s = sb("y1s", [P, TOKENS])
        stats = sb("stats", [P, TILES, 6])
        mean_var = sb("mean_var", [P, TILES, 2])
        var_eps = sb("var_eps", [P, TILES])
        rstd = sb("rstd", [P, TILES])
        y_hat = sb("y_hat", [P, TOKENS])
        xn = sb("xn", [P, TOKENS])
        gates = sb("gates", [P, 3, TOKENS])
        table_pick = sb("table_pick", [P, 2])
        A = [ph.ps(f"A{i}", [P, TOKENS]) for i in range(4)]
        B = [ph.ps(f"B{i}", [P, TOKENS]) for i in range(4)]

        per_tile = {"qk_projected": 4, "scores_done": 4, "v_projected": 4, "probs_turned": 4, "pv_done": 3, "qk_turned": 4,
                    "out_turned": 2, "wo_done": 1,
                    "squared": 4, "v_copied": 4, "exp_done": 2, "probs_t_ready": 4, "qkt_copied": 4, "out_copied": 2,
                    "masked": 4, "max_ready": 2, "norms_ready": 2, "qk_normed": 4, "cos_ready": 2, "sums_inverted": 1,
                    "att_ready": 3, "y_added": 1,
                    "centred": 2, "norms_guarded": 2, "inv_norms_ready": 2, "sin_ready": 2, "rotated": 2}
        per_seq = {"ffn_turned": 1, "ffn_back": 1, "gate_done": 3, "a_done": 3, "w2_done": 1,
                   "head_hi_ready": 1, "head_ready": 1, "ys_hi_ready": 1, "ys_ready": 1, "y1s_ready": 1, "xn_ready": 1, "gelu_done": 3,
                   "stats_ready": 1, "aggregated": 1, "var_ready": 1, "y_hat_ready": 1, "prod_ready": 3, "seq_done": 1,
                   "rstd_ready": 1}
        q = {k: ph.sem(k) for k in (*per_tile, *per_seq)}
        consts_loaded, wqkv_loaded, wo_loaded, ffn_loaded = (ph.sem(k) for k in ("consts_loaded", "wqkv_loaded", "wo_loaded", "ffn_loaded"))
        wait_taken = ph.sem("wait_taken")
        split_hi, qk_split, v_split = (ph.sem(k) for k in ("split_hi", "qk_split", "v_split"))
        tables_ready, pads_ready = ph.sem("tables_ready"), ph.sem("pads_ready")
        CONST_LOADS, FFN_LOADS = 16 * 4, 16 * 11
        PE_MADE = ("qk_projected", "scores_done", "v_projected", "probs_turned", "pv_done", "qk_turned", "out_turned", "wo_done",
                   "ffn_turned", "ffn_back", "gate_done", "a_done", "w2_done")
        ACT_MADE = ("squared", "v_copied", "exp_done", "probs_t_ready", "qkt_copied", "out_copied", "head_hi_ready", "ys_hi_ready", "y1s_ready",
                    "xn_ready", "gelu_done")
        DVE_MADE = ("masked", "max_ready", "centred", "rotated", "norms_ready", "norms_guarded", "qk_normed", "cos_ready", "sums_inverted", "att_ready", "y_added",
                    "stats_ready", "aggregated", "var_ready", "y_hat_ready", "prod_ready", "seq_done")
        POOL_MADE = ("head_ready", "ys_ready", "inv_norms_ready", "sin_ready", "rstd_ready")

        def credit(eng, made):
            for k in made:
                eng.sem_inc(q[k], per_tile[k] * TILES if k in per_tile else per_seq[k])

        def of_tile(n, key, t, k):
            c = per_tile[key]
            return n * (TILES * c) + (t * c + k)

        def of_seq(n, key, k=1):
            return n * per_seq[key] + k

        def place(h):
            return 8 * (h // 8) + HPG * (h % 2) + (h % 8) // 2

        def y_of(s, c0=0, c1=TOKENS, rows=slice(0, P)):
            return g.XH[rows, bass.ds(s - 1, 1), c0:c1].rearrange("p a t -> p (a t)")

        def of_heads(buf, a):
            return buf[:, a * INNER:(a + 1) * INNER].rearrange("p (h d) -> p h d", d=HD)

        def sine_product(engine, t, a, half):
            to, of = slice(32 * half, 32 * half + 32), slice(32 - 32 * half, 64 - 32 * half)
            return engine.tensor_tensor(of_heads(squares, a)[:, :, to], of_heads(normed, a)[:, :, of],
                                        table[:, t % TILES, 2 * a + 1, to].unsqueeze(1).to_broadcast([P, HEADS, 32]), ALU.mult)

        norm = Normaliser(nc, ph, g, B[0:2], rot[:].rearrange("p (i t) -> p i t", i=4)[:, 0:2])

        with nc.Block() as block:

            @block.sync
            def _(sp):
                sp.dma_start(base[:], w["rotary"]).then_inc(consts_loaded, 16)
                sp.dma_start(band[:], w["band"]).then_inc(consts_loaded, 16)
                for i, key in enumerate(("q_scale", "k_scale")):
                    sp.dma_start(scales[:, i].rearrange("p l d -> p (l d)"), w[key].rearrange("l d -> (l d)").partition_broadcast(P)).then_inc(consts_loaded, 16)
                with sp.Fori(1, LAYERS + 1) as layer:
                    one = bass.ds(layer - 1, 1)
                    sp.wait_ge(v_split, layer)
                    sp.dma_start(stage[:], w["Wqkv"][one].rearrange("a d n -> (a d) n")).then_inc(wqkv_loaded, 16)
                    sp.wait_ge(q["wo_done"], layer * (SEQS * TILES) - (SEQS - 1) * TILES)
                    sp.dma_start(wo[:], w["Wo"][one].rearrange("a (c p) d -> p (a c) d", p=P)).then_inc(wo_loaded, 16)
                    sp.wait_ge(q["seq_done"], layer * SEQS - (SEQS - 1))
                    sp.dma_start(w1[:], w["W1"][one].rearrange("a d n -> (a d) n")).then_inc(ffn_loaded, 16)
                    sp.dma_start(w2[:, 0:2], w["W2"][one, 0:2 * P].rearrange("a (c p) d -> p (a c) d", p=P)).then_inc(ffn_loaded, 16)
                    sp.dma_start(w2[0:HIDDEN - 2 * P, 2], w["W2"][one, 2 * P:HIDDEN].rearrange("a p d -> (a p) d")).then_inc(ffn_loaded, 16)
                    for i, key in enumerate(("ln_g", "ln_b", "b2")):
                        sp.dma_start(ln[:, i:i + 1], w[key][one].rearrange("a d -> d a")).then_inc(ffn_loaded, 16)
                    for side in range(2):
                        at = side * HIDDEN
                        sp.dma_start(b1[:, 3 * side:3 * side + 2], w["b1"][one, at:at + 2 * P].rearrange("a (c p) -> p (a c)", p=P),
                                     allow_slow_non_contiguous=True).then_inc(ffn_loaded, 16)
                        sp.dma_start(b1[0:HIDDEN - 2 * P, 3 * side + 2:3 * side + 3], w["b1"][one, at + 2 * P:at + HIDDEN].rearrange("a p -> p a")).then_inc(ffn_loaded, 16)
                    sp.nop().then_inc(ffn_loaded, 16)

            @block.tensor
            def _(pe):
                norm.tensor(pe)
                credit(pe, PE_MADE)
                pe.wait_ge(pads_ready, 3)

                def product(out, hi, lo, d0, d1):
                    nc.tensor.matmul(out, hi, wqkv_hi[:, d0:d1], start=True, stop=False)
                    nc.tensor.matmul(out, hi, wqkv_lo[:, d0:d1], start=False, stop=False)
                    return nc.tensor.matmul(out, lo, wqkv_hi[:, d0:d1], start=False, stop=True)

                def project_qk(n, t):
                    first = t % TILES == 0
                    if first:
                        pe.wait_ge(q["head_ready"], of_seq(n, "head_ready", 1 + t // TILES))
                        hi, lo = head_hi[:], head_lo[:]
                    else:
                        if t == 1:
                            pe.wait_ge(q["ys_ready"], of_seq(n, "ys_ready"))
                        hi, lo = (y[:, BACK + t * P:BACK + (t + 1) * P] for y in (ys_hi, ys_lo))
                    for i in range(4):
                        pe.wait_ge(q["qkt_copied"], of_tile(n, "qkt_copied", t - 1, i + 1))
                        product(A[i][:], hi, lo, i * 512, (i + 1) * 512).then_inc(q["qk_projected"], 1)

                def turn_qk(n, t):
                    for i in range(4):
                        if i % 2 == 0:
                            pe.wait_ge(q["rotated"], of_tile(n, "rotated", t, i // 2 + 1))
                        if i == 0:
                            pe.wait_ge(q["qk_normed"], of_tile(n, "qk_normed", t, 4))
                        for j in range(4):
                            last = nc.tensor.transpose(A[i][:, j * P:(j + 1) * P], rot[:, (4 * i + j) * P:(4 * i + j + 1) * P], g.ident[:])
                        last.then_inc(q["qk_turned"], 1)

                def make_scores(n, t, half):
                    if half == 0:
                        pe.wait_ge(q["qkt_copied"], of_tile(n, "qkt_copied", t, 4))
                        if t >= 2:
                            pe.wait_ge(q["y_added"], of_tile(n, "y_added", t - 2, 1))
                        if t >= 1:
                            pe.wait_ge(q["att_ready"], of_tile(n, "att_ready", t - 1, 3))
                    pe.sem_inc(wait_taken, 1)
                    for j in range(HPG):
                        for odd in range(2):
                            rows, c = slice(HD * odd, HD * odd + HD), 4 * half + j
                            bank = B[s_banks(t)[2 * half + odd]]
                            for b in range(2):
                                c0 = t * P + b * BLOCK
                                last = nc.tensor.matmul(bank[b * BLOCK:(b + 1) * BLOCK, j * WIN:(j + 1) * WIN],
                                                        q_t[rows, c, b * BLOCK:(b + 1) * BLOCK], k_t[rows, c, c0:c0 + WIN],
                                                        start=True, stop=True)
                            if j == HPG - 1:
                                last.then_inc(q["scores_done"], 1)

                def project_v(n, t):
                    if t == 0:
                        pe.wait_ge(q["seq_done"], n)
                    for i in range(4):
                        b, half = i // 2, i % 2
                        c0 = t * P + b * BLOCK
                        pe.wait_ge(q["masked"], of_tile(n, "masked", t, i + 1))
                        product(B[s_banks(t)[i]][0:WIN, :], ys_hi[:, c0:c0 + WIN], ys_lo[:, c0:c0 + WIN], 2 * INNER + half * 512, 2 * INNER + (half + 1) * 512).then_inc(q["v_projected"], 1)

                def turn_probs(n, t, ahead, half):
                    for i in (2 * half, 2 * half + 1):
                        if i % 2 == 0:
                            pe.wait_ge(q["exp_done"], of_tile(n, "exp_done", t, i // 2 + 1))
                        if ahead:
                            pe.wait_ge(q["qk_normed"], of_tile(n, "qk_normed", t + 1, i + 1))
                        for h in range(HPG * i, HPG * (i + 1)):
                            last = nc.tensor.transpose(A[i][0:WIN, (h % HPG) * P:(h % HPG + 1) * P], scores[:, h, :], g.ident[:])
                        last.then_inc(q["probs_turned"], 1)

                def weigh_values(n, t):
                    pe.wait_ge(q["v_copied"], of_tile(n, "v_copied", t, 4))
                    if t >= 1:
                        pe.wait_ge(q["out_copied"], of_tile(n, "out_copied", t - 1, 2))
                    for i, (h0, h1) in enumerate(PV_HEADS):
                        pe.wait_ge(q["probs_t_ready"], of_tile(n, "probs_t_ready", t, 2 if h1 <= 8 else 4))
                        for h in range(h0, h1):
                            for b in range(2):
                                last = nc.tensor.matmul(B[pv_banks(t)[i]][b * BLOCK:(b + 1) * BLOCK, (h - h0) * (HD + 1):(h - h0 + 1) * (HD + 1)],
                                                        probs_t[:, place(h), b * BLOCK:(b + 1) * BLOCK], vals[:, b, h, :], start=True, stop=True)
                        last.then_inc(q["pv_done"], 1)

                def project_out(n, t, banks, meanwhile=None):
                    pe.wait_ge(q["att_ready"], of_tile(n, "att_ready", t, 3))
                    for i in range(2):
                        if t + 1 < TILES:
                            pe.wait_ge(q["v_copied"], of_tile(n, "v_copied", t + 1, i + 1))
                        for j in range(4):
                            c = 4 * i + j
                            last = nc.tensor.transpose(B[banks[i]][:, j * P:(j + 1) * P], att[:, c * P:(c + 1) * P], g.ident[:])
                        last.then_inc(q["out_turned"], 1)
                    if t + 1 < TILES:
                        pe.wait_ge(q["v_copied"], of_tile(n, "v_copied", t + 1, 3))
                    if meanwhile:
                        meanwhile()
                    pe.wait_ge(q["out_copied"], of_tile(n, "out_copied", t, 2))
                    for c in range(CH):
                        last = nc.tensor.matmul(B[banks[2]][:, 0:P], wo[:, c, :], att_t[:, c, :], start=(c == 0), stop=(c == CH - 1))
                    last.then_inc(q["wo_done"], 1)

                def sequence(layer, n, more, switch=False):
                    for t in range(TILES):
                        ahead = t + 1 < TILES or more
                        if switch and t + 1 == TILES:
                            pe.wait_ge(qk_split, layer + 1)
                        if ahead and t:
                            project_qk(n, t + 1)
                        if t:
                            make_scores(n, t, 0)
                        make_scores(n, t, 1)
                        project_v(n, t)
                        if t:
                            project_out(n, t - 1, s_banks(t)[0:3], lambda: turn_probs(n, t, ahead, 0))
                        else:
                            pe.wait_ge(wo_loaded, layer * 16)
                            turn_probs(n, t, ahead, 0)
                        turn_probs(n, t, ahead, 1)
                        weigh_values(n, t)
                        if ahead:
                            turn_qk(n, t + 1)
                    if more:
                        project_qk(n + 1, 1)
                    project_out(n, TILES - 1, LAST_OUT)

                    pe.wait_ge(q["y1s_ready"], of_seq(n, "y1s_ready"))
                    for t in range(TILES):
                        last = nc.tensor.transpose(B[FFN_TURN][:, t * P:(t + 1) * P], y1s[:, t * P:(t + 1) * P], g.ident[:])
                    last.then_inc(q["ffn_turned"], 1)
                    if more:
                        make_scores(n + 1, 0, 0)
                    pe.wait_ge(q["y_hat_ready"], of_seq(n, "y_hat_ready"))
                    for t in range(TILES):
                        last = nc.tensor.transpose(B[FFN_BACK][:, t * P:(t + 1) * P], y_hat[:, t * P:(t + 1) * P], g.ident[:])
                    last.then_inc(q["ffn_back"], 1)
                    pe.wait_ge(ffn_loaded, layer * FFN_LOADS)
                    pe.wait_ge(q["xn_ready"], of_seq(n, "xn_ready"))
                    for i, (h0, hn) in enumerate(HCH):
                        if i == 1 and more:
                            pe.wait_ge(q["masked"], of_tile(n + 1, "masked", 0, 2))
                        if i == 2:
                            pe.wait_ge(q["gelu_done"], of_seq(n, "gelu_done", 1))
                        nc.tensor.matmul(B[FFN_GATE[i]][0:hn, :], w1[:, HIDDEN + h0:HIDDEN + h0 + hn], xn[:], start=True, stop=True).then_inc(q["gate_done"], 1)
                        if i == 2:
                            pe.wait_ge(q["prod_ready"], of_seq(n, "prod_ready", 1))
                        nc.tensor.matmul(B[FFN_A[i]][0:hn, :], w1[:, h0:h0 + hn], xn[:], start=True, stop=True).then_inc(q["a_done"], 1)
                    for i, (h0, hn) in enumerate(HCH):
                        pe.wait_ge(q["prod_ready"], of_seq(n, "prod_ready", max(i + 1, 2)))
                        last = nc.tensor.matmul(B[FFN_OUT][:], w2[0:hn, i, :], gates[0:hn, i, :], start=(i == 0), stop=(i == 2))
                    last.then_inc(q["w2_done"], 1)
                    if switch:
                        pe.wait_ge(v_split, layer + 2)
                        pe.sem_inc(wait_taken, 1)

                pe.wait_ge(qk_split, 1)
                project_qk(1, 0)
                turn_qk(1, 0)
                project_qk(1, 1)
                make_scores(1, 0, 0)
                pe.wait_ge(v_split, 2)
                pe.sem_inc(wait_taken, 1)
                with pe.Fori(1, LAYERS) as layer:
                    with pe.Fori(1, SEQS) as s:
                        sequence(layer, pe.snap(layer * SEQS + (s - SEQS)), True)
                    sequence(layer, layer * SEQS, True, switch=True)
                with pe.Fori(1, SEQS) as s:
                    sequence(LAYERS, pe.snap(s + (LAYERS - 1) * SEQS), True)
                sequence(LAYERS, LAYERS * SEQS, False)

            @block.scalar
            def _(act):
                norm.scalar(act)
                credit(act, ACT_MADE)
                act.wait_ge(pads_ready, 3)

                def square(n, t):
                    for i in range(4):
                        act.wait_ge(q["qk_projected"], of_tile(n, "qk_projected", t, i + 1))
                        if i % 2 == 0:
                            act.wait_ge(q["rotated"], of_tile(n, "rotated", t - 1, i // 2 + 1))
                        nc.scalar.activation(squares[:, i * 512:(i + 1) * 512], A[i][:], ACT.Square).then_inc(q["squared"], 1)

                def copy_qk(n, t):
                    for i in range(4):
                        act.wait_ge(q["qk_turned"], of_tile(n, "qk_turned", t, i + 1))
                        src = A[i][:].rearrange("p (c t) -> p c t", t=P)
                        c0 = BACK + t % TILES * P
                        dst = q_t[:, 4 * i:4 * i + 4, :] if i < 2 else k_t[:, 4 * i - 8:4 * i - 4, c0:c0 + P]
                        nc.scalar.copy(dst, src).then_inc(q["qkt_copied"], 1)

                def copy_v(n, t):
                    for i in range(4):
                        act.wait_ge(q["v_projected"], of_tile(n, "v_projected", t, i + 1))
                        nc.scalar.copy(vals[:, i // 2, 8 * (i % 2):8 * (i % 2) + 8, 0:HD],
                                       B[s_banks(t)[i]][0:WIN, :].rearrange("p (h d) -> p h d", d=HD)).then_inc(q["v_copied"], 1)

                def copy_out(n, t, banks):
                    for i in range(2):
                        act.wait_ge(q["out_turned"], of_tile(n, "out_turned", t, i + 1))
                        nc.scalar.copy(att_t[:, 4 * i:4 * i + 4, :], B[banks[i]][:].rearrange("p (c t) -> p c t", t=P)).then_inc(q["out_copied"], 1)

                def shift_output(n, t):
                    c0, c1 = t * P, (t + 1) * P
                    act.wait_ge(q["y_added"], of_tile(n, "y_added", t, 1))
                    nc.scalar.copy(y1s[0:HD, c0:c1], y1[0:HD, c0:c1])
                    return nc.scalar.copy(y1s[HD:P, c0 + 1:min(c1 + 1, TOKENS)], y1[HD:P, c0:min(c1, TOKENS - 1)])

                def exponentials(n, t, half):
                    act.wait_ge(q["centred"], of_tile(n, "centred", t, half + 1))
                    nc.scalar.activation(scores[:, 8 * half:8 * half + 8, :], scores[:, 8 * half:8 * half + 8, :], ACT.Exp).then_inc(q["exp_done"], 1)

                def read_head(n, s):
                    act.sem_inc(wait_taken, 1)
                    nc.scalar.copy(head_hi[0:HD, :], y_of(s, 0, P, rows=slice(0, HD)))
                    nc.scalar.copy(head_hi[HD:P, 1:], y_of(s, 0, P - 1, rows=slice(HD, P))).then_inc(q["head_hi_ready"], 1)

                def read_sequence(n, s):
                    act.sem_inc(wait_taken, 1)
                    nc.scalar.copy(ys_hi[0:HD, BACK:], y_of(s, rows=slice(0, HD)))
                    nc.scalar.copy(ys_hi[HD:P, BACK + 1:], y_of(s, 0, TOKENS - 1, rows=slice(HD, P))).then_inc(q["ys_hi_ready"], 1)

                def sequence(layer, n, following):
                    more = following is not None
                    for t in range(TILES):
                        ahead = t + 1 < TILES or more
                        if ahead and t:
                            square(n, t + 1)
                        exponentials(n, t, 0)
                        copy_v(n, t)
                        if t:
                            copy_out(n, t - 1, s_banks(t))
                        exponentials(n, t, 1)
                        if t == 1 and more:
                            act.wait_ge(q["head_ready"], of_seq(n, "head_ready"))
                            read_head(n + 1, following)
                        if t + 1 == TILES and more:
                            act.wait_ge(q["ys_ready"], of_seq(n, "ys_ready"))
                            read_sequence(n + 1, following)
                        for i in range(GROUPS):
                            act.wait_ge(q["probs_turned"], of_tile(n, "probs_turned", t, i + 1))
                            nc.scalar.copy(probs_t[:, HPG * i:HPG * (i + 1), :], A[i][0:WIN, :].rearrange("p (h t) -> p h t", t=P)).then_inc(q["probs_t_ready"], 1)
                        if t:
                            shift_output(n, t - 1)
                        if ahead:
                            copy_qk(n, t + 1)
                    if more:
                        square(n + 1, 1)
                    copy_out(n, TILES - 1, LAST_OUT)

                    shift_output(n, TILES - 1).then_inc(q["y1s_ready"], 1)
                    nc.scalar.activation(table_pick[:, 1:2], table_pick[:, 0:1], ACT.Gelu)
                    act.wait_ge(ffn_loaded, layer * FFN_LOADS)
                    act.wait_ge(q["ffn_back"], of_seq(n, "ffn_back"))
                    nc.scalar.activation(xn[:], B[FFN_BACK][:], ACT.Identity, bias=ln[:, 1:2], scale=ln[:, 0:1]).then_inc(q["xn_ready"], 1)
                    for i, (h0, hn) in enumerate(HCH):
                        act.wait_ge(q["gate_done"], of_seq(n, "gate_done", i + 1))
                        nc.scalar.activation(gates[0:hn, i, :], B[FFN_GATE[i]][0:hn, :], ACT.Gelu, bias=b1[0:hn, 3 + i:4 + i]).then_inc(q["gelu_done"], 1)
                    nc.scalar.activation(table_pick[:, 1:2], table_pick[:, 0:1], ACT.Exp)

                read_head(1, 1)
                read_sequence(1, 1)
                square(1, 0)
                copy_qk(1, 0)
                square(1, 1)
                act.sem_inc(wait_taken, 1)
                with act.Fori(1, LAYERS) as layer:
                    with act.Fori(1, SEQS) as s:
                        sequence(layer, act.snap(layer * SEQS + (s - SEQS)), s + 1)
                    sequence(layer, layer * SEQS, 1)
                with act.Fori(1, SEQS) as s:
                    sequence(LAYERS, act.snap(s + (LAYERS - 1) * SEQS), s + 1)
                sequence(LAYERS, LAYERS * SEQS, None)

            @block.gpsimd
            def _(pool):
                norm.gpsimd(pool)
                nc.gpsimd.memset(k_t[:, :, 0:BACK], 0.0)
                nc.gpsimd.memset(vals[:, :, :, HD:HD + 1], 1.0).then_inc(pads_ready, 1)
                credit(pool, POOL_MADE)

                def read_head(n, s):
                    pool.wait_ge(q["head_hi_ready"], of_seq(n, "head_hi_ready"))
                    pool.sem_inc(wait_taken, 1)
                    nc.gpsimd.tensor_tensor(head_lo[0:HD, :], y_of(s, 0, P, rows=slice(0, HD)), head_hi[0:HD, :].bitcast(F32), ALU.subtract)
                    nc.gpsimd.tensor_tensor(head_lo[HD:P, 1:], y_of(s, 0, P - 1, rows=slice(HD, P)), head_hi[HD:P, 1:].bitcast(F32),
                                            ALU.subtract).then_inc(q["head_ready"], 1)
                    pool.wait_ge(q["head_ready"], of_seq(n, "head_ready"))

                def read_sequence(n, s):
                    pool.wait_ge(q["ys_hi_ready"], of_seq(n, "ys_hi_ready"))
                    pool.sem_inc(wait_taken, 1)
                    nc.gpsimd.tensor_tensor(ys_lo[0:HD, BACK:], y_of(s, rows=slice(0, HD)), ys_hi[0:HD, BACK:].bitcast(F32), ALU.subtract)
                    nc.gpsimd.tensor_tensor(ys_lo[HD:P, BACK + 1:], y_of(s, 0, TOKENS - 1, rows=slice(HD, P)), ys_hi[HD:P, BACK + 1:].bitcast(F32),
                                            ALU.subtract).then_inc(q["ys_ready"], 1)
                    pool.wait_ge(q["ys_ready"], of_seq(n, "ys_ready"))

                def invert_norms(n, t):
                    for a in range(2):
                        cols = slice(a * HEADS, (a + 1) * HEADS)
                        pool.wait_ge(q["norms_guarded"], of_tile(n, "norms_guarded", t, a + 1))
                        nc.gpsimd.tensor_tensor(inv_norm[:, cols], norm2c[:, cols], g.minus_half[:, cols], ALU.pow).then_inc(q["inv_norms_ready"], 1)

                def sine_products(n, t):
                    for a in range(2):
                        pool.wait_ge(q["qk_normed"], of_tile(n, "qk_normed", t, 2 * a + 2))
                        for half in range(2 - a):
                            last = sine_product(nc.gpsimd, t, a, half)
                        last.then_inc(q["sin_ready"], 1)

                def sequence(n, following):
                    more = following is not None
                    for t in range(TILES):
                        if t + 1 < TILES or more:
                            if t:
                                invert_norms(n, t + 1)
                            sine_products(n, t + 1)
                        if t == 1 and more:
                            pool.wait_ge(q["sin_ready"], of_tile(n, "sin_ready", t + 1, 2))
                            read_head(n + 1, following)
                    if more:
                        pool.wait_ge(q["sin_ready"], of_tile(n, "sin_ready", TILES, 2))
                        read_sequence(n + 1, following)
                    if more:
                        invert_norms(n + 1, 1)
                    pool.wait_ge(q["var_ready"], of_seq(n, "var_ready"))
                    nc.gpsimd.tensor_tensor(rstd[:], var_eps[:], g.minus_half[:, 0:TILES], ALU.pow).then_inc(q["rstd_ready"], 1)

                read_head(1, 1)
                read_sequence(1, 1)
                invert_norms(1, 0)
                sine_products(1, 0)
                invert_norms(1, 1)
                pool.sem_inc(wait_taken, 1)
                with pool.Fori(1, LAYERS) as layer:
                    with pool.Fori(1, SEQS) as s:
                        sequence(pool.snap(layer * SEQS + (s - SEQS)), s + 1)
                    sequence(layer * SEQS, 1)
                with pool.Fori(1, SEQS) as s:
                    sequence(pool.snap(s + (LAYERS - 1) * SEQS), s + 1)
                sequence(LAYERS * SEQS, None)

            @block.vector
            def _(dve):
                norm.vector(dve)
                nc.vector.memset(ys_hi[:].bitcast(F32), 0.0).then_inc(pads_ready, 1)
                nc.vector.memset(ys_lo[:].bitcast(F32), 0.0)
                nc.vector.memset(head_hi[:].bitcast(F32), 0.0)
                nc.vector.memset(head_lo[:].bitcast(F32), 0.0)
                nc.vector.memset(table_pick[:], 0.0)
                nc.vector.memset(y1s[:], 0.0).then_inc(pads_ready, 1)
                credit(dve, DVE_MADE)
                dve.sem_inc(v_split, 1)
                dve.wait_ge(consts_loaded, CONST_LOADS)

                def sum_squares(n, t):
                    for a in range(2):
                        for i in (2 * a, 2 * a + 1):
                            dve.wait_ge(q["squared"], of_tile(n, "squared", t, i + 1))
                            last = nc.vector.tensor_reduce(norm2[:, 8 * i:8 * i + 8], squares[:, i * 512:(i + 1) * 512].rearrange("p (h d) -> p h d", d=HD), AX, ALU.add)
                        last.then_inc(q["norms_ready"], 1)
                        dve.wait_ge(q["norms_ready"], of_tile(n, "norms_ready", t, a + 1))
                        cols = slice(a * HEADS, (a + 1) * HEADS)
                        nc.vector.tensor_scalar(norm2c[:, cols], norm2[:, cols], 1e-24, None, ALU.max).then_inc(q["norms_guarded"], 1)

                def normalise(n, t, part=range(4)):
                    for i in part:
                        if i % 2 == 0:
                            dve.wait_ge(q["inv_norms_ready"], of_tile(n, "inv_norms_ready", t, i // 2 + 1))
                        nc.vector.tensor_tensor(normed[:, i * 512:(i + 1) * 512].rearrange("p (h d) -> p h d", d=HD), A[i][:].rearrange("p (h d) -> p h d", d=HD),
                                                inv_norm[:, 8 * i:8 * i + 8].unsqueeze(2).to_broadcast([P, 8, HD]), ALU.mult).then_inc(q["qk_normed"], 1)

                def cosine_products(n, t):
                    for a in range(2):
                        dve.wait_ge(q["qk_normed"], of_tile(n, "qk_normed", t, 2 * a + 2))
                        dve.wait_ge(q["qk_turned"], of_tile(n, "qk_turned", t - 1, 2 * a + 2))
                        last = nc.vector.tensor_tensor(of_heads(rot, a), of_heads(normed, a), table[:, t % TILES, 2 * a, :].unsqueeze(1).to_broadcast([P, HEADS, HD]), ALU.mult)
                        if a:
                            last = sine_product(nc.vector, t, 1, 1)
                        last.then_inc(q["cos_ready"], 1)

                def add_rotated(n, t):
                    for a in range(2):
                        dve.wait_ge(q["cos_ready"], of_tile(n, "cos_ready", t, a + 1))
                        dve.wait_ge(q["sin_ready"], of_tile(n, "sin_ready", t, a + 1))
                        nc.vector.tensor_tensor(of_heads(rot, a), of_heads(rot, a), of_heads(squares, a), ALU.add).then_inc(q["rotated"], 1)

                def mask(n, t, half):
                    for i in (2 * half, 2 * half + 1):
                        dve.wait_ge(q["scores_done"], of_tile(n, "scores_done", t, i + 1))
                        src = B[s_banks(t)[i]][:, 0:HPG * WIN].rearrange("p (h k) -> p h k", k=WIN)
                        nc.vector.tensor_tensor(scores[:, HPG * i:HPG * (i + 1), :], src, band[:, min(t, 1), :].unsqueeze(1).to_broadcast([P, HPG, WIN]),
                                                ALU.add).then_inc(q["masked"], 1)

                def centre(n, t, half):
                    rows = scores[:, 8 * half:8 * half + 8, :]
                    dve.wait_ge(q["masked"], of_tile(n, "masked", t, 2 * half + 2))
                    nc.vector.tensor_reduce(top[:, 8 * half:8 * half + 8], rows, AX, ALU.max).then_inc(q["max_ready"], 1)
                    dve.wait_ge(q["max_ready"], of_tile(n, "max_ready", t, half + 1))
                    nc.vector.tensor_tensor(rows, rows, top[:, 8 * half:8 * half + 8].unsqueeze(2).to_broadcast([P, 8, WIN]), ALU.subtract).then_inc(q["centred"], 1)

                def divide(n, t):
                    for i, (h0, h1) in enumerate(PV_HEADS):
                        dve.wait_ge(q["pv_done"], of_tile(n, "pv_done", t, i + 1))
                        src = B[pv_banks(t)[i]][:, 0:(h1 - h0) * (HD + 1)].rearrange("p (h d) -> p h d", d=HD + 1)
                        last = nc.vector.reciprocal(inv_sum[:, h0:h1].unsqueeze(2), src[:, :, HD:HD + 1])
                    last.then_inc(q["sums_inverted"], 1)
                    dve.wait_ge(q["sums_inverted"], of_tile(n, "sums_inverted", t, 1))
                    dve.wait_ge(q["out_turned"], of_tile(n, "out_turned", t - 1, 2))
                    for i, (h0, h1) in enumerate(PV_HEADS):
                        src = B[pv_banks(t)[i]][:, 0:(h1 - h0) * (HD + 1)].rearrange("p (h d) -> p h d", d=HD + 1)
                        nc.vector.tensor_tensor(att[:, h0 * HD:h1 * HD].rearrange("p (h d) -> p h d", d=HD), src[:, :, 0:HD],
                                                inv_sum[:, h0:h1].unsqueeze(2).to_broadcast([P, h1 - h0, HD]), ALU.mult).then_inc(q["att_ready"], 1)

                def add_output(n, s, t, bank):
                    dve.wait_ge(q["wo_done"], of_tile(n, "wo_done", t, 1))
                    nc.vector.tensor_tensor(y1[:, t * P:(t + 1) * P], B[bank][:, 0:P], y_of(s, t * P, (t + 1) * P), ALU.add).then_inc(q["y_added"], 1)

                def scale_tables(layer):
                    for a in range(2):
                        def scale_of(cols, width):
                            return scales[:, a, bass.ds(layer - 1, 1), cols].to_broadcast([P, TILES, width])
                        nc.vector.tensor_tensor(table[:, :, 2 * a, :], base[:, :, 2 * a, :], scale_of(slice(0, 64), 64), ALU.mult)
                        nc.vector.tensor_tensor(table[:, :, 2 * a + 1, 0:32], base[:, :, 2 * a + 1, 0:32], scale_of(slice(32, 64), 32), ALU.mult)
                        last = nc.vector.tensor_tensor(table[:, :, 2 * a + 1, 32:64], base[:, :, 2 * a + 1, 32:64], scale_of(slice(0, 32), 32), ALU.mult)
                    last.then_inc(tables_ready, 1)
                    dve.wait_ge(tables_ready, layer)
                    dve.sem_inc(wait_taken, 1)

                def split_weights(c0, c1, nth):
                    nc.vector.tensor_copy(wqkv_hi[:, c0:c1], stage[:, c0:c1]).then_inc(split_hi, 1)
                    dve.wait_ge(split_hi, nth)
                    return nc.vector.tensor_tensor(wqkv_lo[:, c0:c1], stage[:, c0:c1], wqkv_hi[:, c0:c1].bitcast(F32), ALU.subtract)

                def sequence(layer, n, s, more, switch=False):
                    for t in range(TILES):
                        ahead = t + 1 < TILES or more
                        if ahead and t:
                            sum_squares(n, t + 1)
                        if t:
                            mask(n, t, 0)
                            centre(n, t, 0)
                        mask(n, t, 1)
                        if ahead and t:
                            normalise(n, t + 1, (0, 1))
                        centre(n, t, 1)
                        if ahead:
                            if t:
                                normalise(n, t + 1, (2, 3))
                            cosine_products(n, t + 1)
                        if t:
                            add_output(n, s, t - 1, s_banks(t)[2])
                        if ahead:
                            add_rotated(n, t + 1)
                        divide(n, t)
                        if switch and t == TILES - 2:
                            scale_tables(layer + 1)
                            dve.wait_ge(wqkv_loaded, (layer + 1) * 16)
                            split_weights(0, 2 * INNER, layer * 2 + 1).then_inc(qk_split, 1)
                        if switch and t == TILES - 1:
                            split_weights(2 * INNER, 3 * INNER, layer * 2 + 2).then_inc(v_split, 1)
                    if more:
                        sum_squares(n + 1, 1)
                    add_output(n, s, TILES - 1, LAST_OUT[2])

                    dve.wait_ge(q["ffn_turned"], of_seq(n, "ffn_turned"))
                    for t in range(TILES):
                        last = nc.vector.bn_stats(stats[:, t, :], B[FFN_TURN][:, t * P:(t + 1) * P])
                    last.then_inc(q["stats_ready"], 1)
                    dve.wait_ge(q["stats_ready"], of_seq(n, "stats_ready"))
                    dve.sem_inc(wait_taken, 1)
                    for t in range(TILES):
                        last = nc.vector.bn_aggr(mean_var[:, t, :], stats[:, t, :])
                    last.then_inc(q["aggregated"], 1)
                    dve.wait_ge(q["aggregated"], of_seq(n, "aggregated"))
                    nc.vector.tensor_scalar(var_eps[:], mean_var[:, :, 1], LN_EPS, None, ALU.add).then_inc(q["var_ready"], 1)
                    dve.wait_ge(q["rstd_ready"], of_seq(n, "rstd_ready"))
                    for t in range(TILES):
                        last = nc.vector.tensor_scalar(y_hat[:, t * P:(t + 1) * P], B[FFN_TURN][:, t * P:(t + 1) * P], mean_var[:, t, 0:1], rstd[:, t:t + 1],
                                                       ALU.subtract, ALU.mult)
                    last.then_inc(q["y_hat_ready"], 1)
                    if more:
                        mask(n + 1, 0, 0)
                        centre(n + 1, 0, 0)
                        normalise(n + 1, 1)
                    dve.wait_ge(ffn_loaded, layer * FFN_LOADS)
                    for i, (h0, hn) in enumerate(HCH):
                        dve.wait_ge(q["gelu_done"], of_seq(n, "gelu_done", i + 1))
                        dve.wait_ge(q["a_done"], of_seq(n, "a_done", i + 1))
                        nc.vector.scalar_tensor_tensor(gates[0:hn, i, :], B[FFN_A[i]][0:hn, :], b1[0:hn, i:i + 1], gates[0:hn, i, :],
                                                       ALU.add, ALU.mult).then_inc(q["prod_ready"], 1)
                    dve.wait_ge(q["w2_done"], of_seq(n, "w2_done"))
                    nc.vector.scalar_tensor_tensor(y_of(s), B[FFN_OUT][:], ln[:, 2:3], y1[:], ALU.add, ALU.add).then_inc(q["seq_done"], 1)

                scale_tables(1)
                dve.wait_ge(wqkv_loaded, 16)
                split_weights(0, 2 * INNER, 1).then_inc(qk_split, 1)
                split_weights(2 * INNER, 3 * INNER, 2).then_inc(v_split, 1)
                sum_squares(1, 0)
                normalise(1, 0)
                cosine_products(1, 0)
                add_rotated(1, 0)
                sum_squares(1, 1)
                normalise(1, 1)
                mask(1, 0, 0)
                centre(1, 0, 0)
                dve.sem_inc(wait_taken, 1)
                with dve.Fori(1, LAYERS) as layer:
                    with dve.Fori(1, SEQS) as s:
                        sequence(layer, dve.snap(layer * SEQS + (s - SEQS)), s, True)
                    sequence(layer, layer * SEQS, SEQS, True, switch=True)
                with dve.Fori(1, SEQS) as s:
                    sequence(LAYERS, dve.snap(s + (LAYERS - 1) * SEQS), s, True)
                sequence(LAYERS, LAYERS * SEQS, SEQS, False)

    run_phase(nc, name, body)


def add_back_phase(nc, g, name):

    def body(ph):
        xs = ph.sb("xs", [P, 2, TOKENS])
        turned = [ph.ps(f"turned{i}", [P, TOKENS]) for i in range(2)]
        xs_ready, done, added = ph.sem("xs_ready"), ph.sem("turned_ready"), ph.sem("added")
        PAIRS = SEQS // 2

        with nc.Block() as block:

            @block.scalar
            def _(act):
                with act.Fori(1, PAIRS + 1) as pair:
                    for i in range(2):
                        act.wait_ge(done, (pair - 1) * 2 + (i + 1))
                        nc.scalar.copy(xs[:, i], g.XH[:, bass.ds(pair * 2 + (i - 2), 1), :].rearrange("p a t -> p (a t)")).then_inc(xs_ready, 1)

            @block.tensor
            def _(pe):
                pe.sem_inc(done, 2)
                with pe.Fori(1, PAIRS + 1) as pair:
                    for i in range(2):
                        pe.wait_ge(xs_ready, (pair - 1) * 2 + (i + 1))
                        pe.wait_ge(added, (pair - 1) * 2 + (i + 1))
                        for t in range(TILES):
                            last = nc.tensor.transpose(turned[i][:, t * P:(t + 1) * P], xs[:, i, t * P:(t + 1) * P], g.ident[:])
                        last.then_inc(done, 1)

            @block.vector
            def _(dve):
                dve.sem_inc(added, 2)
                with dve.Fori(1, PAIRS + 1) as pair:
                    for i in range(2):
                        dve.wait_ge(done, pair * 2 + (i + 1))
                        xt = g.X[:, bass.ds(pair * 2 + (i - 2), 1), :].rearrange("p a t -> p (a t)")
                        nc.vector.tensor_tensor(xt, xt, turned[i][:], ALU.add).then_inc(added, 1)

    run_phase(nc, name, body)


def delta_rule_phase(nc, g, name, w):
    PAIRS, CHUNK, LEVELS = SEQS // 2, 64, 6
    CHUNKS = TOKENS // CHUNK

    def body(ph):
        wwrite = ph.sb("wwrite", [P, P])
        wwrite_t = ph.sb("wwrite_t", [P, P])
        wout = ph.sb("wout", [P, P])
        wout_t = ph.sb("wout_t", [P, P])
        wgates = ph.sb("wgates", [P, 3])
        dt_bias = ph.sb("dt_bias", [P, 1])
        a_log = ph.sb("a_log", [P, 1])
        rate = ph.sb("rate", [P, 1])
        until = ph.sb("until", [P, P])
        within = ph.sb("within", [P, P])
        ends = ph.sb("ends", [P, 2])
        ceiling = ph.sb("ceiling", [P, P])
        corner = ph.sb("corner", [P, LEVELS, P])
        big = {n: ph.sb(n, [P, 2, TOKENS]) for n in (
            "xs", "xt", "rk", "wk", "wkb", "vb", "rkd", "wkbd", "wkdw", "wkb_t", "rkd_t", "decayed", "m_t", "attn_t",
            "t1", "inv", "inv_t", "vp", "wkcd_t", "v_new", "o_t", "y")}
        off_t = ph.sb("off_t", [P, 2, LEVELS, TOKENS])
        keys_t = ph.sb("keys_t", [P, 2, TOKENS + 1])
        state = ph.sb("state", [P, 2, P])
        sm = {n: ph.sb(n, [P, 2, TILES]) for n in ("norm2", "norm2c", "inv_norm", "u", "abs_u", "e_u", "ln_u", "sp", "decay", "dec", "to_end", "e_dec", "e_to_end")}
        e_gates = ph.sb("e_gates", [P, 2, TILES, 2])
        e_gates1 = ph.sb("e_gates1", [P, 2, TILES, 2])
        gates = ph.sb("gates", [P, 2, TILES, 2])
        carry = ph.sb("carry", [P, 2, CHUNKS])
        bank = [[ph.ps(f"bank{i}{k}", [P, TOKENS]) for k in range(4)] for i in range(2)]

        pe_made = ["x_turned", "z_done", "v_done", "rk_turned", "decs_done", "dec_rows_done", "wk_turned", "wkb_turned", "rkd_turned",
                   "gram_done", "attn_done", "t1_done", "u_done", "ut_done", "vp_done", "wkcd_done", "vs_done", "update_done", "o_done", "out_done"]
        act_made = ["xs_ready", "xt_ready", "e_gates_ready", "abs_ready", "e_u_ready", "ln_ready", "rk_t_ready", "dec_ready", "e_dec_ready", "carry_ready",
                    "e_to_end_ready", "decayed_ready", "wk_ready", "wkb_t_ready", "rkd_t_ready", "t1_ready", "vp_ready", "wkcd_ready", "o_ready"]
        dve_made = ["squares_ready", "norm2_ready", "norm2c_ready", "rk_ready", "e_gates1_ready", "gates_ready", "u_ready", "sp_ready", "sp_sum_ready", "decay_ready",
                    "to_end_ready", "floor_ready", "wkb_ready", "vb_ready", "m_ready", "attn_ready", "inv_ready", "inv_t_ready",
                    "v_new_ready", "state_ready", "y_ready", "x_added"]
        pool_made = ["inv_norm_ready", "rkd_ready", "wkbd_ready", "wkdw_ready", "off_ready"]
        count = {k: 1 for k in pe_made + act_made + dve_made + pool_made}
        count.update(t1_done=LEVELS, t1_ready=LEVELS - 1, u_done=LEVELS - 2, ut_done=LEVELS - 1, inv_ready=LEVELS, inv_t_ready=LEVELS, off_ready=LEVELS,
                     vs_done=CHUNKS, update_done=CHUNKS, v_new_ready=CHUNKS, state_ready=CHUNKS + 1)
        q = {k: [ph.sem(f"{k}{i}") for i in range(2)] for k in ("t1_done", "t1_ready", "u_done", "ut_done", "inv_ready", "inv_t_ready", "off_ready",
                                                                 "vs_done", "update_done", "v_new_ready", "state_ready")}
        q.update({k: ph.sem(k) for k in count if k not in q})
        loaded, weights_turned, weights_ready, rate_ready, pads_ready, wait_taken = (
            ph.sem(k) for k in ("loaded", "weights_turned", "weights_ready", "rate_ready", "pads_ready", "wait_taken"))
        LOADS = 16 * 12

        def credit(eng, made):
            for k in made:
                if isinstance(q[k], list):
                    for one in q[k]:
                        eng.sem_inc(one, count[k])
                else:
                    eng.sem_inc(q[k], 2)

        def wait(eng, pair, key, i, k=1):
            if isinstance(q[key], list):
                eng.wait_ge(q[key][i], pair * count[key] + k)
            else:
                eng.wait_ge(q[key], pair * 2 + (i + 1))

        def done(ins, key, i):
            ins.then_inc(q[key][i] if isinstance(q[key], list) else q[key], 1)

        def tiled(buf, i):
            return buf[:, i].rearrange("p (t d) -> p t d", d=P)

        def banked(i, k):
            return bank[i][k][:].rearrange("p (t d) -> p t d", d=P)

        def spread(col):
            return col.unsqueeze(2).to_broadcast([P, TILES, P])

        def every(table):
            return table.unsqueeze(1).to_broadcast([P, TILES, P])

        def seq_of(buf, pair, i, c0=0, c1=TOKENS):
            return buf[:, bass.ds(pair * 2 + (i - 2), 1), c0:c1].rearrange("p a t -> p (a t)")

        cols = [slice(t * P, (t + 1) * P) for t in range(TILES)]

        norm = Normaliser(nc, ph, g, (bank[0][0], bank[1][0]), big["y"][:])

        with nc.Block() as block:

            @block.sync
            def _(sp):
                for dst, src in ((wwrite[:], w["W_write"]), (wout[:], w["W_out"]), (wgates[:, 0:1], w["W_gate"].rearrange("a d -> d a")),
                                 (wgates[:, 1:2], w["W_beta"].rearrange("a d -> d a")), (wgates[:, 2:3], w["W_alpha"].rearrange("a d -> d a")),
                                 (dt_bias[:], w["dt_bias"].partition_broadcast(P)), (a_log[:], w["A_log"].partition_broadcast(P)),
                                 (until[:], w["until"]), (within[:], w["within"]), (ends[:], w["ends"]), (ceiling[:], w["ceiling"]),
                                 (corner[:], w["corner"])):
                    sp.dma_start(dst, src).then_inc(loaded, 16)

            @block.tensor
            def _(pe):
                norm.tensor(pe)
                credit(pe, pe_made)
                pe.wait_ge(loaded, LOADS)
                nc.tensor.transpose(bank[0][0][:, 0:P], wwrite[:], g.ident[:])
                nc.tensor.transpose(bank[0][0][:, P:2 * P], wout[:], g.ident[:]).then_inc(weights_turned, 1)
                pe.wait_ge(weights_ready, 1)
                pe.wait_ge(pads_ready, 1)
                with pe.Fori(1, PAIRS + 1) as pair:

                    def products(i, k, lhs, rhs, key):
                        for t in range(TILES):
                            last = nc.tensor.matmul(bank[i][k][:, cols[t]], lhs(t), rhs(t), start=True, stop=True)
                        done(last, key, i)

                    def turns(i, k, src, key):
                        for t in range(TILES):
                            last = nc.tensor.transpose(bank[i][k][:, cols[t]], src(t), g.ident[:])
                        done(last, key, i)

                    for i in range(2):
                        wait(pe, pair, "xs_ready", i)
                        wait(pe, pair - 1, "x_added", i)
                        turns(i, 0, lambda t: big["xs"][:, i, cols[t]], "x_turned")
                        for t in range(TILES):
                            last = nc.tensor.matmul(bank[i][1][:, 3 * t:3 * t + 3], big["xs"][:, i, cols[t]], wgates[:], start=True, stop=True)
                        done(last, "z_done", i)
                        products(i, 2, lambda t: big["xs"][:, i, cols[t]], lambda t: wwrite_t[:], "v_done")
                    for i in range(2):
                        wait(pe, pair, "rk_ready", i)
                        turns(i, 3, lambda t: big["rk"][:, i, cols[t]], "rk_turned")
                    for i in range(2):
                        wait(pe, pair, "decay_ready", i)
                        nc.tensor.matmul(bank[i][1][:, 16:20], until[:], sm["decay"][:, i], start=True, stop=True)
                        nc.tensor.matmul(bank[i][1][:, 20:24], within[:], sm["decay"][:, i], start=True, stop=True)
                        for t in range(TILES):
                            last = nc.tensor.matmul(bank[i][1][:, 24 + 2 * t:26 + 2 * t], sm["decay"][:, i, t:t + 1].to_broadcast([P, P]), ends[:],
                                                    start=True, stop=True)
                        done(last, "decs_done", i)
                        wait(pe, pair, "xt_ready", i)
                        products(i, 0, lambda t: sm["decay"][:, i, t:t + 1].to_broadcast([P, P]), lambda t: until[:], "dec_rows_done")
                    for i in range(2):
                        wait(pe, pair, "rk_t_ready", i)
                        turns(i, 3, lambda t: keys_t[:, i, t * P:(t + 1) * P], "wk_turned")
                    for i in range(2):
                        wait(pe, pair, "rkd_ready", i)
                        wait(pe, pair, "vb_ready", i)
                        turns(i, 2, lambda t: big["rkd"][:, i, cols[t]], "rkd_turned")
                        wait(pe, pair, "wkb_ready", i)
                        wait(pe, pair, "e_to_end_ready", i)
                        wait(pe, pair, "carry_ready", i)
                        turns(i, 1, lambda t: big["wkb"][:, i, cols[t]], "wkb_turned")
                    for i in range(2):
                        wait(pe, pair, "floor_ready", i)
                        products(i, 0, lambda t: keys_t[:, i, t * P:(t + 1) * P], lambda t: keys_t[:, i, t * P + 1:(t + 1) * P + 1], "attn_done")
                        wait(pe, pair, "wkb_t_ready", i)
                        products(i, 3, lambda t: keys_t[:, i, t * P:(t + 1) * P], lambda t: big["wkb_t"][:, i, cols[t]], "gram_done")
                    for level in range(LEVELS):
                        for i in range(2):
                            wait(pe, pair, "off_ready", i, level + 1)
                            if level == 0:
                                wait(pe, pair, "attn_ready", i)
                                wait(pe, pair, "m_ready", i)
                                products(i, 0, lambda t: off_t[:, i, 0, cols[t]], lambda t: g.ident[:], "t1_done")
                                continue
                            wait(pe, pair, "inv_ready", i, level)
                            products(i, 0, lambda t: off_t[:, i, level, cols[t]], lambda t: big["inv"][:, i, cols[t]], "t1_done")
                        if level == 0:
                            continue
                        for i in range(2):
                            wait(pe, pair, "t1_ready", i, level)
                            wait(pe, pair, "inv_t_ready", i, level)
                            if level < LEVELS - 1:
                                products(i, 1, lambda t: big["inv_t"][:, i, cols[t]], lambda t: big["t1"][:, i, cols[t]], "u_done")
                            if level == 1:
                                wait(pe, pair, "rkd_t_ready", i)
                            products(i, 2, lambda t: big["t1"][:, i, cols[t]], lambda t: big["inv_t"][:, i, cols[t]], "ut_done")
                    for i in range(2):
                        wait(pe, pair, "inv_t_ready", i, LEVELS)
                        products(i, 0, lambda t: big["inv_t"][:, i, cols[t]], lambda t: big["vb"][:, i, cols[t]], "vp_done")
                        wait(pe, pair, "wkbd_ready", i)
                        products(i, 1, lambda t: big["wkbd"][:, i, cols[t]], lambda t: big["inv_t"][:, i, cols[t]], "wkcd_done")
                    for c in range(CHUNKS):
                        t, rows, own = c // 2, slice(CHUNK * (c % 2), CHUNK * (c % 2) + CHUNK), slice(c * CHUNK, (c + 1) * CHUNK)
                        for i in range(2):
                            if c == 0:
                                wait(pe, pair, "wkcd_ready", i)
                                wait(pe, pair, "vp_ready", i)
                            wait(pe, pair, "state_ready", i, c + 1)
                            done(nc.tensor.matmul(bank[i][2][rows, 0:P], big["wkcd_t"][:, i, own], state[:, i], start=True, stop=True), "vs_done", i)
                            nc.tensor.matmul(bank[i][3][:, own], state[:, i], big["rkd_t"][:, i, own], start=True, stop=False)
                        for i in range(2):
                            wait(pe, pair, "v_new_ready", i, c + 1)
                            if c == 0:
                                wait(pe, pair, "wkdw_ready", i)
                            last = nc.tensor.matmul(bank[i][3][:, own], big["v_new"][rows, i, cols[t]], big["attn_t"][rows, i, own], start=False, stop=True)
                            if c == CHUNKS - 1:
                                done(last, "o_done", i)
                            done(nc.tensor.matmul(bank[i][0][:, 0:P], big["wkdw"][rows, i, cols[t]], big["v_new"][rows, i, cols[t]], start=True, stop=True), "update_done", i)
                    for i in range(2):
                        wait(pe, pair, "o_ready", i)
                        products(i, 1, lambda t: big["o_t"][:, i, cols[t]], lambda t: wout_t[:], "out_done")

            @block.scalar
            def _(act):
                norm.scalar(act)
                credit(act, act_made)
                act.wait_ge(loaded, LOADS)
                nc.scalar.activation(rate[:], a_log[:], ACT.Exp).then_inc(rate_ready, 1)
                act.wait_ge(weights_turned, 1)
                nc.scalar.copy(wwrite_t[:], bank[0][0][:, 0:P])
                nc.scalar.copy(wout_t[:], bank[0][0][:, P:2 * P]).then_inc(weights_ready, 1)
                with act.Fori(1, PAIRS + 1) as pair:

                    def copy(i, k, dst, key, done_key):
                        wait(act, pair, done_key, i)
                        done(nc.scalar.copy(dst, bank[i][k][:]), key, i)

                    for i in range(2):
                        wait(act, pair - 1, "out_done", i)
                        done(nc.scalar.copy(big["xs"][:, i], seq_of(g.XH, pair, i)), "xs_ready", i)
                    for i in range(2):
                        wait(act, pair - 1, "x_added", i)
                        copy(i, 0, big["xt"][:, i], "xt_ready", "x_turned")
                        z = bank[i][1][:, 0:12].rearrange("p (t k) -> p t k", k=3)
                        wait(act, pair, "z_done", i)
                        done(nc.scalar.activation(e_gates[:, i], z[:, :, 0:2], ACT.Exp, scale=-1.0), "e_gates_ready", i)
                    for i in range(2):
                        wait(act, pair, "u_ready", i)
                        done(nc.scalar.activation(sm["abs_u"][:, i], sm["u"][:, i], ACT.Abs), "abs_ready", i)
                        wait(act, pair, "abs_ready", i)
                        done(nc.scalar.activation(sm["e_u"][:, i], sm["abs_u"][:, i], ACT.Exp, scale=-1.0), "e_u_ready", i)
                        wait(act, pair, "e_u_ready", i)
                        done(nc.scalar.activation(sm["ln_u"][:, i], sm["e_u"][:, i], ACT.Ln, bias=1.0), "ln_ready", i)
                    for i in range(2):
                        copy(i, 3, keys_t[:, i, 1:TOKENS + 1], "rk_t_ready", "rk_turned")
                    for i in range(2):
                        wait(act, pair, "decs_done", i)
                        done(nc.scalar.copy(sm["dec"][:, i], bank[i][1][:, 16:20]), "dec_ready", i)
                        done(nc.scalar.activation(sm["e_dec"][:, i], bank[i][1][:, 16:20], ACT.Exp), "e_dec_ready", i)
                        done(nc.scalar.activation(carry[:, i], bank[i][1][:, 24:32], ACT.Exp), "carry_ready", i)
                        wait(act, pair, "to_end_ready", i)
                        done(nc.scalar.activation(sm["e_to_end"][:, i], sm["to_end"][:, i], ACT.Exp), "e_to_end_ready", i)
                    for i in range(2):
                        wait(act, pair, "floor_ready", i)
                        done(nc.scalar.activation(big["decayed"][:, i], big["decayed"][:, i], ACT.Exp), "decayed_ready", i)
                        copy(i, 3, big["wk"][:, i], "wk_ready", "wk_turned")
                    for i in range(2):
                        copy(i, 2, big["rkd_t"][:, i], "rkd_t_ready", "rkd_turned")
                        copy(i, 1, big["wkb_t"][:, i], "wkb_t_ready", "wkb_turned")
                    for level in range(1, LEVELS):
                        for i in range(2):
                            wait(act, pair, "t1_done", i, level + 1)
                            done(nc.scalar.copy(big["t1"][:, i], bank[i][0][:]), "t1_ready", i)
                    for i in range(2):
                        copy(i, 0, big["vp"][:, i], "vp_ready", "vp_done")
                        copy(i, 1, big["wkcd_t"][:, i], "wkcd_ready", "wkcd_done")
                    for i in range(2):
                        copy(i, 3, big["o_t"][:, i], "o_ready", "o_done")

            @block.gpsimd
            def _(pool):
                norm.gpsimd(pool)
                credit(pool, pool_made)
                pool.wait_ge(loaded, LOADS)
                with pool.Fori(1, PAIRS + 1) as pair:
                    for i in range(2):
                        wait(pool, pair, "norm2c_ready", i)
                        done(nc.gpsimd.tensor_tensor(sm["inv_norm"][:, i], sm["norm2c"][:, i], g.minus_half[:, 0:TILES], ALU.pow), "inv_norm_ready", i)
                    for i in range(2):
                        wait(pool, pair, "rk_ready", i)
                        wait(pool, pair, "e_dec_ready", i)
                        done(nc.gpsimd.tensor_tensor(tiled(big["rkd"], i), tiled(big["rk"], i), spread(sm["e_dec"][:, i]), ALU.mult), "rkd_ready", i)
                    for level in range(LEVELS):
                        for i in range(2):
                            wait(pool, pair, "m_ready", i)
                            done(nc.gpsimd.tensor_tensor(off_t[:, i, level].rearrange("p (t d) -> p t d", d=P), tiled(big["m_t"], i), every(corner[:, level]), ALU.mult), "off_ready", i)
                    for i in range(2):
                        wait(pool, pair, "wkb_ready", i)
                        done(nc.gpsimd.tensor_tensor(tiled(big["wkbd"], i), tiled(big["wkb"], i), spread(sm["e_dec"][:, i]), ALU.mult), "wkbd_ready", i)
                        wait(pool, pair, "wk_ready", i)
                        wait(pool, pair, "e_to_end_ready", i)
                        done(nc.gpsimd.tensor_tensor(tiled(big["wkdw"], i), tiled(big["wk"], i), spread(sm["e_to_end"][:, i]), ALU.mult), "wkdw_ready", i)

            @block.vector
            def _(dve):
                norm.vector(dve)
                nc.vector.memset(keys_t[:], 0.0).then_inc(pads_ready, 1)
                credit(dve, dve_made)
                dve.wait_ge(loaded, LOADS)
                dve.wait_ge(rate_ready, 1)
                with dve.Fori(1, PAIRS + 1) as pair:
                    for i in range(2):
                        wait(dve, pair, "xt_ready", i)
                        done(nc.vector.tensor_tensor(big["y"][:, i], big["xt"][:, i], big["xt"][:, i], ALU.mult), "squares_ready", i)
                        wait(dve, pair, "squares_ready", i)
                        done(nc.vector.tensor_reduce(sm["norm2"][:, i], tiled(big["y"], i), AX, ALU.add), "norm2_ready", i)
                        wait(dve, pair, "norm2_ready", i)
                        done(nc.vector.tensor_scalar(sm["norm2c"][:, i], sm["norm2"][:, i], 1e-24, None, ALU.max), "norm2c_ready", i)
                    for i in range(2):
                        z = bank[i][1][:, 0:12].rearrange("p (t k) -> p t k", k=3)
                        wait(dve, pair, "z_done", i)
                        wait(dve, pair, "e_gates_ready", i)
                        done(nc.vector.tensor_scalar(sm["u"][:, i], z[:, :, 2], dt_bias[:], None, ALU.add), "u_ready", i)
                        done(nc.vector.tensor_scalar(e_gates1[:, i], e_gates[:, i], 1.0, None, ALU.add), "e_gates1_ready", i)
                        wait(dve, pair, "e_gates1_ready", i)
                        done(nc.vector.reciprocal(gates[:, i], e_gates1[:, i]), "gates_ready", i)
                    for i in range(2):
                        wait(dve, pair, "inv_norm_ready", i)
                        done(nc.vector.tensor_tensor(tiled(big["rk"], i), tiled(big["xt"], i), spread(sm["inv_norm"][:, i]), ALU.mult), "rk_ready", i)
                    for i in range(2):
                        wait(dve, pair, "ln_ready", i)
                        done(nc.vector.scalar_tensor_tensor(sm["sp"][:, i], sm["u"][:, i], 0.0, sm["ln_u"][:, i], ALU.max, ALU.add), "sp_ready", i)
                        wait(dve, pair, "sp_ready", i)
                        done(nc.vector.tensor_scalar(sm["decay"][:, i], sm["sp"][:, i], rate[:], -1.0, ALU.mult, ALU.mult), "decay_ready", i)
                    for i in range(2):
                        wait(dve, pair, "v_done", i)
                        wait(dve, pair, "gates_ready", i)
                        done(nc.vector.tensor_tensor(tiled(big["vb"], i), banked(i, 2), spread(gates[:, i, :, 1]), ALU.mult), "vb_ready", i)
                    for i in range(2):
                        wait(dve, pair, "carry_ready", i)
                        done(nc.vector.tensor_tensor(sm["to_end"][:, i], bank[i][1][:, 20:24], sm["dec"][:, i], ALU.subtract), "to_end_ready", i)
                        wait(dve, pair, "dec_rows_done", i)
                        for t in range(TILES):
                            last = nc.vector.scalar_tensor_tensor(big["decayed"][:, i, cols[t]], bank[i][0][:, cols[t]], sm["dec"][:, i, t:t + 1], ceiling[:],
                                                                  ALU.subtract, ALU.min)
                        done(last, "floor_ready", i)
                    for i in range(2):
                        wait(dve, pair, "wk_ready", i)
                        done(nc.vector.tensor_tensor(tiled(big["wkb"], i), tiled(big["wk"], i), spread(gates[:, i, :, 1]), ALU.mult), "wkb_ready", i)
                    for i in range(2):
                        wait(dve, pair, "decayed_ready", i)
                        wait(dve, pair, "attn_done", i)
                        done(nc.vector.tensor_tensor(big["attn_t"][:, i], bank[i][0][:], big["decayed"][:, i], ALU.mult), "attn_ready", i)
                        wait(dve, pair, "gram_done", i)
                        done(nc.vector.tensor_tensor(big["m_t"][:, i], bank[i][3][:], big["decayed"][:, i], ALU.mult), "m_ready", i)
                    for level in range(LEVELS):
                        for i in range(2):
                            if level == 0:
                                wait(dve, pair, "off_ready", i, 1)
                                done(nc.vector.tensor_tensor(tiled(big["inv_t"], i), every(g.ident[:]), off_t[:, i, 0].rearrange("p (t d) -> p t d", d=P), ALU.subtract), "inv_t_ready", i)
                                wait(dve, pair, "t1_done", i, 1)
                                done(nc.vector.tensor_tensor(tiled(big["inv"], i), every(g.ident[:]), banked(i, 0), ALU.subtract), "inv_ready", i)
                                continue
                            if level < LEVELS - 1:
                                wait(dve, pair, "u_done", i, level)
                                wait(dve, pair, "inv_ready", i, level)
                                done(nc.vector.tensor_tensor(big["inv"][:, i], big["inv"][:, i], bank[i][1][:], ALU.subtract), "inv_ready", i)
                            wait(dve, pair, "ut_done", i, level)
                            wait(dve, pair, "inv_t_ready", i, level)
                            done(nc.vector.tensor_tensor(big["inv_t"][:, i], big["inv_t"][:, i], bank[i][2][:], ALU.subtract), "inv_t_ready", i)
                    for i in range(2):
                        done(nc.vector.memset(state[:, i], 0.0), "state_ready", i)
                        dve.sem_inc(q["inv_ready"][i], 1)
                    for c in range(CHUNKS):
                        t, rows = c // 2, slice(CHUNK * (c % 2), CHUNK * (c % 2) + CHUNK)
                        for i in range(2):
                            if c == 0:
                                wait(dve, pair, "vp_ready", i)
                            wait(dve, pair, "vs_done", i, c + 1)
                            done(nc.vector.tensor_tensor(big["v_new"][rows, i, cols[t]], big["vp"][rows, i, cols[t]], bank[i][2][rows, 0:P], ALU.subtract), "v_new_ready", i)
                        for i in range(2):
                            wait(dve, pair, "update_done", i, c + 1)
                            wait(dve, pair, "state_ready", i, c + 1)
                            done(nc.vector.scalar_tensor_tensor(state[:, i], state[:, i], carry[:, i, c:c + 1], bank[i][0][:, 0:P], ALU.mult, ALU.add), "state_ready", i)
                    for i in range(2):
                        wait(dve, pair, "out_done", i)
                        for t in range(TILES):
                            last = nc.vector.scalar_tensor_tensor(big["y"][:, i, cols[t]], bank[i][1][:, cols[t]], gates[:, i, t, 0:1], big["xt"][:, i, cols[t]], ALU.mult, ALU.add)
                        done(last, "y_ready", i)
                        wait(dve, pair, "y_ready", i)
                        xt = seq_of(g.X, pair, i)
                        done(nc.vector.tensor_tensor(xt, xt, big["y"][:, i], ALU.add), "x_added", i)

    run_phase(nc, name, body)


class Kept:

    def __init__(self, nc, ctx):
        def sb(name, shape):
            return ctx.enter_context(nc.sbuf_tensor(name, shape, F32))

        self.X = sb("X", [P, SEQS, TOKENS])
        self.XH = sb("XH", [P, SEQS, TOKENS])
        self.ident = sb("ident", [P, P])
        self.minus_half = sb("minus_half", [P, 64])
        self.rank8 = sb("rank8", [P, 8])


def load_phase(nc, g, x, a):
    def body(ph):
        loaded = ph.sem("loaded")
        with nc.Block() as block:

            @block.sync
            def _(sp):
                sp.dma_start(g.X[:].rearrange("p s (t d) -> p (s t) d", d=P), x.rearrange("s (t p) d -> p (s t) d", p=P)).then_inc(loaded, 16)
                sp.dma_start(g.ident[:], a["ident"]).then_inc(loaded, 16)
                sp.dma_start(g.rank8[:], a["rank8"]).then_inc(loaded, 16)
                sp.wait_ge(loaded, 16 * 3)

            @block.vector
            def _(dve):
                nc.vector.memset(g.minus_half[:], -0.5)

    run_phase(nc, "load", body)


def store_phase(nc, g, out):
    def body(ph):
        stored = ph.sem("stored")
        with nc.Block() as block:

            @block.sync
            def _(sp):
                sp.dma_start(out.rearrange("s (t p) d -> p (s t) d", p=P), g.X[:].rearrange("p s (t d) -> p (s t) d", d=P)).then_inc(stored, 16)
                sp.wait_ge(stored, 16)

    run_phase(nc, "store", body)


def build_program(nc, a, out):
    def of(layer, *names):
        return {n: a[f"{layer}_{n}"] for n in names}

    with ExitStack() as ctx:
        g = Kept(nc, ctx)
        load_phase(nc, g, a["L0_attn_x"], a)

        delta_rule_phase(nc, g, "delta", of("L0_attn", "W_write", "W_gate", "W_out", "W_beta", "W_alpha", "dt_bias", "A_log")
                         | {n: a[n] for n in ("until", "within", "ends", "ceiling", "corner")})

        local_transformer_phase(nc, g, "local", of("L0_ffn", "Wqkv", "q_scale", "k_scale", "Wo", "ln_g", "ln_b", "W1", "b1", "W2", "b2")
                                | {n: a[n] for n in ("rotary", "band")})
        add_back_phase(nc, g, "back")

        l1 = of("L1_attn", "wq", "wk", "wv", "wo")
        softmax_attention_phase(nc, g, "causal", {
            "wq": l1["wq"].rearrange("m h d -> m (h d)"), "wk": l1["wk"].rearrange("m h d -> m (h d)"), "wv": l1["wv"].rearrange("m h d -> m (h d)"),
            "wo": l1["wo"].rearrange("h d m -> (h d) m"), "cos": a["rope_cos"], "sin": a["rope_sin"], "mask": a["never_later"]}, causal_only=True)

        moe_phase(nc, g, "moe1", {"wg": a["L1_ffn_Wg"], "wg_t": None, "bg": a["L1_ffn_bg"], "w1": a["L1_ffn_W1"], "b1": a["L1_ffn_b1"],
                                  "w2": a["L1_ffn_W2"], "b2": a["L1_ffn_b2"]}, ACT.Gelu_apprx_tanh, top2=True)

        chunk_attention_phase(nc, g, "chunked", of("L2_attn", "Wqk", "bqk", "Wv", "bv", "gamma", "beta", "rel_emb")
                              | {n: a[n] for n in ("bucket", "chunk_mask")})

        moe_phase(nc, g, "moe2", {"wg": a["L2_ffn_router_w"], "wg_t": None, "bg": a["L2_ffn_router_b"], "w1": a["L2_ffn_W1"], "b1": a["L2_ffn_b1"],
                                  "w2": a["L2_ffn_W2"], "b2": a["L2_ffn_b2"]}, ACT.Gelu, top2=False)

        softmax_attention_phase(nc, g, "relu", {n.lower(): ap for n, ap in of("L3_attn", "Wq", "Wk", "Wv", "Wo", "bq", "bk", "bv", "bo").items()}
                                | {"mask": a["less_later"]}, causal_only=False)

        moe_phase(nc, g, "moe3", {"wg": None, "wg_t": a["L3_ffn_Wg"], "bg": None, "w1": a["L3_ffn_W1"], "b1": a["L3_ffn_b1"],
                                  "w2": a["L3_ffn_W2"], "b2": a["L3_ffn_b2"]}, ACT.Gelu, top2=False)

        store_phase(nc, g, out)


def shape_constants():
    f = np.float32
    c = {"ident": np.eye(P, dtype=f), "rank8": np.tile(np.arange(8, 0, -1, dtype=f), (P, 1))}

    j, i = np.arange(P)[:, None], np.arange(P)[None]
    same = j // 64 == i // 64
    c["until"] = (same & (j <= i)).astype(f)
    c["within"] = same.astype(f)
    c["ends"] = (j // 64 == np.arange(2)[None]).astype(f)
    c["ceiling"] = np.where(same & (j <= i), f(-NEVER), f(NEVER))
    c["corner"] = np.stack([((i >> b) % 2 == 1) & (j >> b == (i >> b) - 1) for b in range(6)], 1).astype(f)
    c["chunk_mask"] = np.where(same & (i <= j), f(0), f(NEVER))

    half = np.arange(0, 64, 2, dtype=f)
    angle = np.arange(TOKENS, dtype=f)[:, None] * (f(1) / f(10000) ** (half / f(64)))[None]
    scale = ((half + f(25.6)) / f(89.6))[None] ** ((np.arange(TOKENS, dtype=f) - f(256)) / f(16))[:, None]
    angle, scale = np.tile(angle, 2).astype(np.float64), np.tile(scale, 2)
    cos, sin = np.cos(angle), np.sin(angle) * np.where(np.arange(64) < 32, -1, 1)
    rotary = np.stack([cos * scale * 8, sin * scale * 8, cos / scale, sin / scale], 1).astype(f)
    c["rotary"] = rotary.reshape(TILES, P, 4, 64).transpose(1, 0, 2, 3)
    r, k = np.arange(P)[:, None], np.arange(96)[None]
    near = (k >= r % 64) & (k <= r % 64 + 32)
    c["band"] = np.stack([np.where(near & ((r >= 64) | (k >= 32)), 0, NEVER), np.where(near, 0, NEVER)], 1).astype(f)

    angle = np.arange(TOKENS, dtype=f)[:, None] * (f(10000) ** (-(np.arange(32) / 32)).astype(f))[None]
    cos, sin = np.cos(angle.astype(np.float64)).T, np.sin(angle.astype(np.float64)).T
    root = P ** -0.5
    c["rope_cos"] = (np.concatenate([cos, cos, np.ones((64, TOKENS))]) * root).astype(f)
    c["rope_sin"] = (np.concatenate([sin, sin]) * root).astype(f)
    later = np.arange(7 * P)[None] - 3 * P > np.arange(P)[:, None]
    c["never_later"] = np.where(later, f(-1e30), f(0))
    c["less_later"] = np.where(later, f(-1e4), f(0))

    n = np.arange(64)
    large = 16 + np.log(np.maximum(n, 1).astype(f) / 16) / math.log(8) * 16
    bucket = np.where(n < 16, n, np.minimum(large, 31)).astype(np.int32)
    c["bucket"] = np.zeros((32, 2 * P - 1), f)
    c["bucket"][bucket, P - 1 - n] = 1
    return {name: np.ascontiguousarray(table) for name, table in c.items()}


def kernel(**inputs):
    import concourse.bacc as bacc
    from concourse.bass_utils import run_bass_kernel_spmd

    nc = bacc.Bacc("TRN2", target_bir_lowering=False, num_devices=1)
    arrays, aps = {}, {}
    for name, array in [*inputs.items(), *shape_constants().items()]:
        array = np.ascontiguousarray(array)
        arrays[f"in_{name}"] = array
        aps[name] = nc.dram_tensor(f"in_{name}", array.shape, mybir.dt.from_np(array.dtype), kind="ExternalInput").ap()
    out = nc.dram_tensor("out_x", (SEQS, TOKENS, P), F32, kind="ExternalOutput").ap()
    build_program(nc, aps, out)
    return run_bass_kernel_spmd(nc, [arrays], core_ids=[0]).results[0]["out_x"]
```
